# Optimizing a Trainium2 kernel written in Bass

```python
import numpy as np
import jax
import jax.numpy as jnp

def _softmax(x, axis=-1):
    return jax.nn.softmax(x, axis=axis)

def _gelu(x):
    return jax.nn.gelu(x, approximate=True)

def _silu(x):
    return jax.nn.silu(x)

def _sigmoid(x):
    return jax.nn.sigmoid(x)

def _layernorm(x, axis=-1, eps=1e-05):
    m = jnp.mean(x, axis=axis, keepdims=True)
    v = jnp.var(x, axis=axis, keepdims=True)
    return (x - m) / jnp.sqrt(v + eps)

def _scatter_add(tgt, idx, src, axis=0):
    return tgt.at[idx].add(src)

def _segment_sum(src, seg, n):
    return jax.ops.segment_sum(src, seg, n)
kernel_name = 'mk_prb_d2_jaxref_r8_bf2dc6'

def setup_inputs(seed: int=0):
    np.random.seed(seed)
    _w = jnp.asarray

    def _L0_attn_setup():
        import jax, jax.numpy as jnp
        import numpy as np
        ALPHA_SCALE = 8.0
        EPS = 1e-06

        def _depthwise_causal_conv(x, conv_w, conv_b):
            K = conv_w.shape[-1]
            y = jax.lax.conv_general_dilated(x, conv_w, window_strides=(1,), padding=[(K - 1, 0)], dimension_numbers=('NCH', 'OIH', 'NCH'), feature_group_count=x.shape[1])
            return y + conv_b[None, :, None]

        def _linear_scan(alpha, x):

            def combine(c1, c2):
                a1, b1 = c1
                a2, b2 = c2
                return (a1 * a2, a2 * b1 + b2)
            _, h = jax.lax.associative_scan(combine, (alpha, x), axis=1)
            return h
        key = jax.random.key(seed)
        ks = jax.random.split(key, 8)
        N, T, D = (4, 512, 128)
        H, K = (192, 4)
        return {'x': jax.random.normal(ks[0], (N, T, D), dtype=jnp.float32), 'W_in': jax.random.normal(ks[1], (2 * H, D), dtype=jnp.float32) * D ** (-0.5), 'conv_w': jax.random.normal(ks[2], (H, 1, K), dtype=jnp.float32) * 0.1, 'conv_b': jax.random.normal(ks[3], (H,), dtype=jnp.float32) * 0.1, 'W_g': jax.random.normal(ks[4], (2 * H, H), dtype=jnp.float32) * H ** (-0.5), 'b_g': jax.random.normal(ks[5], (2 * H,), dtype=jnp.float32) * 0.1, 'forget_base': jax.random.normal(ks[6], (H,), dtype=jnp.float32), 'W_out': jax.random.normal(ks[7], (D, H), dtype=jnp.float32) * H ** (-0.5)}
    _L0_attn_in = _L0_attn_setup()

    def _L0_ffn_setup():
        import jax, jax.numpy as jnp
        import numpy as np
        E = 16
        K = 4
        B, S, H, I = (4, 128, 128, 256)
        key = jax.random.key(seed)
        k0, k1, k2, k3 = jax.random.split(key, 4)
        scale = 0.02
        return {'hidden_states': jax.random.normal(k0, (B, S, H), jnp.float32), 'router_w': jax.random.normal(k1, (H, E), jnp.float32) * scale, 'router_b': jnp.zeros((E,), jnp.float32), 'w1': jax.random.normal(k2, (E, H, I), jnp.float32) * scale, 'b1': jnp.zeros((E, I), jnp.float32), 'w2': jax.random.normal(k3, (E, I, H), jnp.float32) * scale, 'b2': jnp.zeros((E, H), jnp.float32)}
    _L0_ffn_in = _L0_ffn_setup()

    def _L1_attn_setup():
        import jax, jax.numpy as jnp
        import numpy as np
        B, T, C = (4, 256, 128)
        NQ, D = (8, C // 8)
        key = jax.random.key(seed)
        ks = jax.random.split(key, 6)
        s = 0.02
        return {'x': jax.random.normal(ks[0], (B, T, C), dtype=jnp.float32), 'Wk': jax.random.normal(ks[1], (C, D), dtype=jnp.float32) * s, 'Wv': jax.random.normal(ks[2], (C, D), dtype=jnp.float32) * s, 'Wq': jax.random.normal(ks[3], (NQ, C, D), dtype=jnp.float32) * s, 'Wp': jax.random.normal(ks[4], (NQ * D, C), dtype=jnp.float32) * s, 'bp': jnp.zeros((C,), dtype=jnp.float32)}
    _L1_attn_in = _L1_attn_setup()

    def _L1_ffn_setup():
        import jax, jax.numpy as jnp
        import numpy as np
        DIM = 128
        HID = 256
        E = 8
        K = 2
        R = 16
        B_, S_ = (2, 128)

        def _lora_in(xf, W, b, A, B):
            base = jnp.einsum('td,ehd->teh', xf, W)
            low = jnp.einsum('ter,ehr->teh', jnp.einsum('td,erd->ter', xf, A), B)
            return base + low + b

        def _lora_out(g, W, b, A, B):
            base = jnp.einsum('teh,edh->ted', g, W)
            low = jnp.einsum('ter,edr->ted', jnp.einsum('teh,erh->ter', g, A), B)
            return base + low + b
        key = jax.random.key(seed)
        ks = jax.random.split(key, 14)
        n = lambda k, shape, scale: jax.random.normal(k, shape, jnp.float32) * scale
        inp = {'x': jax.random.normal(ks[0], (B_, S_, DIM), jnp.float32), 'Wg': n(ks[1], (E, DIM), DIM ** (-0.5)), 'W1': n(ks[2], (E, HID, DIM), DIM ** (-0.5)), 'b1': jnp.zeros((E, HID), jnp.float32), 'A1': n(ks[3], (E, R, DIM), DIM ** (-0.5)), 'B1': n(ks[4], (E, HID, R), 0.01), 'W2': n(ks[5], (E, DIM, HID), HID ** (-0.5)), 'b2': jnp.zeros((E, DIM), jnp.float32), 'A2': n(ks[6], (E, R, HID), HID ** (-0.5)), 'B2': n(ks[7], (E, DIM, R), 0.01), 'W3': n(ks[8], (E, HID, DIM), DIM ** (-0.5)), 'b3': jnp.zeros((E, HID), jnp.float32), 'A3': n(ks[9], (E, R, DIM), DIM ** (-0.5)), 'B3': n(ks[10], (E, HID, R), 0.01)}
        return inp
    _L1_ffn_in = _L1_ffn_setup()
    _d = {'L0_attn_x': _L0_attn_in['x'], 'L0_attn_W_in': _L0_attn_in['W_in'], 'L0_attn_conv_w': _L0_attn_in['conv_w'], 'L0_attn_conv_b': _L0_attn_in['conv_b'], 'L0_attn_W_g': _L0_attn_in['W_g'], 'L0_attn_b_g': _L0_attn_in['b_g'], 'L0_attn_forget_base': _L0_attn_in['forget_base'], 'L0_attn_W_out': _L0_attn_in['W_out'], 'L0_ffn_router_w': _L0_ffn_in['router_w'], 'L0_ffn_router_b': _L0_ffn_in['router_b'], 'L0_ffn_w1': _L0_ffn_in['w1'], 'L0_ffn_b1': _L0_ffn_in['b1'], 'L0_ffn_w2': _L0_ffn_in['w2'], 'L0_ffn_b2': _L0_ffn_in['b2'], 'L1_attn_Wk': _L1_attn_in['Wk'], 'L1_attn_Wv': _L1_attn_in['Wv'], 'L1_attn_Wq': _L1_attn_in['Wq'], 'L1_attn_Wp': _L1_attn_in['Wp'], 'L1_attn_bp': _L1_attn_in['bp'], 'L1_ffn_Wg': _L1_ffn_in['Wg'], 'L1_ffn_W1': _L1_ffn_in['W1'], 'L1_ffn_b1': _L1_ffn_in['b1'], 'L1_ffn_A1': _L1_ffn_in['A1'], 'L1_ffn_B1': _L1_ffn_in['B1'], 'L1_ffn_W2': _L1_ffn_in['W2'], 'L1_ffn_b2': _L1_ffn_in['b2'], 'L1_ffn_A2': _L1_ffn_in['A2'], 'L1_ffn_B2': _L1_ffn_in['B2'], 'L1_ffn_W3': _L1_ffn_in['W3'], 'L1_ffn_b3': _L1_ffn_in['b3'], 'L1_ffn_A3': _L1_ffn_in['A3'], 'L1_ffn_B3': _L1_ffn_in['B3']}
    _x0 = _d['L0_attn_x']
    _d['L0_attn_x'] = jax.random.normal(jax.random.fold_in(jax.random.key(seed), 1), (8, 512, 128), dtype=_x0.dtype)
    del _x0
    return _d

def reference(L0_attn_x, L0_attn_W_in, L0_attn_conv_w, L0_attn_conv_b, L0_attn_W_g, L0_attn_b_g, L0_attn_forget_base, L0_attn_W_out, L0_ffn_router_w, L0_ffn_router_b, L0_ffn_w1, L0_ffn_b1, L0_ffn_w2, L0_ffn_b2, L1_attn_Wk, L1_attn_Wv, L1_attn_Wq, L1_attn_Wp, L1_attn_bp, L1_ffn_Wg, L1_ffn_W1, L1_ffn_b1, L1_ffn_A1, L1_ffn_B1, L1_ffn_W2, L1_ffn_b2, L1_ffn_A2, L1_ffn_B2, L1_ffn_W3, L1_ffn_b3, L1_ffn_A3, L1_ffn_B3):

    def _L0_attn_ref(x, W_in, conv_w, conv_b, W_g, b_g, forget_base, W_out):
        import jax, jax.numpy as jnp
        import numpy as np
        ALPHA_SCALE = 8.0
        EPS = 1e-06

        def _depthwise_causal_conv(x, conv_w, conv_b):
            K = conv_w.shape[-1]
            y = jax.lax.conv_general_dilated(x, conv_w, window_strides=(1,), padding=[(K - 1, 0)], dimension_numbers=('NCH', 'OIH', 'NCH'), feature_group_count=x.shape[1])
            return y + conv_b[None, :, None]

        def _linear_scan(alpha, x):

            def combine(c1, c2):
                a1, b1 = c1
                a2, b2 = c2
                return (a1 * a2, a2 * b1 + b2)
            _, h = jax.lax.associative_scan(combine, (alpha, x), axis=1)
            return h
        H = W_g.shape[1]
        gx = jnp.einsum('ntd,hd->nth', x, W_in)
        gate, xb = (gx[..., :H], gx[..., H:])
        xb = _depthwise_causal_conv(jnp.swapaxes(xb, 1, 2), conv_w, conv_b)
        xb = jnp.swapaxes(xb, 1, 2)
        fg = jnp.einsum('nth,gh->ntg', xb, W_g) + b_g
        forget, inp = (fg[..., :H], fg[..., H:])
        alpha = jnp.exp(-ALPHA_SCALE * jax.nn.softplus(forget_base) * jax.nn.sigmoid(forget))
        beta = jnp.sqrt(1.0 - alpha ** 2 + EPS)
        xs = beta * jax.nn.sigmoid(inp) * xb
        h = _linear_scan(alpha, xs)
        return jnp.einsum('nth,dh->ntd', jax.nn.gelu(gate, approximate=False) * h, W_out)

    def _L0_ffn_ref(hidden_states, router_w, router_b, w1, b1, w2, b2):
        import jax, jax.numpy as jnp
        import numpy as np
        E = 16
        K = 4
        B, S, H, I = (4, 128, 128, 256)
        b, s, h = hidden_states.shape
        logits = hidden_states @ router_w + router_b
        probs = jax.nn.softmax(logits, axis=-1)
        topw, topi = jax.lax.top_k(probs, K)
        topw = topw / jnp.sum(topw, axis=-1, keepdims=True)
        combine = jnp.sum(jax.nn.one_hot(topi, E, dtype=hidden_states.dtype) * topw[..., None], axis=2)
        x = hidden_states.reshape(b * s, h)
        c = combine.reshape(b * s, E)

        def body(acc, expert):
            w1e, b1e, w2e, b2e, ce = expert
            hmid = jax.nn.gelu(x @ w1e + b1e, approximate=False)
            return (acc + (hmid @ w2e + b2e) * ce[:, None], None)
        out, _ = jax.lax.scan(body, jnp.zeros_like(x), (w1, b1, w2, b2, c.T))
        return out.reshape(b, s, h)

    def _L1_attn_ref(x, Wk, Wv, Wq, Wp, bp):
        import jax, jax.numpy as jnp
        import numpy as np
        B, T, C = (4, 256, 128)
        NQ, D = (8, C // 8)
        b, t, c = x.shape
        scale = c ** (-0.5)
        k = x @ Wk
        v = x @ Wv
        q = jnp.einsum('btc,qcd->bqtd', x, Wq)
        wei = jnp.einsum('bqtd,bsd->bqts', q, k) * scale
        causal = jnp.tril(jnp.ones((t, t), dtype=bool))
        wei = jnp.where(causal, wei, -jnp.inf)
        wei = jax.nn.softmax(wei, axis=-1)
        out = jnp.einsum('bqts,bsd->btqd', wei, v)
        out = out.reshape(b, t, -1)
        return out @ Wp + bp

    def _L1_ffn_ref(x, Wg, W1, b1, A1, B1, W2, b2, A2, B2, W3, b3, A3, B3):
        import jax, jax.numpy as jnp
        import numpy as np
        DIM = 128
        HID = 256
        E = 8
        K = 2
        R = 16
        B_, S_ = (2, 128)

        def _lora_in(xf, W, b, A, B):
            base = jnp.einsum('td,ehd->teh', xf, W)
            low = jnp.einsum('ter,ehr->teh', jnp.einsum('td,erd->ter', xf, A), B)
            return base + low + b

        def _lora_out(g, W, b, A, B):
            base = jnp.einsum('teh,edh->ted', g, W)
            low = jnp.einsum('ter,edr->ted', jnp.einsum('teh,erh->ter', g, A), B)
            return base + low + b
        orig_shape = x.shape
        xf = x.reshape(-1, x.shape[-1])
        scores = jax.nn.softmax(xf @ Wg.T, axis=-1)
        expert_weights, expert_indices = jax.lax.top_k(scores, K)
        expert_weights = expert_weights / expert_weights.sum(-1, keepdims=True)
        gates = (jax.nn.one_hot(expert_indices, E, dtype=xf.dtype) * expert_weights[..., None]).sum(axis=1)
        h1 = _lora_in(xf, W1, b1, A1, B1)
        h3 = _lora_in(xf, W3, b3, A3, B3)
        g = jax.nn.silu(h1) * h3
        y_e = _lora_out(g, W2, b2, A2, B2)
        y = jnp.einsum('te,ted->td', gates, y_e)
        return y.reshape(orig_shape)
    x = L0_attn_x
    xn = _layernorm(x, axis=-1)
    x = x + _L0_attn_ref(xn, L0_attn_W_in, L0_attn_conv_w, L0_attn_conv_b, L0_attn_W_g, L0_attn_b_g, L0_attn_forget_base, L0_attn_W_out) + _L0_ffn_ref(xn, L0_ffn_router_w, L0_ffn_router_b, L0_ffn_w1, L0_ffn_b1, L0_ffn_w2, L0_ffn_b2)
    xn = _layernorm(x, axis=-1)
    x = x + _L1_attn_ref(xn, L1_attn_Wk, L1_attn_Wv, L1_attn_Wq, L1_attn_Wp, L1_attn_bp) + _L1_ffn_ref(xn, L1_ffn_Wg, L1_ffn_W1, L1_ffn_b1, L1_ffn_A1, L1_ffn_B1, L1_ffn_W2, L1_ffn_b2, L1_ffn_A2, L1_ffn_B2, L1_ffn_W3, L1_ffn_b3, L1_ffn_A3, L1_ffn_B3)
    return x

_drawn_inputs = setup_inputs


def setup_inputs(seed=0):
    import zlib

    import numpy as np

    out = dict(_drawn_inputs(seed))
    spreads = {'L0_ffn_router_b': (0.0, 0.1),
     'L0_ffn_b1': (0.0, 0.1),
     'L0_ffn_b2': (0.0, 0.1),
     'L1_attn_bp': (0.0, 0.1),
     'L1_ffn_b1': (0.0, 0.1),
     'L1_ffn_b2': (0.0, 0.1),
     'L1_ffn_b3': (0.0, 0.1)}
    factors = {'L0_attn_b_g': 2.823,
     'L1_attn_Wk': 8.0,
     'L1_attn_Wv': 8.0,
     'L1_attn_Wq': 8.0,
     'L1_attn_Wp': 8.0,
     'L1_ffn_A1': 3.372,
     'L1_ffn_B1': 3.373,
     'L1_ffn_A2': 3.507,
     'L1_ffn_B2': 3.51,
     'L1_ffn_A3': 3.5,
     'L1_ffn_B3': 3.511}
    for name, (base, spread) in spreads.items():
        noise = np.random.default_rng([zlib.crc32(name.encode()), seed]).standard_normal(out[name].shape)
        drawn = base * np.exp(spread * noise) if base else spread * noise
        out[name] = jnp.asarray(drawn.astype(out[name].dtype))
    for name, factor in factors.items():
        out[name] = (out[name] * factor).astype(out[name].dtype)
    return out
```

```python
from contextlib import ExitStack

import concourse.bass as bass
from concourse import mybir

ALU = mybir.AluOpType
ACT = mybir.ActivationFunctionType
AX = mybir.AxisListType
F32 = mybir.dt.float32
F32R = mybir.dt.float32r
BF16 = mybir.dt.bfloat16
I32 = mybir.dt.int32

P = 128
T = 512
J = T // P
LN_EPS = 1e-5
ALPHA_SCALE = 8.0
BETA_EPS = 1e-6
MASKED = -1e30


def raw(ap):
    return ap.bitcast(F32)


def two_block_kernel(nc, x_in, W_in, conv_w, conv_b, W_g, b_g, forget_base, W_out,
                     router_w, router_b, w1, b1, w2, b2,
                     Wk, Wv, Wq, Wp, bp,
                     Wg, W1, b1_1, A1, B1, W2, b2_1, A2, B2, W3, b3_1, A3, B3, out):
    N, _, D = x_in.shape
    HR = W_out.shape[1]
    C2 = HR // 2
    TAPS = conv_w.shape[2]
    E0, _, I0 = w1.shape
    E1, I1, _ = W1.shape
    R = A1.shape[1]
    NQ, _, DH = Wq.shape
    K0, K1 = 4, 2
    NB = N * J
    SCALE = float(D) ** -0.5
    assert D == P and I0 == 2 * P and I1 == 2 * P and T == x_in.shape[1]

    root = ExitStack()
    scope = [root]

    def sb(name, shape, dt=F32):
        return scope[-1].enter_context(nc.sbuf_tensor(name, shape, dt))

    def ps(name, shape, dt=F32):
        return scope[-1].enter_context(nc.psum_tensor(name, shape, dt))

    def sem(name):
        return root.enter_context(nc.semaphore(name))

    def tile_cols(n):
        return bass.ds(n * T, T)

    def mm3(dst, w_hi, w_lo, m_hi, m_lo, start=True, stop=True):
        nc.tensor.matmul(dst, w_hi, m_hi, start=start, stop=False)
        nc.tensor.matmul(dst, w_hi, m_lo, start=False, stop=False)
        return nc.tensor.matmul(dst, w_lo, m_hi, start=False, stop=stop)

    with root:
        xres = sb("xres", [P, NB, D])
        x_hi = sb("x_hi", [P, N * T], F32R)
        x_lo = sb("x_lo", [P, N * T], F32R)
        yT = sb("yT", [P, N * T])
        gT = sb("gT", [P, N * T], F32R)
        ident = sb("ident", [P, P])
        sel = sb("sel", [P, E0, P], F32R)

        s_const0 = sem("const_zeroed")
        s_const = sem("const_made")
        s_xload = sem("x_loaded")
        scope.append(ExitStack())
        sel_f = sb("sel_f", [P, E0, P])
        with scope[-1], nc.Block() as block:
            @block.sync
            def _(sp):
                for n in range(N):
                    sp.dma_start(xres[:, n * J:(n + 1) * J, :],
                                 x_in[n].rearrange("(j p) d -> p j d", p=P)).then_inc(s_xload, 16)
                sp.wait_ge(s_xload, 16 * N)

            @block.gpsimd
            def _(pool):
                pool.memset(ident[:], 0.0).then_inc(s_const0, 1)
                pool.memset(sel_f[:], 0.0).then_inc(s_const0, 1)
                pool.wait_ge(s_const0, 2)
                pool.affine_select(out=ident[:], in_=ident[:], compare_op=ALU.not_equal, fill=1.0,
                                   base=0, pattern=[[-1, P]], channel_multiplier=1).then_inc(s_const, 1)
                for k, base in enumerate((0, -16)):
                    pool.wait_ge(s_const, k + 1)
                    pool.affine_select(out=sel_f[:], in_=sel_f[:], compare_op=ALU.not_equal,
                                       fill=1.0, base=base, pattern=[[-1, E0], [0, P]],
                                       channel_multiplier=1).then_inc(s_const, 1)
                pool.wait_ge(s_const, 3)
                pool.tensor_copy(sel[:], sel_f[:]).then_inc(s_const, 1)
        scope.pop()

        def norm_and_route(tag, E, K, router_load, router_transposed, bias_load):
            scope.append(ExitStack())
            with scope[-1]:
                stats = sb(tag + "stats", [P, NB, 6])
                mv = sb(tag + "mv", [P, NB, 2])
                rstd = sb(tag + "rstd", [P, NB])
                xn = sb(tag + "xn", [P, 2, J, D])
                rw = sb(tag + "rw", [P, 16])
                rw_raw = sb(tag + "rwraw", [16, P])
                rw_hi = sb(tag + "rw_hi", [P, 16], F32R)
                rw_lo = sb(tag + "rw_lo", [P, 16], F32R)
                rb = sb(tag + "rb", [P, 16])
                lg = sb(tag + "lg", [P, NB, 16])
                pr = sb(tag + "pr", [P, NB, 16])
                mx = sb(tag + "mx", [P, NB])
                sm = sb(tag + "sm", [P, NB])
                top = sb(tag + "top", [P, NB, 8])
                cut = sb(tag + "cut", [P, NB, 16])
                c_hi = sb(tag + "c_hi", [P, NB, 16], F32R)
                c2 = sb(tag + "c2", [P, NB, P])
                p_x = ps(tag + "p_x", [P, 2, T])
                p_lg = ps(tag + "p_lg", [P, NB, 16])
                p_g = ps(tag + "p_g", [P, 2, T])
                p_rw = ps(tag + "p_rw", [P, 16])
                s_rw = sem(tag + "router_loaded")
                s_rb = sem(tag + "router_bias_loaded")
                s_rwz = sem(tag + "router_zeroed")
                s_rwt = sem(tag + "router_transposed")
                s_rwf = sem(tag + "router_in_sbuf")
                s_rwh = sem(tag + "router_split")
                s_st = sem(tag + "stats_made")
                s_mv = sem(tag + "moments_made")
                s_var = sem(tag + "variance_eps")
                s_std = sem(tag + "std_made")
                s_rstd = sem(tag + "rstd_made")
                s_xn = sem(tag + "normalised")
                s_tr = sem(tag + "transposed")
                s_hi = sem(tag + "x_hi_ready")
                s_lo = sem(tag + "x_lo_ready")
                s_lg = sem(tag + "logits_ready")
                s_rt = sem(tag + "route_step")
                s_exp = sem(tag + "exp_ready")
                s_c2 = sem(tag + "gates_ready")
                s_gt = sem(tag + "gates_transposed")
                s_gc = sem(tag + "gates_stored")
                with nc.Block() as block:
                    @block.sync
                    def _(sp):
                        if router_transposed:
                            sp.dma_start(rw_raw[0:E, :], router_load).then_inc(s_rw, 16)
                        else:
                            sp.dma_start(rw[:, 0:E], router_load).then_inc(s_rw, 16)
                        sp.wait_ge(s_rw, 16)
                        if bias_load is not None:
                            sp.dma_start(rb[:, 0:E], bias_load).then_inc(s_rb, 16)
                            sp.wait_ge(s_rb, 16)

                    @block.vector
                    def _(dve):
                        for k in range(NB):
                            nc.vector.bn_stats(stats[:, k, :], xres[:, k, :]).then_inc(s_st, 1)
                        for k in range(NB):
                            dve.wait_ge(s_st, k + 1)
                            nc.vector.bn_aggr(mv[:, k, :], stats[:, k, :]).then_inc(s_mv, 1)
                        dve.wait_ge(s_mv, NB)
                        nc.vector.tensor_scalar(rstd[:], mv[:, :, 1], LN_EPS, None, ALU.add).then_inc(s_var, 1)
                        if router_transposed:
                            nc.vector.memset(rw[:], 0.0).then_inc(s_rwz, 1)
                            dve.wait_ge(s_rwt, 1)
                            dve.wait_ge(s_rwz, 1)
                            nc.vector.tensor_copy(rw[:, 0:E], p_rw[:, 0:E]).then_inc(s_rwf, 1)
                            dve.wait_ge(s_rwf, 1)
                        else:
                            dve.wait_ge(s_rw, 16)
                        nc.vector.tensor_copy(rw_hi[:, 0:E], rw[:, 0:E]).then_inc(s_rwh, 1)
                        dve.wait_ge(s_rwh, 1)
                        nc.vector.tensor_tensor(rw_lo[:, 0:E], rw[:, 0:E], raw(rw_hi[:, 0:E]),
                                                ALU.subtract).then_inc(s_rwh, 1)
                        dve.wait_ge(s_std, 1)
                        nc.vector.reciprocal(rstd[:], rstd[:]).then_inc(s_rstd, 1)
                        dve.wait_ge(s_rstd, 1)
                        for n in range(N):
                            if n >= 2:
                                dve.wait_ge(s_tr, n - 1)
                            for j in range(J):
                                k = n * J + j
                                nc.vector.tensor_scalar(xn[:, n % 2, j, :], xres[:, k, :], mv[:, k, 0:1],
                                                        rstd[:, k:k + 1], ALU.subtract,
                                                        ALU.mult).then_inc(s_xn, 1)
                            if n >= 1:
                                dve.wait_ge(s_hi, n)
                                nc.vector.tensor_tensor(x_lo[:, (n - 1) * T:n * T], p_x[:, (n - 1) % 2, :],
                                                        raw(x_hi[:, (n - 1) * T:n * T]),
                                                        ALU.subtract).then_inc(s_lo, 1)
                        dve.wait_ge(s_hi, N)
                        nc.vector.tensor_tensor(x_lo[:, (N - 1) * T:N * T], p_x[:, (N - 1) % 2, :],
                                                raw(x_hi[:, (N - 1) * T:N * T]), ALU.subtract).then_inc(s_lo, 1)
                        step = [0]

                        def chain(ins):
                            step[0] += 1
                            ins.then_inc(s_rt, 1)
                            dve.wait_ge(s_rt, step[0])

                        def over_experts(ap):
                            return ap.unsqueeze(2).broadcast_to([P, NB, E])

                        dve.wait_ge(s_lg, 1)
                        if bias_load is not None:
                            dve.wait_ge(s_rb, 16)
                            chain(nc.vector.tensor_tensor(lg[:, :, 0:E], p_lg[:, :, 0:E],
                                                          rb[:, 0:E].unsqueeze(1).broadcast_to([P, NB, E]), ALU.add))
                        else:
                            chain(nc.vector.tensor_copy(lg[:, :, 0:E], p_lg[:, :, 0:E]))
                        chain(nc.vector.tensor_reduce(out=mx[:], in_=lg[:, :, 0:E], op=ALU.max, axis=AX.X))
                        chain(nc.vector.tensor_tensor(lg[:, :, 0:E], lg[:, :, 0:E], over_experts(mx[:]), ALU.subtract))
                        dve.wait_ge(s_exp, 1)
                        chain(nc.vector.tensor_reduce(out=sm[:], in_=pr[:, :, 0:E], op=ALU.add, axis=AX.X))
                        chain(nc.vector.reciprocal(sm[:], sm[:]))
                        chain(nc.vector.tensor_tensor(pr[:, :, 0:E], pr[:, :, 0:E], over_experts(sm[:]), ALU.mult))
                        for k in range(NB):
                            last = nc.vector.max(top[:, k, :], pr[:, k, 0:E])
                            last.then_inc(s_rt, 1)
                        step[0] += NB
                        dve.wait_ge(s_rt, step[0])
                        chain(nc.vector.memset(top[:, :, K:8], -1.0))
                        for k in range(NB):
                            nc.vector.match_replace(out=cut[:, k, 0:E], in_to_replace=top[:, k, :],
                                                    in_values=pr[:, k, 0:E], imm_value=-2.0).then_inc(s_rt, 1)
                        step[0] += NB
                        dve.wait_ge(s_rt, step[0])
                        chain(nc.vector.tensor_scalar(cut[:, :, 0:E], cut[:, :, 0:E], -2.0, None, ALU.is_equal))
                        chain(nc.vector.tensor_tensor(pr[:, :, 0:E], pr[:, :, 0:E], cut[:, :, 0:E], ALU.mult))
                        chain(nc.vector.tensor_reduce(out=sm[:], in_=pr[:, :, 0:E], op=ALU.add, axis=AX.X))
                        chain(nc.vector.reciprocal(sm[:], sm[:]))
                        chain(nc.vector.tensor_tensor(pr[:, :, 0:E], pr[:, :, 0:E], over_experts(sm[:]), ALU.mult))
                        chain(nc.vector.memset(c2[:], 0.0))
                        chain(nc.vector.tensor_copy(c_hi[:, :, 0:E], pr[:, :, 0:E]))
                        chain(nc.vector.tensor_copy(c2[:, :, 0:E], raw(c_hi[:, :, 0:E])))
                        nc.vector.tensor_tensor(c2[:, :, 16:16 + E], pr[:, :, 0:E], raw(c_hi[:, :, 0:E]),
                                                ALU.subtract).then_inc(s_c2, 1)

                    @block.scalar
                    def _(act):
                        act.wait_ge(s_var, 1)
                        nc.scalar.activation(rstd[:], rstd[:], ACT.Sqrt).then_inc(s_std, 1)
                        for n in range(N):
                            act.wait_ge(s_tr, n + 1)
                            nc.scalar.activation(x_hi[:, n * T:(n + 1) * T], p_x[:, n % 2, :],
                                                 ACT.Copy).then_inc(s_hi, 1)
                        act.wait_ge(s_rt, 3)
                        nc.scalar.activation(pr[:, :, 0:E], lg[:, :, 0:E], ACT.Exp).then_inc(s_exp, 1)
                        for n in range(N):
                            act.wait_ge(s_gt, n + 1)
                            nc.scalar.activation(gT[:, n * T:(n + 1) * T], p_g[:, n % 2, :],
                                                 ACT.Copy).then_inc(s_gc, 1)

                    @block.tensor
                    def _(pe):
                        if router_transposed:
                            pe.wait_ge(s_rw, 16)
                            nc.tensor.transpose(p_rw[:, 0:E], rw_raw[0:E, :], ident[0:E, 0:E]).then_inc(s_rwt, 1)
                        for n in range(N):
                            pe.wait_ge(s_xn, (n + 1) * J)
                            if n >= 2:
                                pe.wait_ge(s_lo, n - 1)
                            for j in range(J):
                                last = nc.tensor.transpose(p_x[:, n % 2, j * P:(j + 1) * P],
                                                           xn[:, n % 2, j, :], ident[:])
                            last.then_inc(s_tr, 1)
                        pe.wait_ge(s_rwh, 2)
                        for k in range(NB):
                            if k % J == 0:
                                pe.wait_ge(s_lo, k // J + 1)
                            last = mm3(p_lg[:, k, 0:E], x_hi[:, k * P:(k + 1) * P], x_lo[:, k * P:(k + 1) * P],
                                       rw_hi[:, 0:E], rw_lo[:, 0:E])
                        last.then_inc(s_lg, 1)
                        pe.wait_ge(s_c2, 1)
                        for n in range(N):
                            if n >= 2:
                                pe.wait_ge(s_gc, n - 1)
                            for j in range(J):
                                last = nc.tensor.transpose(p_g[:, n % 2, j * P:(j + 1) * P],
                                                           c2[:, n * J + j, :], ident[:])
                            last.then_inc(s_gt, 1)
            scope.pop()

        norm_and_route("a_", E0, K0, router_w, False,
                       router_b.rearrange("(a e) -> a e", a=1).broadcast_to([P, E0]))

        scope.append(ExitStack())
        with scope[-1]:
            win_raw = sb("win_raw", [C2, 4, D])
            wg_raw = sb("wg_raw", [C2, 4, HR])
            wout_raw = sb("wout_raw", [D, HR])
            win_hi = sb("win_hi", [D, 4, C2], F32R)
            win_lo = sb("win_lo", [D, 4, C2], F32R)
            wg_hi = sb("wg_hi", [C2, 8, C2], F32R)
            wg_lo = sb("wg_lo", [C2, 8, C2], F32R)
            wo_hi = sb("wo_hi", [C2, 2, D], F32R)
            wo_lo = sb("wo_lo", [C2, 2, D], F32R)
            cw = sb("cw", [C2, 2, TAPS])
            cb = sb("cb", [C2, 2])
            bg = sb("bg", [C2, 4])
            fb = sb("fb", [C2, 2])
            kf = sb("kf", [C2, 2])
            spt = sb("spt", [C2, 2])
            one_eps = sb("one_eps", [C2, 1])
            xp = sb("xp", [C2, 2, 4 + T])
            xb = sb("xb", [C2, 2, 2, T])
            xb_hi = sb("xb_hi", [C2, 2, T], F32R)
            xb_lo = sb("xb_lo", [C2, 2, T], F32R)
            tf = sb("tf", [C2, 2, T])
            ti = sb("ti", [C2, 2, T])
            al = sb("al", [C2, 2, T])
            be = sb("be", [C2, 2, T])
            gl = sb("gl", [C2, 2, T])
            xs = sb("xs", [C2, 2, T])
            hs = sb("hs", [C2, 2, T])
            z = sb("z", [C2, 2, T])
            z_hi = sb("z_hi", [C2, 2, T], F32R)
            z_lo = sb("z_lo", [C2, 2, T], F32R)
            p_gate = ps("p_gate", [P, 2, T])
            p_xb = ps("p_xb", [P, 2, T])
            p_f = ps("p_f", [P, 2, T])
            p_i = ps("p_i", [P, 2, T])

            s_ld = sem("r_weights_loaded")
            s_wt = sem("r_weights_transposed")
            s_wh = sem("r_weights_high")
            s_wl = sem("r_weights_low")
            s_small = sem("r_small_step")
            s_sp = sem("r_softplus_step")
            pad = TAPS - 1
            with nc.Block() as block:
                @block.sync
                def _(sp):
                    sp.dma_start(win_raw[:], W_in.rearrange("(c p) d -> p c d", p=C2)).then_inc(s_ld, 16)
                    sp.dma_start(wg_raw[:], W_g.rearrange("(c p) h -> p c h", p=C2)).then_inc(s_ld, 16)
                    sp.dma_start(wout_raw[:], W_out).then_inc(s_ld, 16)
                    sp.dma_start(cw[:], conv_w.rearrange("(c p) a k -> p c (a k)", p=C2)).then_inc(s_ld, 16)
                    with nc.allow_non_contiguous_dma(reason="a few hundred bias values"):
                        sp.dma_start(cb[:], conv_b.rearrange("(c p) -> p c", p=C2)).then_inc(s_ld, 16)
                        sp.dma_start(bg[:], b_g.rearrange("(c p) -> p c", p=C2)).then_inc(s_ld, 16)
                        sp.dma_start(fb[:], forget_base.rearrange("(c p) -> p c", p=C2)).then_inc(s_ld, 16)
                    sp.wait_ge(s_ld, 7 * 16)

                @block.tensor
                def _(pe):
                    pe.wait_ge(s_ld, 7 * 16)
                    for c in range(4):
                        last = nc.tensor.transpose(p_gate[:, 0, c * C2:(c + 1) * C2], win_raw[:, c, :],
                                                   ident[0:C2, 0:C2])
                    last.then_inc(s_wt, 1)
                    for hc in range(2):
                        for gc in range(4):
                            last = nc.tensor.transpose(p_f[0:C2, hc, gc * C2:(gc + 1) * C2],
                                                       wg_raw[:, gc, hc * C2:(hc + 1) * C2], ident[0:C2, 0:C2])
                    last.then_inc(s_wt, 1)
                    for hc in range(2):
                        last = nc.tensor.transpose(p_i[0:C2, 0, hc * P:(hc + 1) * P],
                                                   wout_raw[:, hc * C2:(hc + 1) * C2], ident[:])
                    last.then_inc(s_wt, 1)

                splits = [
                    (lambda: win_hi[:].rearrange("p a b -> p (a b)"), lambda: win_lo[:].rearrange("p a b -> p (a b)"),
                     lambda: p_gate[:, 0, 0:4 * C2], 1),
                    (lambda: wg_hi[:, 0:4, :].rearrange("p a b -> p (a b)"), lambda: wg_lo[:, 0:4, :].rearrange("p a b -> p (a b)"),
                     lambda: p_f[0:C2, 0, 0:4 * C2], 2),
                    (lambda: wg_hi[:, 4:8, :].rearrange("p a b -> p (a b)"), lambda: wg_lo[:, 4:8, :].rearrange("p a b -> p (a b)"),
                     lambda: p_f[0:C2, 1, 0:4 * C2], 2),
                    (lambda: wo_hi[:].rearrange("p a b -> p (a b)"), lambda: wo_lo[:].rearrange("p a b -> p (a b)"),
                     lambda: p_i[0:C2, 0, 0:2 * P], 3),
                ]

                @block.scalar
                def _(act):
                    for hi, lo, src, need in splits:
                        act.wait_ge(s_wt, need)
                        nc.scalar.activation(hi(), src(), ACT.Copy).then_inc(s_wh, 1)
                    act.wait_ge(s_ld, 7 * 16)
                    nc.scalar.activation(spt[:], fb[:], ACT.Abs).then_inc(s_sp, 1)
                    act.wait_ge(s_sp, 1)
                    nc.scalar.activation(spt[:], spt[:], ACT.Exp, scale=-1.0).then_inc(s_sp, 1)
                    act.wait_ge(s_sp, 2)
                    nc.scalar.activation(spt[:], spt[:], ACT.Ln, bias=1.0).then_inc(s_sp, 1)

                @block.vector
                def _(dve):
                    for k, (hi, lo, src, need) in enumerate(splits):
                        dve.wait_ge(s_wh, k + 1)
                        nc.vector.tensor_tensor(lo(), src(), raw(hi()), ALU.subtract).then_inc(s_wl, 1)
                    dve.wait_ge(s_ld, 7 * 16)
                    nc.vector.memset(xp[:], 0.0)
                    nc.vector.memset(one_eps[:], 1.0 + BETA_EPS)
                    nc.vector.tensor_scalar(bg[:], bg[:], 0.5, None, ALU.mult)
                    nc.vector.tensor_scalar(kf[:], fb[:], 0.0, None, ALU.max).then_inc(s_small, 1)
                    dve.wait_ge(s_sp, 3)
                    dve.wait_ge(s_small, 1)
                    nc.vector.tensor_tensor(kf[:], kf[:], spt[:], ALU.add).then_inc(s_small, 1)
                    dve.wait_ge(s_small, 2)
                    nc.vector.tensor_scalar(kf[:], kf[:], -ALPHA_SCALE / 2, None, ALU.mult).then_inc(s_small, 1)

            s_proj = sem("r_projected")
            s_xp = sem("r_conv_input")
            s_xb = sem("r_conv_step")
            s_xh = sem("r_conv_high")
            s_xl = sem("r_conv_low")
            s_fi = sem("r_gates_projected")
            s_tf = sem("r_forget_tanh")
            s_ti = sem("r_input_tanh")
            s_al = sem("r_alpha")
            s_a2 = sem("r_alpha_squared")
            s_be = sem("r_beta")
            s_gl = sem("r_gelu")
            s_u = sem("r_scan_input_step")
            s_h = sem("r_scanned")
            s_z = sem("r_gated")
            s_zh = sem("r_gated_high")
            s_zl = sem("r_gated_low")
            s_y = sem("r_output")
            s_yc = sem("r_output_stored")
            with nc.Block() as block:
                @block.tensor
                def _(pe):
                    def project(n):
                        for c in range(2):
                            last = mm3(p_xb[0:C2, c, :], win_hi[:, 2 + c, :], win_lo[:, 2 + c, :],
                                       x_hi[:, tile_cols(n)], x_lo[:, tile_cols(n)])
                        last.then_inc(s_proj, 1)

                    def project_gate(n):
                        for c in range(2):
                            last = mm3(p_gate[0:C2, c, :], win_hi[:, c, :], win_lo[:, c, :],
                                       x_hi[:, tile_cols(n)], x_lo[:, tile_cols(n)])
                        last.then_inc(s_proj, 1)

                    with pe.Fori(0, N) as n:
                        pe.wait_ge(s_yc, n + 1)
                        project(n)
                        project_gate(n)
                        pe.wait_ge(s_xl, n + 1)
                        for gc in range(4):
                            dst = (p_f if gc < 2 else p_i)[0:C2, gc % 2, :]
                            for hc in range(2):
                                last = mm3(dst, wg_hi[:, 4 * hc + gc, :], wg_lo[:, 4 * hc + gc, :],
                                           xb_hi[:, hc, :], xb_lo[:, hc, :], start=hc == 0, stop=hc == 1)
                        last.then_inc(s_fi, 1)
                        pe.wait_ge(s_zl, n + 1)
                        for hc in range(2):
                            last = mm3(p_xb[:, 0, :], wo_hi[:, hc, :], wo_lo[:, hc, :], z_hi[:, hc, :], z_lo[:, hc, :],
                                       start=hc == 0, stop=hc == 1)
                        last.then_inc(s_y, 1)

                @block.scalar
                def _(act):
                    act.sem_inc(s_yc, 1)
                    with act.Fori(0, N) as n:
                        act.wait_ge(s_proj, 2 * n + 1)
                        nc.scalar.activation(xp[:, :, pad:pad + T], p_xb[0:C2, :, :], ACT.Copy).then_inc(s_xp, 1)
                        act.wait_ge(s_proj, 2 * n + 2)
                        nc.scalar.activation(gl[:], p_gate[0:C2, :, :], ACT.Gelu).then_inc(s_gl, 1)
                        act.wait_ge(s_fi, n + 1)
                        for c in range(2):
                            nc.scalar.activation(tf[:, c, :], p_f[0:C2, c, :], ACT.Tanh, bias=bg[:, c:c + 1],
                                                 scale=0.5).then_inc(s_tf, 1)
                        for c in range(2):
                            nc.scalar.activation(ti[:, c, :], p_i[0:C2, c, :], ACT.Tanh, bias=bg[:, 2 + c:3 + c],
                                                 scale=0.5).then_inc(s_ti, 1)
                        for c in range(2):
                            act.wait_ge(s_tf, 2 * n + c + 1)
                            nc.scalar.activation(al[:, c, :], tf[:, c, :], ACT.Exp, bias=kf[:, c:c + 1],
                                                 scale=kf[:, c:c + 1]).then_inc(s_al, 1)
                        act.wait_ge(s_al, 2 * n + 2)
                        nc.scalar.activation(be[:], al[:], ACT.Square).then_inc(s_a2, 1)
                        act.wait_ge(s_a2, n + 1)
                        nc.scalar.activation(be[:], be[:], ACT.Sqrt, bias=one_eps[:, 0:1],
                                             scale=-1.0).then_inc(s_be, 1)
                        act.wait_ge(s_y, n + 1)
                        nc.scalar.activation(yT[:, tile_cols(n)], p_xb[:, 0, :], ACT.Copy).then_inc(s_yc, 1)

                @block.vector
                def _(dve):
                    with dve.Fori(0, N) as n:
                        dve.wait_ge(s_xp, n + 1)
                        for k in range(TAPS):
                            for c in range(2):
                                tap = xp[:, c, pad - k:pad - k + T]
                                w = cw[:, c, TAPS - 1 - k:TAPS - k]
                                if k == 0:
                                    nc.vector.tensor_scalar(xb[:, 0, c, :], tap, w, cb[:, c:c + 1], ALU.mult,
                                                            ALU.add).then_inc(s_xb, 1)
                                else:
                                    dve.wait_ge(s_xb, 2 * TAPS * n + 2 * (k - 1) + c + 1)
                                    nc.vector.scalar_tensor_tensor(out=xb[:, k % 2, c, :], in0=tap, scalar=w,
                                                                   in1=xb[:, (k - 1) % 2, c, :], op0=ALU.mult,
                                                                   op1=ALU.add).then_inc(s_xb, 1)
                        conv = xb[:, (TAPS - 1) % 2, :, :]
                        dve.wait_ge(s_xb, 2 * TAPS * n + 2 * TAPS)
                        nc.vector.tensor_copy(xb_hi[:], conv).then_inc(s_xh, 1)
                        dve.wait_ge(s_xh, n + 1)
                        nc.vector.tensor_tensor(xb_lo[:], conv, raw(xb_hi[:]), ALU.subtract).then_inc(s_xl, 1)
                        dve.wait_ge(s_ti, 2 * n + 2)
                        nc.vector.scalar_tensor_tensor(out=xs[:], in0=ti[:], scalar=1.0, in1=conv, op0=ALU.add,
                                                       op1=ALU.mult).then_inc(s_u, 1)
                        dve.wait_ge(s_u, 2 * n + 1)
                        dve.wait_ge(s_be, n + 1)
                        nc.vector.scalar_tensor_tensor(out=xs[:], in0=xs[:], scalar=0.5, in1=be[:], op0=ALU.mult,
                                                       op1=ALU.mult).then_inc(s_u, 1)
                        dve.wait_ge(s_u, 2 * n + 2)
                        for c in range(2):
                            nc.vector.tensor_tensor_scan(hs[:, c, :], al[:, c, :], xs[:, c, :], 0.0, ALU.mult,
                                                         ALU.add).then_inc(s_h, 1)
                        dve.wait_ge(s_h, 2 * n + 2)
                        dve.wait_ge(s_gl, n + 1)
                        nc.vector.tensor_tensor(z[:], gl[:], hs[:], ALU.mult).then_inc(s_z, 1)
                        dve.wait_ge(s_z, n + 1)
                        nc.vector.tensor_copy(z_hi[:], z[:]).then_inc(s_zh, 1)
                        dve.wait_ge(s_zh, n + 1)
                        nc.vector.tensor_tensor(z_lo[:], z[:], raw(z_hi[:]), ALU.subtract).then_inc(s_zl, 1)
        scope.pop()

        def split_weights(tag, parts):
            s_h = sem(tag + "weights_high")
            s_l = sem(tag + "weights_low")
            return s_h, s_l

        def experts(tag, E, up_hi, up_lo, bias_up, lin_hi, lin_lo, bias_lin, dn_hi, dn_lo, b2_hi, b2_lo, act_fn,
                    store):
            gated = lin_hi is not None
            scope.append(ExitStack())
            with scope[-1]:
                h = sb(tag + "h", [P, 2, 2, T])
                g = sb(tag + "g", [P, 2, 2, T])
                g_hi = sb(tag + "g_hi", [P, 2, 2, T], F32R)
                g_lo = sb(tag + "g_lo", [P, 2, 2, T], F32R)
                ys = sb(tag + "ys", [P, T])
                p_up = ps(tag + "p_up", [P, 2, 2, T]) if not gated else ps(tag + "p_up", [P, 1, 2, T])
                p_lin = ps(tag + "p_lin", [P, 1, 2, T]) if gated else None
                p_gate = ps(tag + "p_gate", [P, 2, T])
                p_acc = ps(tag + "p_acc", [P, T])
                p_tr = ps(tag + "p_tr", [P, T])
                B = 1 if gated else 2
                s_up = sem(tag + "up_done")
                s_h = sem(tag + "activated")
                s_lin = sem(tag + "linear_gated")
                s_g = sem(tag + "gated")
                s_hi = sem(tag + "gated_high")
                s_lo = sem(tag + "gated_low")
                s_dn = sem(tag + "down_done")
                s_ys = sem(tag + "tile_sum")
                s_tr = sem(tag + "tile_transposed")
                s_xr = sem(tag + "residual_added")
                s_out = sem(tag + "stored")

                def blocks(run):
                    run(0, first=True, last=False)
                    yield 1, N - 1
                    run(N - 1, first=False, last=True)

                with nc.Block() as block:
                    @block.tensor
                    def _(pe):
                        pe.sem_inc(s_dn, 2)

                        def up(n, e):
                            q = n * E + e
                            x_h, x_l = x_hi[:, tile_cols(n)], x_lo[:, tile_cols(n)]
                            pe.wait_ge(s_g, q + 1)
                            nc.tensor.matmul(p_gate[:, e % 2, :], sel[:, e, :], gT[:, tile_cols(n)],
                                             start=True, stop=True)
                            pe.wait_ge(s_h, q + 1)
                            for c in range(2):
                                last = mm3(p_up[:, e % B, c, :], up_hi[:, e, c, :], up_lo[:, e, c, :], x_h, x_l)
                            last.then_inc(s_up, 1)
                            if gated:
                                pe.wait_ge(s_g, q + 2)
                                for c in range(2):
                                    last = mm3(p_lin[:, 0, c, :], lin_hi[:, e, c, :], lin_lo[:, e, c, :], x_h, x_l)
                                last.then_inc(s_lin, 1)

                        def down(n, e):
                            pe.wait_ge(s_lo, n * E + e + 3)
                            if e == 0:
                                pe.wait_ge(s_ys, n + 1)
                                for k, b in enumerate((b2_hi, b2_lo)):
                                    nc.tensor.matmul(p_acc[:], b[:], gT[:, tile_cols(n)],
                                                     start=k == 0, stop=False)
                            for c in range(2):
                                last = mm3(p_acc[:], dn_hi[:, e, c, :], dn_lo[:, e, c, :], g_hi[:, e % 2, c, :],
                                           g_lo[:, e % 2, c, :], start=False, stop=(e == E - 1 and c == 1))
                            last.then_inc(s_dn, 1)

                        def turn_back(n):
                            pe.wait_ge(s_ys, n + 2)
                            pe.wait_ge(s_xr, n + 1)
                            for j in range(J):
                                last = nc.tensor.transpose(p_tr[:, j * P:(j + 1) * P], ys[:, j * P:(j + 1) * P],
                                                           ident[:])
                            last.then_inc(s_tr, 1)

                        def tile(n, first, last):
                            if first:
                                up(n, 0)
                                up(n, 1)
                            for k in range(2, E + 2):
                                if k < E:
                                    up(n, k)
                                elif not last:
                                    up(n + 1, k - E)
                                if k == 5 and not first:
                                    turn_back(n - 1)
                                down(n, k - 2)
                            if last:
                                turn_back(n)

                        tile(0, True, False)
                        with pe.Fori(1, N - 1) as n:
                            tile(n, False, False)
                        tile(N - 1, False, True)

                    @block.scalar
                    def _(act):
                        act.sem_inc(s_h, B)

                        def activate(n, e):
                            q = n * E + e
                            act.wait_ge(s_up, q + 1)
                            act.wait_ge(s_g, q + 1)
                            for c in range(2):
                                last = nc.scalar.activation(h[:, e % 2, c, :], p_up[:, e % B, c, :], act_fn,
                                                            bias=bias_up[:, e, c:c + 1])
                            last.then_inc(s_h, 1)

                        def high(n, e):
                            q = n * E + e
                            act.wait_ge(s_g, q + 3)
                            act.wait_ge(s_dn, q + 1)
                            nc.scalar.activation(g_hi[:, e % 2, :, :], g[:, e % 2, :, :], ACT.Copy).then_inc(s_hi, 1)

                        def tile(n, first, last):
                            if first:
                                activate(n, 0)
                            for k in range(1, E + 1):
                                if k < E:
                                    activate(n, k)
                                elif not last:
                                    activate(n + 1, 0)
                                high(n, k - 1)

                        tile(0, True, False)
                        with act.Fori(1, N - 1) as n:
                            tile(n, False, False)
                        tile(N - 1, False, True)

                    @block.vector
                    def _(dve):
                        dve.sem_inc(s_g, 2)
                        dve.sem_inc(s_lo, 2)
                        dve.sem_inc(s_ys, 1)
                        dve.sem_inc(s_xr, 1)

                        def gate(n, e):
                            q = n * E + e
                            dve.wait_ge(s_h, q + B + 1)
                            dve.wait_ge(s_lo, q + 1)
                            if not gated:
                                nc.vector.tensor_tensor(g[:, e % 2, :, :], h[:, e % 2, :, :],
                                                        p_gate[:, e % 2, :].unsqueeze(1).broadcast_to([P, 2, T]),
                                                        ALU.mult).then_inc(s_g, 1)
                            else:
                                nc.vector.tensor_tensor(h[:, e % 2, :, :], h[:, e % 2, :, :],
                                                        p_gate[:, e % 2, :].unsqueeze(1).broadcast_to([P, 2, T]),
                                                        ALU.mult).then_inc(s_hg, 1)
                                dve.wait_ge(s_hg, q + 1)
                                dve.wait_ge(s_lin, q + 1)
                                for c in range(2):
                                    last = nc.vector.scalar_tensor_tensor(
                                        out=g[:, e % 2, c, :], in0=p_lin[:, 0, c, :], scalar=bias_lin[:, e, c:c + 1],
                                        in1=h[:, e % 2, c, :], op0=ALU.add, op1=ALU.mult)
                                last.then_inc(s_g, 1)

                        def low(n, e):
                            q = n * E + e
                            dve.wait_ge(s_hi, q + 1)
                            dve.wait_ge(s_dn, q + 1)
                            nc.vector.tensor_tensor(g_lo[:, e % 2, :, :], g[:, e % 2, :, :], raw(g_hi[:, e % 2, :, :]),
                                                    ALU.subtract).then_inc(s_lo, 1)

                        def tile_sum(n):
                            dve.wait_ge(s_dn, n * E + E + 2)
                            dve.wait_ge(s_xr, n + 1)
                            nc.vector.tensor_tensor(ys[:], p_acc[:], yT[:, tile_cols(n)], ALU.add).then_inc(s_ys, 1)

                        def residual(n):
                            dve.wait_ge(s_tr, n + 1)
                            rows = xres[:, bass.ds(n * J, J), :]
                            nc.vector.tensor_tensor(rows, p_tr[:].rearrange("p (j d) -> p j d", j=J), rows,
                                                    ALU.add).then_inc(s_xr, 1)

                        def tile(n, first, last):
                            if first:
                                gate(n, 0)
                            for k in range(1, E + 1):
                                if k < E:
                                    gate(n, k)
                                elif not last:
                                    gate(n + 1, 0)
                                low(n, k - 1)
                                if not first and k == 1:
                                    tile_sum(n - 1)
                                if not first and k == 6:
                                    residual(n - 1)
                            if last:
                                tile_sum(n)
                                residual(n)

                        s_hg = s_halfgated
                        tile(0, True, False)
                        with dve.Fori(1, N - 1) as n:
                            tile(n, False, False)
                        tile(N - 1, False, True)

                    if store:
                        @block.sync
                        def _(sp):
                            with sp.Fori(0, N) as n:
                                sp.wait_ge(s_xr, n + 2)
                                sp.dma_start(out[bass.ds(n, 1)].rearrange("a (j p) d -> p (a j) d", p=P),
                                             xres[:, bass.ds(n * J, J), :]).then_inc(s_out, 16)
                            sp.wait_ge(s_out, 16 * N)
            scope.pop()

        s_halfgated = sem("half_gated")

        def split_parts(parts, s_hi, s_lo, block, before=0, s_before=None):
            @block.scalar
            def _(act):
                if s_before is not None:
                    act.wait_ge(s_before, before)
                for hi, lo, src in parts:
                    nc.scalar.activation(hi, src, ACT.Copy).then_inc(s_hi, 1)

            @block.vector
            def _(dve):
                for k, (hi, lo, src) in enumerate(parts):
                    dve.wait_ge(s_hi, k + 1)
                    nc.vector.tensor_tensor(lo, src, raw(hi), ALU.subtract).then_inc(s_lo, 1)

        scope.append(ExitStack())
        with scope[-1]:
            w1_hi = sb("w1_hi", [P, E0, 2, P], F32R)
            w1_lo = sb("w1_lo", [P, E0, 2, P], F32R)
            w2_hi = sb("w2_hi", [P, E0, 2, P], F32R)
            w2_lo = sb("w2_lo", [P, E0, 2, P], F32R)
            b1T = sb("b1T", [P, E0, 2])
            b2_hi = sb("b2_hi", [P, D], F32R)
            b2_lo = sb("b2_lo", [P, D], F32R)
            scope.append(ExitStack())
            with scope[-1]:
                w_raw = sb("w_raw", [P, E0, 2, P])
                w2_raw = sb("w2_raw", [P, E0, 2, P])
                b1_raw = sb("b1_raw", [2 * E0, P])
                b2_raw = sb("b2_raw", [P, D])
                p_b1 = ps("p_b1", [P, 2 * E0])
                s_ew = sem("e0_loaded")
                s_b2z = sem("e0_bias_zeroed")
                s_ewh = sem("e0_high")
                s_ewl = sem("e0_low")
                s_b1t = sem("e0_bias_transposed")
                with nc.Block() as block:
                    @block.sync
                    def _(sp):
                        sp.dma_start(w_raw[:].rearrange("p e c m -> p e (c m)"),
                                     w1.rearrange("e h i -> h e i")).then_inc(s_ew, 16)
                        sp.dma_start(w2_raw[:], w2.rearrange("e (c p) d -> p e c d", p=P)).then_inc(s_ew, 16)
                        sp.dma_start(b1_raw[:], b1.rearrange("e (c p) -> (e c) p", p=P)).then_inc(s_ew, 16)
                        sp.wait_ge(s_b2z, 1)
                        for k in range(2):
                            sp.dma_start(b2_raw[16 * k:16 * k + E0, :], b2).then_inc(s_ew, 16)
                        sp.wait_ge(s_ew, 5 * 16)

                    @block.tensor
                    def _(pe):
                        pe.wait_ge(s_ew, 5 * 16)
                        nc.tensor.transpose(p_b1[:], b1_raw[:], ident[0:2 * E0, 0:2 * E0]).then_inc(s_b1t, 1)

                    parts = [(w1_hi[:], w1_lo[:], w_raw[:]), (w2_hi[:], w2_lo[:], w2_raw[:]),
                             (b2_hi[:], b2_lo[:], b2_raw[:])]

                    @block.scalar
                    def _(act):
                        act.wait_ge(s_ew, 5 * 16)
                        for hi, lo, src in parts:
                            nc.scalar.activation(hi, src, ACT.Copy).then_inc(s_ewh, 1)

                    @block.vector
                    def _(dve):
                        nc.vector.memset(b2_raw[:], 0.0).then_inc(s_b2z, 1)
                        for k, (hi, lo, src) in enumerate(parts):
                            dve.wait_ge(s_ewh, k + 1)
                            nc.vector.tensor_tensor(lo, src, raw(hi), ALU.subtract).then_inc(s_ewl, 1)
                        dve.wait_ge(s_b1t, 1)
                        nc.vector.tensor_copy(b1T[:].rearrange("p e c -> p (e c)"), p_b1[:]).then_inc(s_ewl, 1)
            scope.pop()
            experts("e0_", E0, w1_hi, w1_lo, b1T, None, None, None, w2_hi, w2_lo, b2_hi, b2_lo, ACT.Gelu, False)
        scope.pop()

        norm_and_route("b_", E1, K1, Wg, True, None)

        scope.append(ExitStack())
        with scope[-1]:
            wq_raw = sb("wq_raw", [D, NQ, DH])
            wk_raw = sb("wk_raw", [D, DH])
            wv_raw = sb("wv_raw", [D, DH])
            wp_raw = sb("wp_raw", [NQ * DH, D])
            bp_col = sb("bp_col", [D, 1])
            wq_rep = sb("wq_rep", [D, NQ // 2, 2, 4, DH])
            wk_rep = sb("wk_rep", [D, 8, DH])
            wv_rep = sb("wv_rep", [D, 8, DH])
            wq_hi = sb("wq_hi", [D, NQ // 2, P], F32R)
            wq_lo = sb("wq_lo", [D, NQ // 2, P], F32R)
            wk_hi = sb("wk_hi", [D, P], F32R)
            wk_lo = sb("wk_lo", [D, P], F32R)
            wv_hi = sb("wv_hi", [D, P], F32R)
            wv_lo = sb("wv_lo", [D, P], F32R)
            wp_hi = sb("wp_hi", [D, P], F32R)
            wp_lo = sb("wp_lo", [D, P], F32R)
            part = sb("part", [P, 1], I32)
            bit = sb("bit", [P, 2], I32)
            q_m = sb("q_m", [P, 1])
            k_m = sb("k_m", [P, 1])
            idb = sb("idb", [P, P], BF16)
            mask_t = sb("mask_t", [P, P], BF16)
            mask_s = sb("mask_s", [P, P], BF16)
            nsel_f = sb("nsel_f", [P, NQ, P])
            nsel = sb("nsel", [P, NQ, P], F32R)
            qs = sb("qs", [P, NQ // 2, T], F32R)
            kz = sb("kz", [P, 2, T], F32R)
            ktmp = sb("ktmp", [P, T], F32R)
            qtmp = sb("qtmp", [P, T], F32R)
            vT = sb("vT", [P, T])
            va = sb("va", [P, NQ, J, P])
            mxs = sb("mxs", [P, J, NQ])
            mx_hi = sb("mx_hi", [P, J, NQ], F32R)
            mx2 = sb("mx2", [P, J, P])
            mT = sb("mT", [P, T], F32R)
            ex = sb("ex", [P, 2, 1280])
            rd = sb("rd", [P, T])
            at = sb("at", [P, T])
            at_hi = sb("at_hi", [P, T], F32R)
            at_lo = sb("at_lo", [P, T], F32R)
            p_a = ps("p_a", [P, T])
            p_s = ps("p_s", [P, 3 * T])
            p_st = ps("p_st", [P, 3 * T])
            p_o = ps("p_o", [P, T])

            COL = {0: 0, 1: T, 3: T + 3 * P, 2: 2 * T}
            CMAX = {3: 0, 2: T, 0: T + 3 * P, 1: 2 * T}
            WID = {b: T - P * b for b in range(J)}

            s_al_ = sem("t_loaded")
            s_rep = sem("t_replicated")
            s_th = sem("t_high")
            s_tl = sem("t_low")
            s_io = sem("t_iota")
            s_pm = sem("t_mask_zero")
            s_pm2 = sem("t_masks_made")
            s_bits = sem("t_bits")
            wparts = [(wq_hi[:].rearrange("p a b -> p (a b)"), wq_lo[:].rearrange("p a b -> p (a b)"),
                       wq_rep[:].rearrange("p a b c d -> p (a b c d)")),
                      (wk_hi[:], wk_lo[:], wk_rep[:].rearrange("p a b -> p (a b)")),
                      (wv_hi[:], wv_lo[:], wv_rep[:].rearrange("p a b -> p (a b)")),
                      (wp_hi[:], wp_lo[:], wp_raw[:])]
            with nc.Block() as block:
                @block.sync
                def _(sp):
                    sp.dma_start(wq_raw[:], Wq.rearrange("q c d -> c q d")).then_inc(s_al_, 16)
                    sp.dma_start(wk_raw[:], Wk).then_inc(s_al_, 16)
                    sp.dma_start(wv_raw[:], Wv).then_inc(s_al_, 16)
                    sp.dma_start(wp_raw[:], Wp).then_inc(s_al_, 16)
                    with nc.allow_non_contiguous_dma(reason="128 bias values"):
                        sp.dma_start(bp_col[:], bp.rearrange("(p a) -> p a", a=1)).then_inc(s_al_, 16)
                    sp.wait_ge(s_al_, 5 * 16)

                @block.gpsimd
                def _(pool):
                    pool.iota(part[:], pattern=[[0, 1]], base=0, channel_multiplier=1).then_inc(s_io, 1)
                    pool.memset(idb[:], 0.0).then_inc(s_pm, 1)
                    pool.memset(mask_t[:], 0.0).then_inc(s_pm, 1)
                    pool.memset(mask_s[:], 0.0).then_inc(s_pm, 1)
                    pool.memset(nsel_f[:], 0.0).then_inc(s_pm, 1)
                    pool.wait_ge(s_pm, 4)
                    pool.affine_select(out=idb[:], in_=idb[:], compare_op=ALU.not_equal, fill=1.0, base=0,
                                       pattern=[[-1, P]], channel_multiplier=1).then_inc(s_pm2, 1)
                    pool.affine_select(out=mask_t[:], in_=mask_t[:], compare_op=ALU.is_ge, fill=MASKED, base=0,
                                       pattern=[[-1, P]], channel_multiplier=1).then_inc(s_pm2, 1)
                    pool.affine_select(out=mask_s[:], in_=mask_s[:], compare_op=ALU.is_ge, fill=MASKED, base=0,
                                       pattern=[[1, P]], channel_multiplier=-1).then_inc(s_pm2, 1)
                    for k, base in enumerate((0, -NQ)):
                        pool.wait_ge(s_pm2, 3 + k)
                        pool.affine_select(out=nsel_f[:], in_=nsel_f[:], compare_op=ALU.not_equal, fill=-1.0,
                                           base=base, pattern=[[-1, NQ], [0, P]],
                                           channel_multiplier=1).then_inc(s_pm2, 1)
                    pool.wait_ge(s_pm2, 5)
                    pool.tensor_copy(nsel[:], nsel_f[:]).then_inc(s_pm2, 1)

                @block.vector
                def _(dve):
                    dve.wait_ge(s_al_, 5 * 16)
                    nc.vector.tensor_copy(wq_rep[:].rearrange("p a b c d -> p (a b) c d"),
                                          wq_raw[:].unsqueeze(2).broadcast_to([D, NQ, 4, DH])).then_inc(s_rep, 1)
                    nc.vector.tensor_copy(wk_rep[:], wk_raw[:].unsqueeze(1).broadcast_to([D, 8, DH])).then_inc(s_rep, 1)
                    nc.vector.tensor_copy(wv_rep[:], wv_raw[:].unsqueeze(1).broadcast_to([D, 8, DH])).then_inc(s_rep, 1)
                    dve.wait_ge(s_io, 1)
                    nc.vector.tensor_scalar(bit[:, 0:1], part[:], 4, 1, ALU.logical_shift_right,
                                            ALU.bitwise_and).then_inc(s_bits, 1)
                    nc.vector.tensor_scalar(bit[:, 1:2], part[:], 5, 1, ALU.logical_shift_right,
                                            ALU.bitwise_and).then_inc(s_bits, 1)
                    dve.wait_ge(s_bits, 2)
                    nc.vector.tensor_scalar(q_m[:], bit[:, 0:1], -1.0, None, ALU.mult).then_inc(s_bits, 1)
                    nc.vector.tensor_scalar(k_m[:], bit[:, 1:2], -1.0, None, ALU.mult).then_inc(s_bits, 1)
                    nc.vector.memset(raw(kz[:]), 0.0)
                    nc.vector.memset(mx2[:], 0.0)
                    nc.vector.memset(va[:], 0.0).then_inc(s_bits, 1)
                    dve.wait_ge(s_bits, 5)
                    for hd in range(NQ):
                        one = (64 if hd < 4 else 0) + DH * (hd % 4)
                        nc.vector.memset(va[:, hd, :, one:one + DH], 1.0)
                    for k, (hi, lo, src) in enumerate(wparts):
                        dve.wait_ge(s_th, k + 1)
                        nc.vector.tensor_tensor(lo, src, raw(hi), ALU.subtract).then_inc(s_tl, 1)

                @block.scalar
                def _(act):
                    act.wait_ge(s_rep, 3)
                    act.wait_ge(s_al_, 5 * 16)
                    for hi, lo, src in wparts:
                        nc.scalar.activation(hi, src, ACT.Copy).then_inc(s_th, 1)

            s_pa = sem("t_projected")
            s_pah = sem("t_projection_high")
            s_pad = sem("t_projection_used")
            s_sc = sem("t_scores")
            s_mx = sem("t_maxima")
            s_m1 = sem("t_maxima_high")
            s_m2 = sem("t_maxima_split")
            s_mt = sem("t_maxima_transposed")
            s_mc = sem("t_maxima_rows")
            s_va = sem("t_values_placed")
            s_ss = sem("t_shifted_scores")
            s_ex = sem("t_exp")
            s_pv = sem("t_values_summed")
            s_rd = sem("t_reciprocal")
            s_at = sem("t_normalised")
            s_ah = sem("t_out_high")
            s_all = sem("t_out_low")
            s_yo = sem("t_out_projected")
            s_ys_ = sem("t_out_stored")
            NPA = NQ // 2 + 5
            with nc.Block() as block:
                @block.tensor
                def _(pe):
                    with pe.Fori(0, N) as n:
                        x_h, x_l = x_hi[:, tile_cols(n)], x_lo[:, tile_cols(n)]
                        use = [0]

                        def claim():
                            use[0] += 1
                            pe.wait_ge(s_pad, n * NPA + use[0])

                        for w_hi_, w_lo_ in [(wk_hi[:], wk_lo[:])] + \
                                [(wq_hi[:, g, :], wq_lo[:, g, :]) for g in range(NQ // 2)] + [(wv_hi[:], wv_lo[:])]:
                            claim()
                            mm3(p_a[:], w_hi_, w_lo_, x_h, x_l).then_inc(s_pa, 1)
                        claim()
                        for j in range(J):
                            last = nc.tensor.transpose(p_a[:, j * P:(j + 1) * P], vT[:, j * P:(j + 1) * P], ident[:])
                        last.then_inc(s_pa, 1)
                        for hd in range(NQ):
                            pe.wait_ge(s_mx, n * NQ + hd + 1)
                            for b in (3, 2, 0, 1):
                                w = (b + 1) * P
                                q_blk = qs[:, hd // 2, b * P:(b + 1) * P]
                                nc.tensor.matmul(p_s[:, CMAX[b]:CMAX[b] + w], q_blk, kz[:, hd % 2, 0:w],
                                                 start=True, stop=False)
                                last = nc.tensor.matmul(p_s[:, CMAX[b] + b * P:CMAX[b] + w], idb[:], mask_t[:],
                                                        start=False, stop=True)
                            last.then_inc(s_sc, 1)
                        claim()
                        pe.wait_ge(s_m2, 2 * n + 2)
                        for j in range(J):
                            last = nc.tensor.transpose(p_a[:, j * P:(j + 1) * P], mx2[:, j, :], ident[:])
                        last.then_inc(s_mt, 1)
                        pe.wait_ge(s_mc, n + 1)

                        def shifted(hd):
                            pe.wait_ge(s_ex, n * NQ + hd + 1)
                            for b in (0, 1, 3, 2):
                                c0 = COL[b]
                                nc.tensor.matmul(p_st[:, c0:c0 + WID[b]], kz[:, hd % 2, b * P:(b + 1) * P],
                                                 qs[:, hd // 2, b * P:T], start=True, stop=False)
                                nc.tensor.matmul(p_st[:, c0:c0 + WID[b]], nsel[:, hd, :], mT[:, b * P:T],
                                                 start=False, stop=False)
                                last = nc.tensor.matmul(p_st[:, c0:c0 + P], idb[:], mask_s[:], start=False, stop=True)
                            last.then_inc(s_ss, 1)

                        def weigh(hd):
                            pe.wait_ge(s_ex, n * NQ + hd + 2)
                            if hd % 4 == 0:
                                pe.wait_ge(s_at, 2 * n + hd // 4 + 1)
                            for b in range(J):
                                last = nc.tensor.matmul(p_o[:, b * P:T], va[:, hd, b, :],
                                                        ex[:, hd % 2, COL[b]:COL[b] + WID[b]],
                                                        start=(hd % 4 == 0 and b == 0), stop=(hd % 4 == 3 and b == J - 1))
                            last.then_inc(s_pv, 1)

                        shifted(0)
                        pe.wait_ge(s_va, n + 1)
                        for hd in range(1, NQ):
                            shifted(hd)
                            weigh(hd - 1)
                        weigh(NQ - 1)
                        pe.wait_ge(s_all, n + 1)
                        claim()
                        mm3(p_a[:], wp_hi[:], wp_lo[:], at_hi[:], at_lo[:]).then_inc(s_yo, 1)

                @block.scalar
                def _(act):
                    act.sem_inc(s_ex, 1)
                    with act.Fori(0, N) as n:
                        act.wait_ge(s_pa, n * (NQ // 2 + 3) + 1)
                        nc.scalar.activation(ktmp[:], p_a[:], ACT.Copy).then_inc(s_pah, 1)
                        for g in range(NQ // 2):
                            act.wait_ge(s_pa, n * (NQ // 2 + 3) + 2 + g)
                            nc.scalar.activation(qtmp[:], p_a[:], ACT.Copy).then_inc(s_pah, 1)
                        for hd in range(NQ):
                            act.wait_ge(s_ss, n * NQ + hd + 1)
                            if hd >= 2:
                                act.wait_ge(s_pv, n * NQ + hd - 1)
                            nc.scalar.activation(ex[:, hd % 2, :], p_st[:, 0:1280], ACT.Exp,
                                                 scale=SCALE).then_inc(s_ex, 1)

                @block.vector
                def _(dve):
                    dve.sem_inc(s_pad, 1)
                    dve.sem_inc(s_mx, 1)
                    dve.sem_inc(s_at, 1)
                    with dve.Fori(0, N) as n:
                        dve.wait_ge(s_pah, n * (NQ // 2 + 1) + 1)
                        for half in range(2):
                            r = slice(64 * half, 64 * half + 64)
                            last = nc.vector.scalar_tensor_tensor(out=kz[r, half, :], in0=raw(ktmp[r, :]), scalar=k_m[r, :],
                                                                  in1=p_a[r, :], op0=ALU.mult, op1=ALU.add)
                        last.then_inc(s_pad, 1)
                        for g in range(NQ // 2):
                            dve.wait_ge(s_pah, n * (NQ // 2 + 1) + 2 + g)
                            nc.vector.scalar_tensor_tensor(out=qs[:, g, :], in0=raw(qtmp[:]), scalar=q_m[:],
                                                           in1=p_a[:], op0=ALU.mult, op1=ALU.add).then_inc(s_pad, 1)
                        dve.wait_ge(s_pa, n * (NQ // 2 + 3) + NQ // 2 + 2)
                        nc.vector.tensor_copy(vT[:], p_a[:]).then_inc(s_pad, 1)
                        dve.wait_ge(s_pa, n * (NQ // 2 + 3) + NQ // 2 + 3)
                        for hd in range(NQ):
                            c0 = (0 if hd < 4 else 64) + DH * (hd % 4)
                            last = nc.vector.tensor_copy(va[:, hd, :, c0:c0 + DH],
                                                         p_a[:].rearrange("p (j c) -> p j c", j=J)[:, :, 0:DH])
                            if hd == NQ - 2:
                                last.then_inc(s_va, 1)
                        last.then_inc(s_pad, 1)
                        for hd in range(NQ):
                            dve.wait_ge(s_sc, n * NQ + hd + 1)
                            for b in range(J):
                                last = nc.vector.tensor_reduce(out=mxs[:, b, hd:hd + 1],
                                                               in_=p_s[:, CMAX[b]:CMAX[b] + (b + 1) * P],
                                                               op=ALU.max, axis=AX.X)
                            last.then_inc(s_mx, 1)
                        dve.wait_ge(s_mx, n * NQ + NQ + 1)
                        nc.vector.tensor_copy(mx_hi[:], mxs[:]).then_inc(s_m1, 1)
                        dve.wait_ge(s_m1, n + 1)
                        nc.vector.tensor_copy(mx2[:, :, 0:NQ], raw(mx_hi[:])).then_inc(s_m2, 1)
                        nc.vector.tensor_tensor(mx2[:, :, NQ:2 * NQ], mxs[:], raw(mx_hi[:]), ALU.subtract).then_inc(s_m2, 1)
                        dve.wait_ge(s_mt, n + 1)
                        nc.vector.tensor_copy(mT[:], p_a[:]).then_inc(s_mc, 1)
                        dve.wait_ge(s_mc, n + 1)
                        dve.sem_inc(s_pad, 1)
                        for half in range(2):
                            num = slice(64 * half, 64 * half + 64)
                            den = slice(64 - 64 * half, 128 - 64 * half)
                            dve.wait_ge(s_pv, n * NQ + 4 * half + 4)
                            nc.vector.reciprocal(rd[num, :], p_o[den, :]).then_inc(s_rd, 1)
                            dve.wait_ge(s_rd, 2 * n + half + 1)
                            nc.vector.tensor_tensor(at[num, :], p_o[num, :], rd[num, :], ALU.mult).then_inc(s_at, 1)
                        dve.wait_ge(s_at, 2 * n + 3)
                        nc.vector.tensor_copy(at_hi[:], at[:]).then_inc(s_ah, 1)
                        dve.wait_ge(s_ah, n + 1)
                        nc.vector.tensor_tensor(at_lo[:], at[:], raw(at_hi[:]), ALU.subtract).then_inc(s_all, 1)
                        dve.wait_ge(s_yo, n + 1)
                        nc.vector.tensor_scalar(yT[:, tile_cols(n)], p_a[:], bp_col[:], None,
                                                ALU.add).then_inc(s_pad, 1)

        scope.pop()

        scope.append(ExitStack())
        with scope[-1]:
            g1_hi = sb("g1_hi", [P, E1, 2, P], F32R)
            g1_lo = sb("g1_lo", [P, E1, 2, P], F32R)
            g3_hi = sb("g3_hi", [P, E1, 2, P], F32R)
            g3_lo = sb("g3_lo", [P, E1, 2, P], F32R)
            g2_hi = sb("g2_hi", [P, E1, 2, P], F32R)
            g2_lo = sb("g2_lo", [P, E1, 2, P], F32R)
            bT = sb("bT", [P, 2, E1, 2])
            b2b_hi = sb("b2b_hi", [P, D], F32R)
            b2b_lo = sb("b2b_lo", [P, D], F32R)
            scope.append(ExitStack())
            with scope[-1]:
                wr = sb("wr", [P, 3, E1, 2, P])
                br = sb("br", [P, 3, 2 * E1, 32])
                az = sb("az", [P, 2, 4, 4, P])
                az2 = sb("az2", [P, 2, 4, 2 * P])
                bt = sb("bt", [P, 10, P])
                bi_raw = sb("bi_raw", [4 * E1, P])
                b2b_raw = sb("b2b_raw", [P, D])
                p_bt = ps("p_bt", [P, 2, 4, P])
                p_w = ps("p_w", [P, 4, 4, P])
                p_bi = ps("p_bi", [P, 4 * E1])
                s_z = sem("m_zeroed")
                s_zp = sem("m_zeroed_pool")
                s_l = sem("m_loaded")
                s_bt = sem("m_b_transposed")
                s_btc = sem("m_b_stored")
                s_w = sem("m_merged")
                s_wh = sem("m_high")
                s_wl = sem("m_low")
                s_bi = sem("m_bias_transposed")
                NLD = 3 + 3 + 8 + 4 + 2 + 2
                with nc.Block() as block:
                    @block.gpsimd
                    def _(pool):
                        pool.memset(az[:], 0.0).then_inc(s_zp, 1)
                        pool.memset(az2[:], 0.0).then_inc(s_zp, 1)

                    @block.sync
                    def _(sp):
                        for k, w in enumerate((W1, W3)):
                            sp.dma_start(wr[:, k, :, :, :], w.rearrange("e (c p) d -> p e c d", p=P)).then_inc(s_l, 16)
                        sp.dma_start(wr[:, 2, :, :, :].rearrange("p e c m -> p e (c m)"),
                                     W2.rearrange("e d i -> d e i")).then_inc(s_l, 16)
                        sp.dma_start(bi_raw[0:2 * E1, :], b1_1.rearrange("e (c p) -> (e c) p", p=P)).then_inc(s_l, 16)
                        sp.dma_start(bi_raw[2 * E1:4 * E1, :], b3_1.rearrange("e (c p) -> (e c) p", p=P)).then_inc(s_l, 16)
                        sp.wait_ge(s_z, 2)
                        for k in range(2):
                            sp.dma_start(b2b_raw[16 * k:16 * k + E1, :], b2_1).then_inc(s_l, 16)
                        for k, b in enumerate((B1, B3)):
                            sp.dma_start(br[:, k, :, 0:R], b.rearrange("e (c p) r -> p (e c) r", p=P)).then_inc(s_l, 16)
                        sp.dma_start(br[:, 2, 0:E1, 0:R], B2.rearrange("e p r -> p e r")).then_inc(s_l, 16)
                        sp.wait_ge(s_zp, 2)
                        for k, a in enumerate((A1, A3)):
                            av = a.rearrange("(g f) r d -> f r g d", f=2)
                            for j in range(4):
                                sp.dma_start(az[32 * j:32 * j + R, k, :, j, :], av[j // 2]).then_inc(s_l, 16)
                        a2v = A2.rearrange("(g f) r h -> f r g h", f=4)
                        for j in range(4):
                            sp.dma_start(az2[32 * j:32 * j + R, :, j, :], a2v[j]).then_inc(s_l, 16)
                        sp.wait_ge(s_l, NLD * 16)

                    @block.tensor
                    def _(pe):
                        pe.wait_ge(s_l, NLD * 16)
                        nc.tensor.transpose(p_bi[:], bi_raw[:], ident[0:4 * E1, 0:4 * E1]).then_inc(s_bi, 1)
                        for t in range(10):
                            if t % 4 == 0 and t >= 8:
                                pe.wait_ge(s_btc, 1)
                            k, grp = (t // 4, t % 4)
                            last = nc.tensor.transpose(p_bt[:, (t // 4) % 2, t % 4, :],
                                                       br[:, k, 4 * grp:4 * grp + 4, :].rearrange("p a b -> p (a b)"),
                                                       ident[:])
                            if t in (3, 7, 9):
                                last.then_inc(s_bt, 1)
                        pe.wait_ge(s_btc, 3)
                        for s in range(12):
                            kind, pair = s // 4, s % 4
                            if s >= 4:
                                pe.wait_ge(s_wl, s - 3)
                            for m in range(4):
                                e, c = 2 * pair + m // 2, m % 2
                                dst = p_w[:, s % 4, m, :]
                                nc.tensor.matmul(dst, wr[:, kind, e, c, :], ident[:], start=True, stop=False)
                                if kind < 2:
                                    a, b = az[:, kind, pair, m, :], bt[:, 4 * kind + pair, :]
                                else:
                                    a, b = az2[:, e // 4, e % 4, c * P:(c + 1) * P], bt[:, 8 + e // 4, :]
                                last = nc.tensor.matmul(dst, a, b, start=False, stop=True)
                            last.then_inc(s_w, 1)

                    def target(s):
                        kind, pair = s // 4, s % 4
                        hi = (g1_hi, g3_hi, g2_hi)[kind][:, 2 * pair:2 * pair + 2, :, :]
                        lo = (g1_lo, g3_lo, g2_lo)[kind][:, 2 * pair:2 * pair + 2, :, :]
                        return [v.rearrange("p e c m -> p (e c) m") for v in (hi, lo)]

                    @block.scalar
                    def _(act):
                        for s in range(12):
                            act.wait_ge(s_w, s + 1)
                            nc.scalar.activation(target(s)[0], p_w[:, s % 4, :, :], ACT.Copy).then_inc(s_wh, 1)
                        act.wait_ge(s_l, NLD * 16)
                        nc.scalar.activation(b2b_hi[:], b2b_raw[:], ACT.Copy).then_inc(s_wh, 1)

                    @block.vector
                    def _(dve):
                        nc.vector.memset(br[:], 0.0).then_inc(s_z, 1)
                        nc.vector.memset(b2b_raw[:], 0.0).then_inc(s_z, 1)
                        for t, (a, w) in enumerate(((0, 4), (4, 4), (8, 2))):
                            dve.wait_ge(s_bt, t + 1)
                            nc.vector.tensor_copy(bt[:, a:a + w, :], p_bt[:, t % 2, 0:w, :]).then_inc(s_btc, 1)
                        dve.wait_ge(s_bi, 1)
                        nc.vector.tensor_copy(bT[:].rearrange("p a e c -> p (a e c)"), p_bi[:])
                        for s in range(12):
                            dve.wait_ge(s_wh, s + 1)
                            hi, lo = target(s)
                            nc.vector.tensor_tensor(lo, p_w[:, s % 4, :, :], raw(hi), ALU.subtract).then_inc(s_wl, 1)
                        dve.wait_ge(s_wh, 13)
                        nc.vector.tensor_tensor(b2b_lo[:], b2b_raw[:], raw(b2b_hi[:]), ALU.subtract).then_inc(s_wl, 1)
            scope.pop()
            experts("e1_", E1, g1_hi, g1_lo, bT[:, 0], g3_hi, g3_lo, bT[:, 1], g2_hi, g2_lo, b2b_hi, b2b_lo,
                    ACT.Silu, True)
        scope.pop()


_INS = ['L0_attn_x', 'L0_attn_W_in', 'L0_attn_conv_w', 'L0_attn_conv_b', 'L0_attn_W_g', 'L0_attn_b_g',
        'L0_attn_forget_base', 'L0_attn_W_out', 'L0_ffn_router_w', 'L0_ffn_router_b', 'L0_ffn_w1', 'L0_ffn_b1',
        'L0_ffn_w2', 'L0_ffn_b2', 'L1_attn_Wk', 'L1_attn_Wv', 'L1_attn_Wq', 'L1_attn_Wp', 'L1_attn_bp',
        'L1_ffn_Wg', 'L1_ffn_W1', 'L1_ffn_b1', 'L1_ffn_A1', 'L1_ffn_B1', 'L1_ffn_W2', 'L1_ffn_b2', 'L1_ffn_A2',
        'L1_ffn_B2', 'L1_ffn_W3', 'L1_ffn_b3', 'L1_ffn_A3', 'L1_ffn_B3']


def kernel(**inputs):
    import numpy as _np
    import concourse.bacc as _bacc
    from concourse import mybir as _mybir
    from concourse.bass_utils import run_bass_kernel_spmd as _run

    nc = _bacc.Bacc("TRN2", target_bir_lowering=False, num_devices=1)
    arrays, args = {}, []
    for name in _INS:
        a = _np.ascontiguousarray(inputs[name])
        arrays[f"in_{name}_dram"] = a
        args.append(nc.dram_tensor(f"in_{name}_dram", a.shape, _mybir.dt.from_np(a.dtype), kind="ExternalInput").ap())
    shape = inputs['L0_attn_x'].shape
    args.append(nc.dram_tensor("out_0_dram", shape, _mybir.dt.float32, kind="ExternalOutput").ap())
    two_block_kernel(nc, *args)
    r = _run(nc, [arrays], core_ids=[0])
    return r.results[0]["out_0_dram"]
```

```python
from contextlib import ExitStack

import concourse.bass as bass
from concourse import mybir

ALU = mybir.AluOpType
ACT = mybir.ActivationFunctionType
AX = mybir.AxisListType
F32 = mybir.dt.float32
F32R = mybir.dt.float32r
BF16 = mybir.dt.bfloat16
I32 = mybir.dt.int32

P = 128
T = 512
J = T // P
LN_EPS = 1e-5
ALPHA_SCALE = 8.0
BETA_EPS = 1e-6
MASKED = -1e30


def raw(ap):
    return ap.bitcast(F32)


def two_block_kernel(nc, x_in, W_in, conv_w, conv_b, W_g, b_g, forget_base, W_out,
                     router_w, router_b, w1, b1, w2, b2,
                     Wk, Wv, Wq, Wp, bp,
                     Wg, W1, b1_1, A1, B1, W2, b2_1, A2, B2, W3, b3_1, A3, B3, out):
    N, _, D = x_in.shape
    HR = W_out.shape[1]
    C2 = HR // 2
    TAPS = conv_w.shape[2]
    E0, _, I0 = w1.shape
    E1, I1, _ = W1.shape
    R = A1.shape[1]
    NQ, _, DH = Wq.shape
    K0, K1 = 4, 2
    NB = N * J
    SCALE = float(D) ** -0.5
    assert D == P and I0 == 2 * P and I1 == 2 * P and T == x_in.shape[1]

    root = ExitStack()
    scope = [root]

    def sb(name, shape, dt=F32):
        return scope[-1].enter_context(nc.sbuf_tensor(name, shape, dt))

    def ps(name, shape, dt=F32):
        return scope[-1].enter_context(nc.psum_tensor(name, shape, dt))

    def sem(name):
        return root.enter_context(nc.semaphore(name))

    def tile_cols(n):
        return bass.ds(n * T, T)

    def wait_apart(eng, semaphore, value):
        eng.wait_ge(semaphore, 1)
        eng.wait_ge(semaphore, value)
        eng.wait_ge(semaphore, 1)

    def mm3(dst, w_hi, w_lo, m_hi, m_lo, start=True, stop=True):
        nc.tensor.matmul(dst, w_hi, m_hi, start=start, stop=False)
        nc.tensor.matmul(dst, w_hi, m_lo, start=False, stop=False)
        return nc.tensor.matmul(dst, w_lo, m_hi, start=False, stop=stop)

    with root:
        xres = sb("xres", [P, NB, D])
        x_hi = sb("x_hi", [P, N * T], F32R)
        x_lo = sb("x_lo", [P, N * T], F32R)
        yT = sb("yT", [P, N * T])
        gT = sb("gT", [P, N * T], F32R)
        ident = sb("ident", [P, P])
        sel = sb("sel", [P, E0, P], F32R)

        s_const0 = sem("const_zeroed")
        s_const = sem("const_made")
        s_xload = sem("x_loaded")
        scope.append(ExitStack())
        sel_f = sb("sel_f", [P, E0, P])
        with scope[-1], nc.Block() as block:
            @block.sync
            def _(sp):
                for n in range(N):
                    sp.dma_start(xres[:, n * J:(n + 1) * J, :],
                                 x_in[n].rearrange("(j p) d -> p j d", p=P)).then_inc(s_xload, 16)
                sp.wait_ge(s_xload, 16 * N)

            @block.gpsimd
            def _(pool):
                pool.memset(ident[:], 0.0).then_inc(s_const0, 1)
                pool.memset(sel_f[:], 0.0).then_inc(s_const0, 1)
                pool.wait_ge(s_const0, 2)
                pool.affine_select(out=ident[:], in_=ident[:], compare_op=ALU.not_equal, fill=1.0,
                                   base=0, pattern=[[-1, P]], channel_multiplier=1).then_inc(s_const, 1)
                for k, base in enumerate((0, -16)):
                    pool.wait_ge(s_const, k + 1)
                    pool.affine_select(out=sel_f[:], in_=sel_f[:], compare_op=ALU.not_equal,
                                       fill=1.0, base=base, pattern=[[-1, E0], [0, P]],
                                       channel_multiplier=1).then_inc(s_const, 1)
                pool.wait_ge(s_const, 3)
                pool.tensor_copy(sel[:], sel_f[:]).then_inc(s_const, 1)
        scope.pop()

        def norm_and_route(tag, E, K, router_load, router_transposed, bias_load):
            scope.append(ExitStack())
            with scope[-1]:
                stats = sb(tag + "stats", [P, NB, 6])
                mv = sb(tag + "mv", [P, NB, 2])
                rstd = sb(tag + "rstd", [P, NB])
                xn = sb(tag + "xn", [P, 2, J, D])
                rw = sb(tag + "rw", [P, 16])
                rw_raw = sb(tag + "rwraw", [16, P])
                rw_hi = sb(tag + "rw_hi", [P, 16], F32R)
                rw_lo = sb(tag + "rw_lo", [P, 16], F32R)
                rb = sb(tag + "rb", [P, 16])
                lg = sb(tag + "lg", [P, NB, 16])
                pr = sb(tag + "pr", [P, NB, 16])
                mx = sb(tag + "mx", [P, NB])
                sm = sb(tag + "sm", [P, NB])
                top = sb(tag + "top", [P, NB, 8])
                cut = sb(tag + "cut", [P, NB, 16])
                c_hi = sb(tag + "c_hi", [P, NB, 16], F32R)
                c2 = sb(tag + "c2", [P, NB, P])
                p_x = ps(tag + "p_x", [P, 2, T])
                p_lg = ps(tag + "p_lg", [P, NB, 16])
                p_g = ps(tag + "p_g", [P, 2, T])
                p_rw = ps(tag + "p_rw", [P, 16])
                s_rw = sem(tag + "router_loaded")
                s_rb = sem(tag + "router_bias_loaded")
                s_rwz = sem(tag + "router_zeroed")
                s_rwt = sem(tag + "router_transposed")
                s_rwf = sem(tag + "router_in_sbuf")
                s_rwh = sem(tag + "router_split")
                s_st = sem(tag + "stats_made")
                s_mv = sem(tag + "moments_made")
                s_var = sem(tag + "variance_eps")
                s_std = sem(tag + "std_made")
                s_rstd = sem(tag + "rstd_made")
                s_xn = sem(tag + "normalised")
                s_tr = sem(tag + "transposed")
                s_hi = sem(tag + "x_hi_ready")
                s_lo = sem(tag + "x_lo_ready")
                s_lg = sem(tag + "logits_ready")
                s_rt = sem(tag + "route_step")
                s_exp = sem(tag + "exp_ready")
                s_c2 = sem(tag + "gates_ready")
                s_gt = sem(tag + "gates_transposed")
                s_gc = sem(tag + "gates_stored")
                with nc.Block() as block:
                    @block.sync
                    def _(sp):
                        if router_transposed:
                            sp.dma_start(rw_raw[0:E, :], router_load).then_inc(s_rw, 16)
                        else:
                            sp.dma_start(rw[:, 0:E], router_load).then_inc(s_rw, 16)
                        sp.wait_ge(s_rw, 16)
                        if bias_load is not None:
                            sp.dma_start(rb[:, 0:E], bias_load).then_inc(s_rb, 16)
                            sp.wait_ge(s_rb, 16)

                    @block.vector
                    def _(dve):
                        for k in range(NB):
                            nc.vector.bn_stats(stats[:, k, :], xres[:, k, :]).then_inc(s_st, 1)
                        for k in range(NB):
                            dve.wait_ge(s_st, k + 1)
                            nc.vector.bn_aggr(mv[:, k, :], stats[:, k, :]).then_inc(s_mv, 1)
                        dve.wait_ge(s_mv, NB)
                        nc.vector.tensor_scalar(rstd[:], mv[:, :, 1], LN_EPS, None, ALU.add).then_inc(s_var, 1)
                        if router_transposed:
                            nc.vector.memset(rw[:], 0.0).then_inc(s_rwz, 1)
                            dve.wait_ge(s_rwt, 1)
                            dve.wait_ge(s_rwz, 1)
                            nc.vector.tensor_copy(rw[:, 0:E], p_rw[:, 0:E]).then_inc(s_rwf, 1)
                            dve.wait_ge(s_rwf, 1)
                        else:
                            dve.wait_ge(s_rw, 16)
                        nc.vector.tensor_copy(rw_hi[:, 0:E], rw[:, 0:E]).then_inc(s_rwh, 1)
                        dve.wait_ge(s_rwh, 1)
                        nc.vector.tensor_tensor(rw_lo[:, 0:E], rw[:, 0:E], raw(rw_hi[:, 0:E]),
                                                ALU.subtract).then_inc(s_rwh, 1)
                        dve.wait_ge(s_std, 1)
                        nc.vector.reciprocal(rstd[:], rstd[:]).then_inc(s_rstd, 1)
                        dve.wait_ge(s_rstd, 1)
                        for n in range(N):
                            if n >= 2:
                                dve.wait_ge(s_tr, n - 1)
                            for j in range(J):
                                k = n * J + j
                                nc.vector.tensor_scalar(xn[:, n % 2, j, :], xres[:, k, :], mv[:, k, 0:1],
                                                        rstd[:, k:k + 1], ALU.subtract,
                                                        ALU.mult).then_inc(s_xn, 1)
                            if n >= 1:
                                dve.wait_ge(s_hi, n)
                                nc.vector.tensor_tensor(x_lo[:, (n - 1) * T:n * T], p_x[:, (n - 1) % 2, :],
                                                        raw(x_hi[:, (n - 1) * T:n * T]),
                                                        ALU.subtract).then_inc(s_lo, 1)
                        dve.wait_ge(s_hi, N)
                        nc.vector.tensor_tensor(x_lo[:, (N - 1) * T:N * T], p_x[:, (N - 1) % 2, :],
                                                raw(x_hi[:, (N - 1) * T:N * T]), ALU.subtract).then_inc(s_lo, 1)
                        step = [0]

                        def chain(ins):
                            step[0] += 1
                            ins.then_inc(s_rt, 1)
                            dve.wait_ge(s_rt, step[0])

                        def over_experts(ap):
                            return ap.unsqueeze(2).broadcast_to([P, NB, E])

                        dve.wait_ge(s_lg, 1)
                        if bias_load is not None:
                            dve.wait_ge(s_rb, 16)
                            chain(nc.vector.tensor_tensor(lg[:, :, 0:E], p_lg[:, :, 0:E],
                                                          rb[:, 0:E].unsqueeze(1).broadcast_to([P, NB, E]), ALU.add))
                        else:
                            chain(nc.vector.tensor_copy(lg[:, :, 0:E], p_lg[:, :, 0:E]))
                        chain(nc.vector.tensor_reduce(out=mx[:], in_=lg[:, :, 0:E], op=ALU.max, axis=AX.X))
                        chain(nc.vector.tensor_tensor(lg[:, :, 0:E], lg[:, :, 0:E], over_experts(mx[:]), ALU.subtract))
                        dve.wait_ge(s_exp, 1)
                        chain(nc.vector.tensor_reduce(out=sm[:], in_=pr[:, :, 0:E], op=ALU.add, axis=AX.X))
                        chain(nc.vector.reciprocal(sm[:], sm[:]))
                        chain(nc.vector.tensor_tensor(pr[:, :, 0:E], pr[:, :, 0:E], over_experts(sm[:]), ALU.mult))
                        for k in range(NB):
                            last = nc.vector.max(top[:, k, :], pr[:, k, 0:E])
                            last.then_inc(s_rt, 1)
                        step[0] += NB
                        dve.wait_ge(s_rt, step[0])
                        chain(nc.vector.memset(top[:, :, K:8], -1.0))
                        for k in range(NB):
                            nc.vector.match_replace(out=cut[:, k, 0:E], in_to_replace=top[:, k, :],
                                                    in_values=pr[:, k, 0:E], imm_value=-2.0).then_inc(s_rt, 1)
                        step[0] += NB
                        dve.wait_ge(s_rt, step[0])
                        chain(nc.vector.tensor_scalar(cut[:, :, 0:E], cut[:, :, 0:E], -2.0, None, ALU.is_equal))
                        chain(nc.vector.tensor_tensor(pr[:, :, 0:E], pr[:, :, 0:E], cut[:, :, 0:E], ALU.mult))
                        chain(nc.vector.tensor_reduce(out=sm[:], in_=pr[:, :, 0:E], op=ALU.add, axis=AX.X))
                        chain(nc.vector.reciprocal(sm[:], sm[:]))
                        chain(nc.vector.tensor_tensor(pr[:, :, 0:E], pr[:, :, 0:E], over_experts(sm[:]), ALU.mult))
                        chain(nc.vector.memset(c2[:], 0.0))
                        chain(nc.vector.tensor_copy(c_hi[:, :, 0:E], pr[:, :, 0:E]))
                        chain(nc.vector.tensor_copy(c2[:, :, 0:E], raw(c_hi[:, :, 0:E])))
                        nc.vector.tensor_tensor(c2[:, :, 16:16 + E], pr[:, :, 0:E], raw(c_hi[:, :, 0:E]),
                                                ALU.subtract).then_inc(s_c2, 1)

                    @block.scalar
                    def _(act):
                        act.wait_ge(s_var, 1)
                        nc.scalar.activation(rstd[:], rstd[:], ACT.Sqrt).then_inc(s_std, 1)
                        for n in range(N):
                            act.wait_ge(s_tr, n + 1)
                            nc.scalar.activation(x_hi[:, n * T:(n + 1) * T], p_x[:, n % 2, :],
                                                 ACT.Copy).then_inc(s_hi, 1)
                        act.wait_ge(s_rt, 3)
                        nc.scalar.activation(pr[:, :, 0:E], lg[:, :, 0:E], ACT.Exp).then_inc(s_exp, 1)
                        for n in range(N):
                            act.wait_ge(s_gt, n + 1)
                            nc.scalar.activation(gT[:, n * T:(n + 1) * T], p_g[:, n % 2, :],
                                                 ACT.Copy).then_inc(s_gc, 1)

                    @block.tensor
                    def _(pe):
                        if router_transposed:
                            pe.wait_ge(s_rw, 16)
                            nc.tensor.transpose(p_rw[:, 0:E], rw_raw[0:E, :], ident[0:E, 0:E]).then_inc(s_rwt, 1)
                        for n in range(N):
                            pe.wait_ge(s_xn, (n + 1) * J)
                            if n >= 2:
                                pe.wait_ge(s_lo, n - 1)
                            for j in range(J):
                                last = nc.tensor.transpose(p_x[:, n % 2, j * P:(j + 1) * P],
                                                           xn[:, n % 2, j, :], ident[:])
                            last.then_inc(s_tr, 1)
                        pe.wait_ge(s_rwh, 2)
                        for k in range(NB):
                            if k % J == 0:
                                pe.wait_ge(s_lo, k // J + 1)
                            last = mm3(p_lg[:, k, 0:E], x_hi[:, k * P:(k + 1) * P], x_lo[:, k * P:(k + 1) * P],
                                       rw_hi[:, 0:E], rw_lo[:, 0:E])
                        last.then_inc(s_lg, 1)
                        pe.wait_ge(s_c2, 1)
                        for n in range(N):
                            if n >= 2:
                                pe.wait_ge(s_gc, n - 1)
                            for j in range(J):
                                last = nc.tensor.transpose(p_g[:, n % 2, j * P:(j + 1) * P],
                                                           c2[:, n * J + j, :], ident[:])
                            last.then_inc(s_gt, 1)
            scope.pop()

        norm_and_route("a_", E0, K0, router_w, False,
                       router_b.rearrange("(a e) -> a e", a=1).broadcast_to([P, E0]))

        scope.append(ExitStack())
        with scope[-1]:
            win_raw = sb("win_raw", [C2, 4, D])
            wg_raw = sb("wg_raw", [C2, 4, HR])
            wout_raw = sb("wout_raw", [D, HR])
            win_hi = sb("win_hi", [D, 4, C2], F32R)
            win_lo = sb("win_lo", [D, 4, C2], F32R)
            wg_hi = sb("wg_hi", [C2, 8, C2], F32R)
            wg_lo = sb("wg_lo", [C2, 8, C2], F32R)
            wo = sb("wo", [C2, 2, D])
            cw = sb("cw", [C2, 2, TAPS])
            cb = sb("cb", [C2, 2])
            bg = sb("bg", [C2, 4])
            fb = sb("fb", [C2, 2])
            kf = sb("kf", [C2, 2])
            spt = sb("spt", [C2, 2])
            one_eps = sb("one_eps", [C2, 1])
            xp = sb("xp", [C2, 4, 4 + T])
            cv = sb("cv", [C2, 2, T])
            xb = sb("xb", [C2, 4, T])
            xb_hi = sb("xb_hi", [C2, 2, T], F32R)
            xb_lo = sb("xb_lo", [C2, 2, T], F32R)
            tf = sb("tf", [C2, 2, T])
            ti = sb("ti", [C2, 4, T])
            al = sb("al", [C2, 4, T])
            sq = sb("sq", [C2, 2, T])
            be = sb("be", [C2, 2, T])
            gl = sb("gl", [C2, 4, T])
            xs = sb("xs", [C2, 2, T])
            hs = sb("hs", [C2, 2, T])
            z = sb("z", [C2, 2, T])
            p_gate = ps("p_gate", [P, 2, T])
            p_xb = ps("p_xb", [P, 2, T])
            p_f = ps("p_f", [P, 3, T])
            p_y = ps("p_y", [P, T])

            s_ld = sem("r_weights_loaded")
            s_wt = sem("r_weights_transposed")
            s_wh = sem("r_weights_high")
            s_wl = sem("r_weights_low")
            s_small = sem("r_small_step")
            s_sp = sem("r_softplus_step")
            pad = TAPS - 1
            with nc.Block() as block:
                @block.sync
                def _(sp):
                    sp.dma_start(win_raw[:], W_in.rearrange("(c p) d -> p c d", p=C2)).then_inc(s_ld, 16)
                    sp.dma_start(wg_raw[:], W_g.rearrange("(c p) h -> p c h", p=C2)).then_inc(s_ld, 16)
                    sp.dma_start(wout_raw[:], W_out).then_inc(s_ld, 16)
                    sp.dma_start(cw[:], conv_w.rearrange("(c p) a k -> p c (a k)", p=C2)).then_inc(s_ld, 16)
                    with nc.allow_non_contiguous_dma(reason="a few hundred bias values"):
                        sp.dma_start(cb[:], conv_b.rearrange("(c p) -> p c", p=C2)).then_inc(s_ld, 16)
                        sp.dma_start(bg[:], b_g.rearrange("(c p) -> p c", p=C2)).then_inc(s_ld, 16)
                        sp.dma_start(fb[:], forget_base.rearrange("(c p) -> p c", p=C2)).then_inc(s_ld, 16)
                    sp.wait_ge(s_ld, 7 * 16)

                @block.tensor
                def _(pe):
                    pe.wait_ge(s_ld, 7 * 16)
                    for c in range(4):
                        last = nc.tensor.transpose(p_gate[:, 0, c * C2:(c + 1) * C2], win_raw[:, c, :],
                                                   ident[0:C2, 0:C2])
                    last.then_inc(s_wt, 1)
                    for hc in range(2):
                        for gc in range(4):
                            last = nc.tensor.transpose(p_f[0:C2, hc, gc * C2:(gc + 1) * C2],
                                                       wg_raw[:, gc, hc * C2:(hc + 1) * C2], ident[0:C2, 0:C2])
                    last.then_inc(s_wt, 1)
                    for hc in range(2):
                        last = nc.tensor.transpose(p_y[0:C2, hc * P:(hc + 1) * P],
                                                   wout_raw[:, hc * C2:(hc + 1) * C2], ident[:])
                    last.then_inc(s_wt, 1)

                splits = [
                    (lambda: win_hi[:].rearrange("p a b -> p (a b)"), lambda: win_lo[:].rearrange("p a b -> p (a b)"),
                     lambda: p_gate[:, 0, 0:4 * C2], 1),
                    (lambda: wg_hi[:, 0:4, :].rearrange("p a b -> p (a b)"), lambda: wg_lo[:, 0:4, :].rearrange("p a b -> p (a b)"),
                     lambda: p_f[0:C2, 0, 0:4 * C2], 2),
                    (lambda: wg_hi[:, 4:8, :].rearrange("p a b -> p (a b)"), lambda: wg_lo[:, 4:8, :].rearrange("p a b -> p (a b)"),
                     lambda: p_f[0:C2, 1, 0:4 * C2], 2),
                ]

                @block.scalar
                def _(act):
                    for hi, lo, src, need in splits:
                        act.wait_ge(s_wt, need)
                        nc.scalar.activation(hi(), src(), ACT.Copy).then_inc(s_wh, 1)
                    act.wait_ge(s_ld, 7 * 16)
                    nc.scalar.activation(spt[:], fb[:], ACT.Abs).then_inc(s_sp, 1)
                    act.wait_ge(s_sp, 1)
                    nc.scalar.activation(spt[:], spt[:], ACT.Exp, scale=-1.0).then_inc(s_sp, 1)
                    act.wait_ge(s_sp, 2)
                    nc.scalar.activation(spt[:], spt[:], ACT.Ln, bias=1.0).then_inc(s_sp, 1)

                @block.vector
                def _(dve):
                    for k, (hi, lo, src, need) in enumerate(splits):
                        dve.wait_ge(s_wh, k + 1)
                        nc.vector.tensor_tensor(lo(), src(), raw(hi()), ALU.subtract).then_inc(s_wl, 1)
                    dve.wait_ge(s_ld, 7 * 16)
                    nc.vector.memset(xp[:], 0.0)
                    nc.vector.memset(one_eps[:], (1.0 + BETA_EPS) / 4)
                    dve.wait_ge(s_wt, 3)
                    nc.vector.tensor_copy(wo[:].rearrange("p a b -> p (a b)"), p_y[0:C2, 0:2 * P])
                    nc.vector.tensor_scalar(bg[:], bg[:], 0.5, None, ALU.mult)
                    nc.vector.tensor_scalar(kf[:], fb[:], 0.0, None, ALU.max).then_inc(s_small, 1)
                    dve.wait_ge(s_sp, 3)
                    dve.wait_ge(s_small, 1)
                    nc.vector.tensor_tensor(kf[:], kf[:], spt[:], ALU.add).then_inc(s_small, 1)
                    dve.wait_ge(s_small, 2)
                    nc.vector.tensor_scalar(kf[:], kf[:], -ALPHA_SCALE / 2, None, ALU.mult).then_inc(s_small, 1)

            s_a = sem("r_input_projected")
            s_g = sem("r_gate_projected")
            s_xp = sem("r_conv_input")
            s_xb = sem("r_conv_step")
            s_xh = sem("r_conv_high")
            s_xl = sem("r_conv_low")
            s_fi = sem("r_gates_projected")
            s_tf = sem("r_forget_tanh")
            s_ti = sem("r_input_tanh")
            s_al = sem("r_alpha")
            s_a2 = sem("r_alpha_squared")
            s_be = sem("r_beta")
            s_gl = sem("r_gelu")
            s_u = sem("r_scan_input_step")
            s_h = sem("r_scanned")
            s_z = sem("r_gated")
            s_y = sem("r_output")
            s_yc = sem("r_output_stored")

            def both(buf, n):
                return buf[:, bass.ds((n % 2) * 2, 2), :]

            def chunk(buf, n, c):
                return buf[:, bass.ds((n % 2) * 2 + c, 1), :]

            with nc.Block() as block:
                @block.tensor
                def _(pe):
                    def project_input(n):
                        for c in range(2):
                            last = mm3(p_xb[0:C2, c, :], win_hi[:, 2 + c, :], win_lo[:, 2 + c, :],
                                       x_hi[:, tile_cols(n)], x_lo[:, tile_cols(n)])
                        last.then_inc(s_a, 1)

                    def project_gate(n):
                        for c in range(2):
                            last = mm3(p_gate[0:C2, c, :], win_hi[:, c, :], win_lo[:, c, :],
                                       x_hi[:, tile_cols(n)], x_lo[:, tile_cols(n)])
                        last.then_inc(s_g, 1)

                    def gates(n):
                        pe.wait_ge(s_xl, n + 1)
                        pe.wait_ge(s_ti, 2 * n + 1)
                        for gc in range(4):
                            if gc == 3:
                                pe.wait_ge(s_tf, 2 * n + 1)
                            for hc in range(2):
                                last = mm3(p_f[0:C2, gc % 3, :], wg_hi[:, 4 * hc + gc, :], wg_lo[:, 4 * hc + gc, :],
                                           xb_hi[:, hc, :], xb_lo[:, hc, :], start=hc == 0, stop=hc == 1)
                            last.then_inc(s_fi, 1)

                    def output(n):
                        pe.wait_ge(s_yc, n + 1)
                        pe.wait_ge(s_z, n + 1)
                        for hc in range(2):
                            last = nc.tensor.matmul(p_y[:], wo[:, hc, :], z[:, hc, :],
                                                    start=hc == 0, stop=hc == 1)
                        last.then_inc(s_y, 1)

                    def turn(n, before=True, after=2):
                        gates(n)
                        if before:
                            output(n - 1)
                        if after == 2:
                            pe.wait_ge(s_xp, n + 2)
                            project_input(n + 2)
                        if after >= 1:
                            pe.wait_ge(s_gl, n + 1)
                            project_gate(n + 1)

                    pe.sem_inc(s_y, 1)
                    project_input(0)
                    project_gate(0)
                    pe.wait_ge(s_xp, 1)
                    project_input(1)
                    turn(0, before=False)
                    with pe.Fori(1, N - 2) as n:
                        turn(n)
                    turn(N - 2, after=1)
                    turn(N - 1, after=0)
                    output(N - 1)

                @block.scalar
                def _(act):
                    act.sem_inc(s_yc, 1)
                    act.sem_inc(s_ti, 1)

                    def conv_input(n):
                        wait_apart(act, s_a, n + 1)
                        nc.scalar.activation(xp[:, bass.ds((n % 2) * 2, 2), pad:pad + T], p_xb[0:C2, :, :],
                                             ACT.Copy).then_inc(s_xp, 1)

                    def gelu(n):
                        wait_apart(act, s_g, n + 1)
                        nc.scalar.activation(both(gl, n), p_gate[0:C2, :, :], ACT.Gelu).then_inc(s_gl, 1)

                    def gates(n):
                        for c in range(2):
                            act.wait_ge(s_fi, n * 4 + c + 1)
                            nc.scalar.activation(tf[:, c, :], p_f[0:C2, c, :], ACT.Tanh, bias=bg[:, c:c + 1],
                                                 scale=0.5).then_inc(s_tf, 1)
                        for c in range(2):
                            wait_apart(act, s_fi, n * 4 + c + 3)
                            b = (2 + c) % 3
                            nc.scalar.activation(chunk(ti, n, c), p_f[0:C2, b:b + 1, :], ACT.Tanh,
                                                 bias=bg[:, 2 + c:3 + c], scale=0.5).then_inc(s_ti, 1)
                        for c in range(2):
                            wait_apart(act, s_tf, 2 * n + c + 1)
                            nc.scalar.activation(chunk(al, n, c), tf[:, c:c + 1, :], ACT.Exp, bias=kf[:, c:c + 1],
                                                 scale=kf[:, c:c + 1]).then_inc(s_al, 1)
                        wait_apart(act, s_al, 2 * n + 2)
                        nc.scalar.activation(sq[:], both(al, n), ACT.Square).then_inc(s_a2, 1)
                        act.wait_ge(s_u, 2 * n + 1)
                        act.wait_ge(s_a2, n + 1)
                        nc.scalar.activation(be[:], sq[:], ACT.Sqrt, bias=one_eps[:, 0:1],
                                             scale=-0.25).then_inc(s_be, 1)

                    def store(n):
                        wait_apart(act, s_y, n + 2)
                        nc.scalar.activation(yT[:, tile_cols(n)], p_y[:], ACT.Copy).then_inc(s_yc, 1)

                    def turn(n, before=True, after=2):
                        gates(n)
                        if before:
                            store(n - 1)
                        if after == 2:
                            conv_input(n + 2)
                        if after >= 1:
                            gelu(n + 1)

                    conv_input(0)
                    gelu(0)
                    conv_input(1)
                    turn(0, before=False)
                    with act.Fori(1, N - 2) as n:
                        turn(n)
                    turn(N - 2, after=1)
                    turn(N - 1, after=0)
                    store(N - 1)

                @block.vector
                def _(dve):
                    def convolve(n):
                        dve.wait_ge(s_xp, n + 1)
                        for k in range(TAPS):
                            for c in range(2):
                                tap = xp[:, bass.ds((n % 2) * 2 + c, 1), pad - k:pad - k + T]
                                w = cw[:, c, TAPS - 1 - k:TAPS - k]
                                steps = [cv[:, c:c + 1, :], chunk(xb, n, c)]
                                if k == 0:
                                    nc.vector.tensor_scalar(steps[0], tap, w, cb[:, c:c + 1], ALU.mult,
                                                            ALU.add).then_inc(s_xb, 1)
                                else:
                                    dve.wait_ge(s_xb, n * (2 * TAPS) + 2 * (k - 1) + c + 1)
                                    nc.vector.scalar_tensor_tensor(out=steps[k % 2], in0=tap, scalar=w,
                                                                   in1=steps[1 - k % 2], op0=ALU.mult,
                                                                   op1=ALU.add).then_inc(s_xb, 1)
                        dve.wait_ge(s_xb, n * (2 * TAPS) + 2 * TAPS)

                    def split(n):
                        nc.vector.tensor_scalar(xb_hi[:], both(xb, n), 1.0, None, ALU.mult).then_inc(s_xh, 1)
                        dve.wait_ge(s_xh, n + 1)
                        nc.vector.tensor_tensor(xb_lo[:], both(xb, n), raw(xb_hi[:]), ALU.subtract).then_inc(s_xl, 1)

                    def scan(n):
                        dve.wait_ge(s_ti, 2 * n + 3)
                        nc.vector.scalar_tensor_tensor(out=xs[:], in0=both(ti, n), scalar=1.0, in1=both(xb, n),
                                                       op0=ALU.add, op1=ALU.mult).then_inc(s_u, 1)
                        dve.wait_ge(s_u, 2 * n + 2)
                        dve.wait_ge(s_be, n + 1)
                        nc.vector.tensor_tensor(xs[:], xs[:], be[:], ALU.mult).then_inc(s_u, 1)
                        dve.wait_ge(s_u, 2 * n + 3)
                        for c in range(2):
                            nc.vector.tensor_tensor_scan(hs[:, c, :], al[:, bass.ds((n % 2) * 2 + c, 1), :].rearrange(
                                "p a t -> p (a t)"), xs[:, c, :], 0.0, ALU.mult, ALU.add).then_inc(s_h, 1)
                        dve.wait_ge(s_h, 2 * n + 2)
                        dve.wait_ge(s_gl, n + 1)
                        dve.wait_ge(s_y, n + 1)
                        nc.vector.tensor_tensor(z[:], both(gl, n), hs[:], ALU.mult).then_inc(s_z, 1)

                    dve.sem_inc(s_u, 1)
                    convolve(0)
                    split(0)
                    with dve.Fori(0, N - 1) as n:
                        convolve(n + 1)
                        dve.wait_ge(s_fi, n * 4 + 4)
                        split(n + 1)
                        scan(n)
                    scan(N - 1)
        scope.pop()

        def split_weights(tag, parts):
            s_h = sem(tag + "weights_high")
            s_l = sem(tag + "weights_low")
            return s_h, s_l

        def experts(tag, E, up_hi, up_lo, bias_up, lin_hi, lin_lo, bias_lin, dn_hi, dn_lo, b2_hi, b2_lo, act_fn,
                    store):
            gated = lin_hi is not None
            LAG = 3
            BUFS = 4
            scope.append(ExitStack())
            with scope[-1]:
                h = sb(tag + "h", [P, 2, 2, T])
                g = sb(tag + "g", [P, 2, 2, T])
                g_hi = sb(tag + "g_hi", [P, BUFS, 2, T], F32R)
                g_lo = sb(tag + "g_lo", [P, BUFS, 2, T], F32R)
                ys = sb(tag + "ys", [P, T])
                p_up = ps(tag + "p_up", [P, 2, 2, T]) if not gated else ps(tag + "p_up", [P, 1, 2, T])
                p_lin = ps(tag + "p_lin", [P, 1, 2, T]) if gated else None
                p_gate = ps(tag + "p_gate", [P, 2, T])
                p_acc = ps(tag + "p_acc", [P, T])
                p_tr = ps(tag + "p_tr", [P, T])
                B = 1 if gated else 2
                s_up = sem(tag + "up_done")
                s_h = sem(tag + "activated")
                s_lin = sem(tag + "linear_gated")
                s_g = sem(tag + "gated")
                s_hi = sem(tag + "gated_high")
                s_lo = sem(tag + "gated_low")
                s_dn = sem(tag + "down_done")
                s_ys = sem(tag + "tile_sum")
                s_tr = sem(tag + "tile_transposed")
                s_xr = sem(tag + "residual_added")
                s_out = sem(tag + "stored")

                def blocks(run):
                    run(0, first=True, last=False)
                    yield 1, N - 1
                    run(N - 1, first=False, last=True)

                with nc.Block() as block:
                    @block.tensor
                    def _(pe):
                        pe.sem_inc(s_dn, BUFS)

                        def up(n, e):
                            q = n * E + e
                            x_h, x_l = x_hi[:, tile_cols(n)], x_lo[:, tile_cols(n)]
                            pe.wait_ge(s_g, q + 1)
                            nc.tensor.matmul(p_gate[:, e % 2, :], sel[:, e, :], gT[:, tile_cols(n)],
                                             start=True, stop=True)
                            pe.wait_ge(s_h, q + 1)
                            for c in range(2):
                                last = mm3(p_up[:, e % B, c, :], up_hi[:, e, c, :], up_lo[:, e, c, :], x_h, x_l)
                            last.then_inc(s_up, 1)
                            if gated:
                                pe.wait_ge(s_g, q + 2)
                                for c in range(2):
                                    last = mm3(p_lin[:, 0, c, :], lin_hi[:, e, c, :], lin_lo[:, e, c, :], x_h, x_l)
                                last.then_inc(s_lin, 1)

                        def down(n, e):
                            pe.wait_ge(s_lo, n * E + e + 3)
                            if e == 0:
                                pe.wait_ge(s_ys, n + 1)
                                for k, b in enumerate((b2_hi, b2_lo)):
                                    nc.tensor.matmul(p_acc[:], b[:], gT[:, tile_cols(n)],
                                                     start=k == 0, stop=False)
                            for c in range(2):
                                last = mm3(p_acc[:], dn_hi[:, e, c, :], dn_lo[:, e, c, :], g_hi[:, e % BUFS, c, :],
                                           g_lo[:, e % BUFS, c, :], start=False, stop=(e == E - 1 and c == 1))
                            last.then_inc(s_dn, 1)

                        def turn_back(n):
                            pe.wait_ge(s_ys, n + 2)
                            pe.wait_ge(s_xr, n + 1)
                            for j in range(J):
                                last = nc.tensor.transpose(p_tr[:, j * P:(j + 1) * P], ys[:, j * P:(j + 1) * P],
                                                           ident[:])
                            last.then_inc(s_tr, 1)

                        def tile(n, first, last):
                            if first:
                                for e in range(LAG):
                                    up(n, e)
                            for k in range(LAG, E + LAG):
                                if k < E:
                                    up(n, k)
                                elif not last:
                                    up(n + 1, k - E)
                                if k == 6 and not first:
                                    turn_back(n - 1)
                                down(n, k - LAG)
                            if last:
                                turn_back(n)

                        tile(0, True, False)
                        with pe.Fori(1, N - 1) as n:
                            tile(n, False, False)
                        tile(N - 1, False, True)

                    @block.scalar
                    def _(act):
                        act.sem_inc(s_h, B)

                        def activate(n, e):
                            q = n * E + e
                            act.wait_ge(s_up, q + 1)
                            act.wait_ge(s_g, q + 1)
                            for c in range(2):
                                last = nc.scalar.activation(h[:, e % 2, c, :], p_up[:, e % B, c, :], act_fn,
                                                            bias=bias_up[:, e, c:c + 1])
                            last.then_inc(s_h, 1)

                        def high(n, e):
                            q = n * E + e
                            act.wait_ge(s_g, q + 3)
                            act.wait_ge(s_dn, q + 1)
                            nc.scalar.activation(g_hi[:, e % BUFS, :, :], g[:, e % 2, :, :], ACT.Copy).then_inc(s_hi, 1)

                        def tile(n, first, last):
                            if first:
                                activate(n, 0)
                            for k in range(1, E + 1):
                                if k < E:
                                    activate(n, k)
                                elif not last:
                                    activate(n + 1, 0)
                                high(n, k - 1)

                        tile(0, True, False)
                        with act.Fori(1, N - 1) as n:
                            tile(n, False, False)
                        tile(N - 1, False, True)

                    @block.vector
                    def _(dve):
                        dve.sem_inc(s_g, 2)
                        dve.sem_inc(s_lo, 2)
                        dve.sem_inc(s_ys, 1)
                        dve.sem_inc(s_xr, 1)

                        def gate(n, e):
                            q = n * E + e
                            dve.wait_ge(s_h, q + B + 1)
                            dve.wait_ge(s_lo, q + 1)
                            if not gated:
                                nc.vector.tensor_tensor(g[:, e % 2, :, :], h[:, e % 2, :, :],
                                                        p_gate[:, e % 2, :].unsqueeze(1).broadcast_to([P, 2, T]),
                                                        ALU.mult).then_inc(s_g, 1)
                            else:
                                nc.vector.tensor_tensor(h[:, e % 2, :, :], h[:, e % 2, :, :],
                                                        p_gate[:, e % 2, :].unsqueeze(1).broadcast_to([P, 2, T]),
                                                        ALU.mult).then_inc(s_hg, 1)
                                dve.wait_ge(s_hg, q + 1)
                                dve.wait_ge(s_lin, q + 1)
                                for c in range(2):
                                    last = nc.vector.scalar_tensor_tensor(
                                        out=g[:, e % 2, c, :], in0=p_lin[:, 0, c, :], scalar=bias_lin[:, e, c:c + 1],
                                        in1=h[:, e % 2, c, :], op0=ALU.add, op1=ALU.mult)
                                last.then_inc(s_g, 1)

                        def low(n, e):
                            q = n * E + e
                            dve.wait_ge(s_hi, q + 1)
                            dve.wait_ge(s_dn, q + 1)
                            nc.vector.tensor_tensor(g_lo[:, e % BUFS, :, :], g[:, e % 2, :, :],
                                                    raw(g_hi[:, e % BUFS, :, :]),
                                                    ALU.subtract).then_inc(s_lo, 1)

                        def tile_sum(n):
                            dve.wait_ge(s_dn, n * E + E + BUFS)
                            dve.wait_ge(s_xr, n + 1)
                            nc.vector.tensor_tensor(ys[:], p_acc[:], yT[:, tile_cols(n)], ALU.add).then_inc(s_ys, 1)

                        def residual(n):
                            dve.wait_ge(s_tr, n + 1)
                            rows = xres[:, bass.ds(n * J, J), :]
                            nc.vector.tensor_tensor(rows, p_tr[:].rearrange("p (j d) -> p j d", j=J), rows,
                                                    ALU.add).then_inc(s_xr, 1)

                        def tile(n, first, last):
                            if first:
                                gate(n, 0)
                            for k in range(1, E + 1):
                                if k < E:
                                    gate(n, k)
                                elif not last:
                                    gate(n + 1, 0)
                                low(n, k - 1)
                                if not first and k == 2:
                                    tile_sum(n - 1)
                                if not first and k == 6:
                                    residual(n - 1)
                            if last:
                                tile_sum(n)
                                residual(n)

                        s_hg = s_halfgated
                        tile(0, True, False)
                        with dve.Fori(1, N - 1) as n:
                            tile(n, False, False)
                        tile(N - 1, False, True)

                    if store:
                        @block.sync
                        def _(sp):
                            with sp.Fori(0, N) as n:
                                sp.wait_ge(s_xr, n + 2)
                                sp.dma_start(out[bass.ds(n, 1)].rearrange("a (j p) d -> p (a j) d", p=P),
                                             xres[:, bass.ds(n * J, J), :]).then_inc(s_out, 16)
                            sp.wait_ge(s_out, 16 * N)
            scope.pop()

        s_halfgated = sem("half_gated")

        def split_parts(parts, s_hi, s_lo, block, before=0, s_before=None):
            @block.scalar
            def _(act):
                if s_before is not None:
                    act.wait_ge(s_before, before)
                for hi, lo, src in parts:
                    nc.scalar.activation(hi, src, ACT.Copy).then_inc(s_hi, 1)

            @block.vector
            def _(dve):
                for k, (hi, lo, src) in enumerate(parts):
                    dve.wait_ge(s_hi, k + 1)
                    nc.vector.tensor_tensor(lo, src, raw(hi), ALU.subtract).then_inc(s_lo, 1)

        scope.append(ExitStack())
        with scope[-1]:
            w1_hi = sb("w1_hi", [P, E0, 2, P], F32R)
            w1_lo = sb("w1_lo", [P, E0, 2, P], F32R)
            w2_hi = sb("w2_hi", [P, E0, 2, P], F32R)
            w2_lo = sb("w2_lo", [P, E0, 2, P], F32R)
            b1T = sb("b1T", [P, E0, 2])
            b2_hi = sb("b2_hi", [P, D], F32R)
            b2_lo = sb("b2_lo", [P, D], F32R)
            scope.append(ExitStack())
            with scope[-1]:
                w_raw = sb("w_raw", [P, E0, 2, P])
                w2_raw = sb("w2_raw", [P, E0, 2, P])
                b1_raw = sb("b1_raw", [2 * E0, P])
                b2_raw = sb("b2_raw", [P, D])
                p_b1 = ps("p_b1", [P, 2 * E0])
                s_ew = sem("e0_loaded")
                s_b2z = sem("e0_bias_zeroed")
                s_ewh = sem("e0_high")
                s_ewl = sem("e0_low")
                s_b1t = sem("e0_bias_transposed")
                with nc.Block() as block:
                    @block.sync
                    def _(sp):
                        sp.dma_start(w_raw[:].rearrange("p e c m -> p e (c m)"),
                                     w1.rearrange("e h i -> h e i")).then_inc(s_ew, 16)
                        sp.dma_start(w2_raw[:], w2.rearrange("e (c p) d -> p e c d", p=P)).then_inc(s_ew, 16)
                        sp.dma_start(b1_raw[:], b1.rearrange("e (c p) -> (e c) p", p=P)).then_inc(s_ew, 16)
                        sp.wait_ge(s_b2z, 1)
                        for k in range(2):
                            sp.dma_start(b2_raw[16 * k:16 * k + E0, :], b2).then_inc(s_ew, 16)
                        sp.wait_ge(s_ew, 5 * 16)

                    @block.tensor
                    def _(pe):
                        pe.wait_ge(s_ew, 5 * 16)
                        nc.tensor.transpose(p_b1[:], b1_raw[:], ident[0:2 * E0, 0:2 * E0]).then_inc(s_b1t, 1)

                    parts = [(w1_hi[:], w1_lo[:], w_raw[:]), (w2_hi[:], w2_lo[:], w2_raw[:]),
                             (b2_hi[:], b2_lo[:], b2_raw[:])]

                    @block.scalar
                    def _(act):
                        act.wait_ge(s_ew, 5 * 16)
                        for hi, lo, src in parts:
                            nc.scalar.activation(hi, src, ACT.Copy).then_inc(s_ewh, 1)

                    @block.vector
                    def _(dve):
                        nc.vector.memset(b2_raw[:], 0.0).then_inc(s_b2z, 1)
                        for k, (hi, lo, src) in enumerate(parts):
                            dve.wait_ge(s_ewh, k + 1)
                            nc.vector.tensor_tensor(lo, src, raw(hi), ALU.subtract).then_inc(s_ewl, 1)
                        dve.wait_ge(s_b1t, 1)
                        nc.vector.tensor_copy(b1T[:].rearrange("p e c -> p (e c)"), p_b1[:]).then_inc(s_ewl, 1)
            scope.pop()
            experts("e0_", E0, w1_hi, w1_lo, b1T, None, None, None, w2_hi, w2_lo, b2_hi, b2_lo, ACT.Gelu, False)
        scope.pop()

        norm_and_route("b_", E1, K1, Wg, True, None)

        scope.append(ExitStack())
        with scope[-1]:
            wq_raw = sb("wq_raw", [D, NQ, DH])
            wk_raw = sb("wk_raw", [D, DH])
            wv_raw = sb("wv_raw", [D, DH])
            wp_raw = sb("wp_raw", [NQ * DH, D])
            bp_col = sb("bp_col", [D, 1])
            wq_rep = sb("wq_rep", [D, NQ // 2, 2, 4, DH])
            wk_rep = sb("wk_rep", [D, 8, DH])
            wv_rep = sb("wv_rep", [D, 8, DH])
            wq_hi = sb("wq_hi", [D, NQ // 2, P], F32R)
            wq_lo = sb("wq_lo", [D, NQ // 2, P], F32R)
            wk_hi = sb("wk_hi", [D, P], F32R)
            wk_lo = sb("wk_lo", [D, P], F32R)
            wv_hi = sb("wv_hi", [D, P], F32R)
            wv_lo = sb("wv_lo", [D, P], F32R)
            wp_hi = sb("wp_hi", [D, P], F32R)
            wp_lo = sb("wp_lo", [D, P], F32R)
            part = sb("part", [P, 1], I32)
            bit = sb("bit", [P, 2], I32)
            q_m = sb("q_m", [P, 1])
            k_m = sb("k_m", [P, 1])
            idb = sb("idb", [P, P], BF16)
            mask_t = sb("mask_t", [P, P], BF16)
            mask_s = sb("mask_s", [P, P], BF16)
            nsel_f = sb("nsel_f", [P, NQ, P])
            nsel = sb("nsel", [P, NQ, P], F32R)
            qs = sb("qs", [P, 2, NQ // 2, T], F32R)
            kz = sb("kz", [P, 2, 2, T], F32R)
            ktmp = sb("ktmp", [P, T], F32R)
            qtmp = sb("qtmp", [P, T], F32R)
            vT = sb("vT", [P, T])
            va = sb("va", [P, 2, NQ, J, P])
            mxs = sb("mxs", [P, J, NQ])
            mx_hi = sb("mx_hi", [P, J, NQ], F32R)
            mx2 = sb("mx2", [P, J, P])
            mT = sb("mT", [P, 2, T], F32R)
            ex = sb("ex", [P, 2, 1280])
            ob = sb("ob", [P, 2, T])
            rd = sb("rd", [P, T])
            at = sb("at", [P, T])
            at_hi = sb("at_hi", [P, T], F32R)
            at_lo = sb("at_lo", [P, T], F32R)
            p_a = ps("p_a", [P, T])
            p_s = ps("p_s", [P, 3 * T])
            p_st = ps("p_st", [P, 3 * T])
            p_o = ps("p_o", [P, T])

            COL = {0: 0, 1: T, 3: T + 3 * P, 2: 2 * T}
            CMAX = {3: 0, 2: T, 0: T + 3 * P, 1: 2 * T}
            WID = {b: T - P * b for b in range(J)}

            s_al_ = sem("t_loaded")
            s_rep = sem("t_replicated")
            s_th = sem("t_high")
            s_tl = sem("t_low")
            s_io = sem("t_iota")
            s_pm = sem("t_mask_zero")
            s_pm2 = sem("t_masks_made")
            s_bits = sem("t_bits")
            wparts = [(wq_hi[:].rearrange("p a b -> p (a b)"), wq_lo[:].rearrange("p a b -> p (a b)"),
                       wq_rep[:].rearrange("p a b c d -> p (a b c d)")),
                      (wk_hi[:], wk_lo[:], wk_rep[:].rearrange("p a b -> p (a b)")),
                      (wv_hi[:], wv_lo[:], wv_rep[:].rearrange("p a b -> p (a b)")),
                      (wp_hi[:], wp_lo[:], wp_raw[:])]
            with nc.Block() as block:
                @block.sync
                def _(sp):
                    sp.dma_start(wq_raw[:], Wq.rearrange("q c d -> c q d")).then_inc(s_al_, 16)
                    sp.dma_start(wk_raw[:], Wk).then_inc(s_al_, 16)
                    sp.dma_start(wv_raw[:], Wv).then_inc(s_al_, 16)
                    sp.dma_start(wp_raw[:], Wp).then_inc(s_al_, 16)
                    with nc.allow_non_contiguous_dma(reason="128 bias values"):
                        sp.dma_start(bp_col[:], bp.rearrange("(p a) -> p a", a=1)).then_inc(s_al_, 16)
                    sp.wait_ge(s_al_, 5 * 16)

                @block.gpsimd
                def _(pool):
                    pool.iota(part[:], pattern=[[0, 1]], base=0, channel_multiplier=1).then_inc(s_io, 1)
                    pool.memset(idb[:], 0.0).then_inc(s_pm, 1)
                    pool.memset(mask_t[:], 0.0).then_inc(s_pm, 1)
                    pool.memset(mask_s[:], 0.0).then_inc(s_pm, 1)
                    pool.memset(nsel_f[:], 0.0).then_inc(s_pm, 1)
                    pool.wait_ge(s_pm, 4)
                    pool.affine_select(out=idb[:], in_=idb[:], compare_op=ALU.not_equal, fill=1.0, base=0,
                                       pattern=[[-1, P]], channel_multiplier=1).then_inc(s_pm2, 1)
                    pool.affine_select(out=mask_t[:], in_=mask_t[:], compare_op=ALU.is_ge, fill=MASKED, base=0,
                                       pattern=[[-1, P]], channel_multiplier=1).then_inc(s_pm2, 1)
                    pool.affine_select(out=mask_s[:], in_=mask_s[:], compare_op=ALU.is_ge, fill=MASKED, base=0,
                                       pattern=[[1, P]], channel_multiplier=-1).then_inc(s_pm2, 1)
                    for k, base in enumerate((0, -NQ)):
                        pool.wait_ge(s_pm2, 3 + k)
                        pool.affine_select(out=nsel_f[:], in_=nsel_f[:], compare_op=ALU.not_equal, fill=-1.0,
                                           base=base, pattern=[[-1, NQ], [0, P]],
                                           channel_multiplier=1).then_inc(s_pm2, 1)
                    pool.wait_ge(s_pm2, 5)
                    pool.tensor_copy(nsel[:], nsel_f[:]).then_inc(s_pm2, 1)

                @block.vector
                def _(dve):
                    dve.wait_ge(s_al_, 5 * 16)
                    nc.vector.tensor_copy(wq_rep[:].rearrange("p a b c d -> p (a b) c d"),
                                          wq_raw[:].unsqueeze(2).broadcast_to([D, NQ, 4, DH])).then_inc(s_rep, 1)
                    nc.vector.tensor_copy(wk_rep[:], wk_raw[:].unsqueeze(1).broadcast_to([D, 8, DH])).then_inc(s_rep, 1)
                    nc.vector.tensor_copy(wv_rep[:], wv_raw[:].unsqueeze(1).broadcast_to([D, 8, DH])).then_inc(s_rep, 1)
                    dve.wait_ge(s_io, 1)
                    nc.vector.tensor_scalar(bit[:, 0:1], part[:], 4, 1, ALU.logical_shift_right,
                                            ALU.bitwise_and).then_inc(s_bits, 1)
                    nc.vector.tensor_scalar(bit[:, 1:2], part[:], 5, 1, ALU.logical_shift_right,
                                            ALU.bitwise_and).then_inc(s_bits, 1)
                    dve.wait_ge(s_bits, 2)
                    nc.vector.tensor_scalar(q_m[:], bit[:, 0:1], -1.0, None, ALU.mult).then_inc(s_bits, 1)
                    nc.vector.tensor_scalar(k_m[:], bit[:, 1:2], -1.0, None, ALU.mult).then_inc(s_bits, 1)
                    nc.vector.memset(raw(kz[:]), 0.0)
                    nc.vector.memset(mx2[:], 0.0)
                    nc.vector.memset(va[:], 0.0).then_inc(s_bits, 1)
                    dve.wait_ge(s_bits, 5)
                    for hd in range(NQ):
                        one = (64 if hd < 4 else 0) + DH * (hd % 4)
                        nc.vector.memset(va[:, :, hd, :, one:one + DH], 1.0)
                    for k, (hi, lo, src) in enumerate(wparts):
                        dve.wait_ge(s_th, k + 1)
                        nc.vector.tensor_tensor(lo, src, raw(hi), ALU.subtract).then_inc(s_tl, 1)

                @block.scalar
                def _(act):
                    act.wait_ge(s_rep, 3)
                    act.wait_ge(s_al_, 5 * 16)
                    for hi, lo, src in wparts:
                        nc.scalar.activation(hi, src, ACT.Copy).then_inc(s_th, 1)

            FRONT0 = ["k", "q0", "q1", "q2", "q3", "v", "vt", "m"]
            FRONT = ["k", "q0", "q1", "q2", "o", "q3", "v", "vt", "m"]

            def use(n, what):
                if isinstance(n, int) and n < 1:
                    return (n + 1) * len(FRONT0) + FRONT0.index(what)
                base = len(FRONT) * n + (2 * len(FRONT0) - len(FRONT))
                if isinstance(n, int) and n == N - 1:
                    return base + {"o": 0, "last": 1}[what]
                return base + FRONT.index(what)

            s_pa = sem("t_projected")
            s_pad = sem("t_projection_used")
            s_pah = sem("t_projection_high")
            s_sc = sem("t_scores")
            s_mx = sem("t_maxima")
            s_m1 = sem("t_maxima_high")
            s_m2 = sem("t_maxima_split")
            s_ss = sem("t_shifted_scores")
            s_ex = sem("t_exp")
            s_pv = sem("t_values_summed")
            s_po = sem("t_sums_copied")
            s_rd = sem("t_reciprocal")
            s_at = sem("t_normalised")
            s_ah = sem("t_out_high")
            s_all = sem("t_out_low")
            HALF = NQ // 2
            with nc.Block() as block:
                @block.tensor
                def _(pe):
                    pe.sem_inc(s_pv, 2)

                    def claim(u):
                        pe.wait_ge(s_pad, u + 1)

                    def project(n, f, what):
                        claim(use(n, what))
                        w_hi_, w_lo_ = {"k": (wk_hi[:], wk_lo[:]), "v": (wv_hi[:], wv_lo[:])}.get(what) or \
                            (wq_hi[:, int(what[1]), :], wq_lo[:, int(what[1]), :])
                        mm3(p_a[:], w_hi_, w_lo_, x_hi[:, tile_cols(f)], x_lo[:, tile_cols(f)]).then_inc(s_pa, 1)

                    def turn_values(n):
                        claim(use(n, "vt"))
                        for j in range(J):
                            last = nc.tensor.transpose(p_a[:, j * P:(j + 1) * P], vT[:, j * P:(j + 1) * P], ident[:])
                        last.then_inc(s_pa, 1)

                    def scores(f, fp, hd):
                        pe.wait_ge(s_mx, f * NQ + hd + 1)
                        for b in (3, 2, 0, 1):
                            w = (b + 1) * P
                            nc.tensor.matmul(p_s[:, CMAX[b]:CMAX[b] + w], qs[:, fp, hd // 2, b * P:(b + 1) * P],
                                             kz[:, fp, hd % 2, 0:w], start=True, stop=False)
                            last = nc.tensor.matmul(p_s[:, CMAX[b] + b * P:CMAX[b] + w], idb[:], mask_t[:],
                                                    start=False, stop=True)
                        last.then_inc(s_sc, 1)

                    def turn_maxima(n, f):
                        claim(use(n, "m"))
                        pe.wait_ge(s_m2, f * 2 + 2)
                        for j in range(J):
                            last = nc.tensor.transpose(p_a[:, j * P:(j + 1) * P], mx2[:, j, :], ident[:])
                        last.then_inc(s_pa, 1)

                    def shifted(n, par, hd):
                        pe.wait_ge(s_ex, n * NQ + hd + 1)
                        for b in (0, 1, 3, 2):
                            c0 = COL[b]
                            nc.tensor.matmul(p_st[:, c0:c0 + WID[b]], kz[:, par, hd % 2, b * P:(b + 1) * P],
                                             qs[:, par, hd // 2, b * P:T], start=True, stop=False)
                            nc.tensor.matmul(p_st[:, c0:c0 + WID[b]], nsel[:, hd, :], mT[:, par, b * P:T],
                                             start=False, stop=False)
                            last = nc.tensor.matmul(p_st[:, c0:c0 + P], idb[:], mask_s[:], start=False, stop=True)
                        last.then_inc(s_ss, 1)

                    def weigh(n, par, hd):
                        pe.wait_ge(s_ex, n * NQ + hd + 2)
                        if hd % HALF == 0:
                            pe.wait_ge(s_po, 2 * n + hd // HALF + 1)
                        for b in range(J):
                            last = nc.tensor.matmul(p_o[:, b * P:T], va[:, par, hd, b, :],
                                                    ex[:, hd % 2, COL[b]:COL[b] + WID[b]],
                                                    start=(hd % HALF == 0 and b == 0),
                                                    stop=(hd % HALF == HALF - 1 and b == J - 1))
                        last.then_inc(s_pv, 1)

                    def output(n, m, what):
                        claim(use(n, what))
                        pe.wait_ge(s_all, m + 1)
                        mm3(p_a[:], wp_hi[:], wp_lo[:], at_hi[:], at_lo[:]).then_inc(s_pa, 1)

                    def turn(n, par, front=True, before=True):
                        f, fp = n + 1, 1 - par
                        for hd in range(NQ):
                            shifted(n, par, hd)
                            if front:
                                if hd == 0:
                                    project(n, f, "k")
                                elif hd == 1:
                                    project(n, f, "q1")
                                elif 3 <= hd <= 5:
                                    scores(f, fp, 2 * hd - 4)
                                elif hd == 7:
                                    turn_maxima(n, f)
                            if hd == 2 and before:
                                output(n, n - 1, "o")
                            if front and hd == 2:
                                scores(f, fp, 0)
                            if hd > 0:
                                weigh(n, par, hd - 1)
                            if front:
                                if hd == 0:
                                    project(n, f, "q0")
                                elif hd == 1:
                                    project(n, f, "q2")
                                elif hd == 2:
                                    project(n, f, "q3")
                                    scores(f, fp, 1)
                                elif 3 <= hd <= 5:
                                    if hd == 3:
                                        project(n, f, "v")
                                    scores(f, fp, 2 * hd - 3)
                                elif hd == 6:
                                    turn_values(n)
                        weigh(n, par, NQ - 1)

                    for what in FRONT0[:6]:
                        project(-1, 0, what)
                    turn_values(-1)
                    for hd in range(NQ):
                        scores(0, 0, hd)
                    turn_maxima(-1, 0)
                    pe.wait_ge(s_pad, use(-1, "m") + 2)
                    turn(0, 0, before=False)
                    with pe.Fori(0, (N - 2) // 2) as m:
                        for par in (1, 0):
                            n = m * 2 + (2 - par)
                            pe.wait_ge(s_pad, use(n, "k") + 1)
                            turn(n, par)
                    pe.wait_ge(s_pad, use(N - 1, "o") + 1)
                    turn(N - 1, 1, front=False)
                    output(N - 1, N - 1, "last")

                @block.scalar
                def _(act):
                    act.sem_inc(s_ex, 1)
                    act.sem_inc(s_po, 1)

                    def high(n, what):
                        act.wait_ge(s_pa, use(n, what) + 1)
                        nc.scalar.activation((ktmp if what == "k" else qtmp)[:], p_a[:], ACT.Copy).then_inc(s_pah, 1)

                    def copy(n, what, dst):
                        act.wait_ge(s_pa, use(n, what) + 1)
                        nc.scalar.activation(dst, p_a[:], ACT.Copy).then_inc(s_pad, 1)

                    def exp(n, hd):
                        act.wait_ge(s_ss, n * NQ + hd + 1)
                        act.wait_ge(s_pv, n * NQ + hd + 1)
                        nc.scalar.activation(ex[:, hd % 2, :], p_st[:, 0:1280], ACT.Exp, scale=SCALE).then_inc(s_ex, 1)

                    def sums(n, half):
                        act.wait_ge(s_pv, n * NQ + HALF * (half + 1) + 2)
                        act.wait_ge(s_at, 2 * n + half + 1)
                        nc.scalar.activation(ob[:, half, :], p_o[:], ACT.Copy).then_inc(s_po, 1)

                    def store(n, m, what):
                        wait_apart(act, s_pa, use(n, what) + 1)
                        nc.scalar.activation(yT[:, tile_cols(m)], p_a[:], ACT.Identity, bias=bp_col[:]).then_inc(s_pad, 1)

                    def turn(n, par, front=True, before=True):
                        fp = 1 - par
                        for hd in range(NQ):
                            exp(n, hd)
                            if front:
                                if hd == 0:
                                    high(n, "k")
                                    high(n, "q0")
                                elif hd == 1:
                                    high(n, "q1")
                                    high(n, "q2")
                            if hd == 2 and before:
                                store(n, n - 1, "o")
                            if front:
                                if hd == 2:
                                    high(n, "q3")
                                elif hd == 3:
                                    copy(n, "v", vT[:])
                                elif hd == 7:
                                    copy(n, "m", mT[:, fp, :])
                            if hd == HALF:
                                sums(n, 0)
                        sums(n, 1)

                    for what in FRONT0[:5]:
                        high(-1, what)
                    copy(-1, "v", vT[:])
                    copy(-1, "m", mT[:, 0, :])
                    turn(0, 0, before=False)
                    with act.Fori(0, (N - 2) // 2) as m:
                        for par in (1, 0):
                            turn(m * 2 + (2 - par), par)
                    turn(N - 1, 1, front=False)
                    store(N - 1, N - 1, "last")

                @block.vector
                def _(dve):
                    dve.sem_inc(s_pad, 1)
                    dve.sem_inc(s_mx, 1)
                    dve.sem_inc(s_at, 2)

                    def stack(n, f, fp, what):
                        dve.wait_ge(s_pah, f * (HALF + 1) + 1 + ["k", "q0", "q1", "q2", "q3"].index(what))
                        if what == "k":
                            for half in range(2):
                                r = slice(64 * half, 64 * half + 64)
                                last = nc.vector.scalar_tensor_tensor(
                                    out=kz[r, fp, half, :], in0=raw(ktmp[r, :]), scalar=k_m[r, :],
                                    in1=p_a[r, :], op0=ALU.mult, op1=ALU.add)
                        else:
                            last = nc.vector.scalar_tensor_tensor(out=qs[:, fp, int(what[1]), :], in0=raw(qtmp[:]),
                                                                  scalar=q_m[:], in1=p_a[:], op0=ALU.mult,
                                                                  op1=ALU.add)
                        last.then_inc(s_pad, 1)

                    def values(n, fp):
                        dve.wait_ge(s_pa, use(n, "vt") + 1)
                        for hd in range(NQ):
                            c0 = (0 if hd < HALF else 64) + DH * (hd % HALF)
                            last = nc.vector.tensor_copy(va[:, fp, hd, :, c0:c0 + DH],
                                                         p_a[:].rearrange("p (j c) -> p j c", j=J)[:, :, 0:DH])
                        last.then_inc(s_pad, 1)

                    def maxima(f, hd):
                        dve.wait_ge(s_sc, f * NQ + hd + 1)
                        for b in range(J):
                            last = nc.vector.tensor_reduce(out=mxs[:, b, hd:hd + 1],
                                                           in_=p_s[:, CMAX[b]:CMAX[b] + (b + 1) * P],
                                                           op=ALU.max, axis=AX.X)
                        last.then_inc(s_mx, 1)

                    def split_maxima(n, f):
                        dve.wait_ge(s_mx, f * NQ + NQ + 1)
                        nc.vector.tensor_copy(mx_hi[:], mxs[:]).then_inc(s_m1, 1)
                        dve.wait_ge(s_m1, f + 1)
                        nc.vector.tensor_copy(mx2[:, :, 0:NQ], raw(mx_hi[:])).then_inc(s_m2, 1)
                        nc.vector.tensor_tensor(mx2[:, :, NQ:2 * NQ], mxs[:], raw(mx_hi[:]), ALU.subtract).then_inc(s_m2, 1)

                    def normalise(n, half):
                        num = slice(64 * half, 64 * half + 64)
                        den = slice(64 - 64 * half, 128 - 64 * half)
                        dve.wait_ge(s_po, 2 * n + half + 2)
                        nc.vector.reciprocal(rd[num, :], ob[den, half, :]).then_inc(s_rd, 1)
                        dve.wait_ge(s_rd, 2 * n + half + 1)
                        nc.vector.tensor_tensor(at[num, :], ob[num, half, :], rd[num, :], ALU.mult).then_inc(s_at, 1)

                    def split_out(n):
                        dve.wait_ge(s_at, 2 * n + 4)
                        nc.vector.tensor_copy(at_hi[:], at[:]).then_inc(s_ah, 1)
                        dve.wait_ge(s_ah, n + 1)
                        nc.vector.tensor_tensor(at_lo[:], at[:], raw(at_hi[:]), ALU.subtract).then_inc(s_all, 1)

                    def turn(n, par, front=True, before=True):
                        f, fp = n + 1, 1 - par
                        if front:
                            stack(n, f, fp, "k")
                            stack(n, f, fp, "q0")
                        if before:
                            normalise(n - 1, 1)
                            split_out(n - 1)
                        if front:
                            stack(n, f, fp, "q1")
                            stack(n, f, fp, "q2")
                            maxima(f, 0)
                            stack(n, f, fp, "q3")
                            for hd in range(1, 6):
                                maxima(f, hd)
                        normalise(n, 0)
                        if front:
                            maxima(f, 6)
                            maxima(f, 7)
                            split_maxima(n, f)
                            values(n, fp)

                    for what in FRONT0[:5]:
                        stack(-1, 0, 0, what)
                    values(-1, 0)
                    for hd in range(NQ):
                        maxima(0, hd)
                    split_maxima(-1, 0)
                    turn(0, 0, before=False)
                    with dve.Fori(0, (N - 2) // 2) as m:
                        for par in (1, 0):
                            turn(m * 2 + (2 - par), par)
                    turn(N - 1, 1, front=False)
                    normalise(N - 1, 1)
                    split_out(N - 1)
        scope.pop()

        scope.append(ExitStack())
        with scope[-1]:
            g1_hi = sb("g1_hi", [P, E1, 2, P], F32R)
            g1_lo = sb("g1_lo", [P, E1, 2, P], F32R)
            g3_hi = sb("g3_hi", [P, E1, 2, P], F32R)
            g3_lo = sb("g3_lo", [P, E1, 2, P], F32R)
            g2_hi = sb("g2_hi", [P, E1, 2, P], F32R)
            g2_lo = sb("g2_lo", [P, E1, 2, P], F32R)
            bT = sb("bT", [P, 2, E1, 2])
            b2b_hi = sb("b2b_hi", [P, D], F32R)
            b2b_lo = sb("b2b_lo", [P, D], F32R)
            scope.append(ExitStack())
            with scope[-1]:
                wr = sb("wr", [P, 3, E1, 2, P])
                br = sb("br", [P, 3, 2 * E1, 32])
                az = sb("az", [P, 2, 4, 4, P])
                az2 = sb("az2", [P, 2, 4, 2 * P])
                bt = sb("bt", [P, 10, P])
                bi_raw = sb("bi_raw", [4 * E1, P])
                b2b_raw = sb("b2b_raw", [P, D])
                p_bt = ps("p_bt", [P, 2, 4, P])
                p_w = ps("p_w", [P, 4, 4, P])
                p_bi = ps("p_bi", [P, 4 * E1])
                s_z = sem("m_zeroed")
                s_zp = sem("m_zeroed_pool")
                s_l = sem("m_loaded")
                s_bt = sem("m_b_transposed")
                s_btc = sem("m_b_stored")
                s_w = sem("m_merged")
                s_wh = sem("m_high")
                s_wl = sem("m_low")
                s_bi = sem("m_bias_transposed")
                NLD = 3 + 3 + 8 + 4 + 2 + 2
                with nc.Block() as block:
                    @block.gpsimd
                    def _(pool):
                        pool.memset(az[:], 0.0).then_inc(s_zp, 1)
                        pool.memset(az2[:], 0.0).then_inc(s_zp, 1)

                    @block.sync
                    def _(sp):
                        for k, w in enumerate((W1, W3)):
                            sp.dma_start(wr[:, k, :, :, :], w.rearrange("e (c p) d -> p e c d", p=P)).then_inc(s_l, 16)
                        sp.dma_start(wr[:, 2, :, :, :].rearrange("p e c m -> p e (c m)"),
                                     W2.rearrange("e d i -> d e i")).then_inc(s_l, 16)
                        sp.dma_start(bi_raw[0:2 * E1, :], b1_1.rearrange("e (c p) -> (e c) p", p=P)).then_inc(s_l, 16)
                        sp.dma_start(bi_raw[2 * E1:4 * E1, :], b3_1.rearrange("e (c p) -> (e c) p", p=P)).then_inc(s_l, 16)
                        sp.wait_ge(s_z, 2)
                        for k in range(2):
                            sp.dma_start(b2b_raw[16 * k:16 * k + E1, :], b2_1).then_inc(s_l, 16)
                        for k, b in enumerate((B1, B3)):
                            sp.dma_start(br[:, k, :, 0:R], b.rearrange("e (c p) r -> p (e c) r", p=P)).then_inc(s_l, 16)
                        sp.dma_start(br[:, 2, 0:E1, 0:R], B2.rearrange("e p r -> p e r")).then_inc(s_l, 16)
                        sp.wait_ge(s_zp, 2)
                        for k, a in enumerate((A1, A3)):
                            av = a.rearrange("(g f) r d -> f r g d", f=2)
                            for j in range(4):
                                sp.dma_start(az[32 * j:32 * j + R, k, :, j, :], av[j // 2]).then_inc(s_l, 16)
                        a2v = A2.rearrange("(g f) r h -> f r g h", f=4)
                        for j in range(4):
                            sp.dma_start(az2[32 * j:32 * j + R, :, j, :], a2v[j]).then_inc(s_l, 16)
                        sp.wait_ge(s_l, NLD * 16)

                    @block.tensor
                    def _(pe):
                        pe.wait_ge(s_l, NLD * 16)
                        nc.tensor.transpose(p_bi[:], bi_raw[:], ident[0:4 * E1, 0:4 * E1]).then_inc(s_bi, 1)
                        for t in range(10):
                            if t % 4 == 0 and t >= 8:
                                pe.wait_ge(s_btc, 1)
                            k, grp = (t // 4, t % 4)
                            last = nc.tensor.transpose(p_bt[:, (t // 4) % 2, t % 4, :],
                                                       br[:, k, 4 * grp:4 * grp + 4, :].rearrange("p a b -> p (a b)"),
                                                       ident[:])
                            if t in (3, 7, 9):
                                last.then_inc(s_bt, 1)
                        pe.wait_ge(s_btc, 3)
                        for s in range(12):
                            kind, pair = s // 4, s % 4
                            if s >= 4:
                                pe.wait_ge(s_wl, s - 3)
                            for m in range(4):
                                e, c = 2 * pair + m // 2, m % 2
                                dst = p_w[:, s % 4, m, :]
                                nc.tensor.matmul(dst, wr[:, kind, e, c, :], ident[:], start=True, stop=False)
                                if kind < 2:
                                    a, b = az[:, kind, pair, m, :], bt[:, 4 * kind + pair, :]
                                else:
                                    a, b = az2[:, e // 4, e % 4, c * P:(c + 1) * P], bt[:, 8 + e // 4, :]
                                last = nc.tensor.matmul(dst, a, b, start=False, stop=True)
                            last.then_inc(s_w, 1)

                    def target(s):
                        kind, pair = s // 4, s % 4
                        hi = (g1_hi, g3_hi, g2_hi)[kind][:, 2 * pair:2 * pair + 2, :, :]
                        lo = (g1_lo, g3_lo, g2_lo)[kind][:, 2 * pair:2 * pair + 2, :, :]
                        return [v.rearrange("p e c m -> p (e c) m") for v in (hi, lo)]

                    @block.scalar
                    def _(act):
                        for s in range(12):
                            act.wait_ge(s_w, s + 1)
                            nc.scalar.activation(target(s)[0], p_w[:, s % 4, :, :], ACT.Copy).then_inc(s_wh, 1)
                        act.wait_ge(s_l, NLD * 16)
                        nc.scalar.activation(b2b_hi[:], b2b_raw[:], ACT.Copy).then_inc(s_wh, 1)

                    @block.vector
                    def _(dve):
                        nc.vector.memset(br[:], 0.0).then_inc(s_z, 1)
                        nc.vector.memset(b2b_raw[:], 0.0).then_inc(s_z, 1)
                        for t, (a, w) in enumerate(((0, 4), (4, 4), (8, 2))):
                            dve.wait_ge(s_bt, t + 1)
                            nc.vector.tensor_copy(bt[:, a:a + w, :], p_bt[:, t % 2, 0:w, :]).then_inc(s_btc, 1)
                        dve.wait_ge(s_bi, 1)
                        nc.vector.tensor_copy(bT[:].rearrange("p a e c -> p (a e c)"), p_bi[:])
                        for s in range(12):
                            dve.wait_ge(s_wh, s + 1)
                            hi, lo = target(s)
                            nc.vector.tensor_tensor(lo, p_w[:, s % 4, :, :], raw(hi), ALU.subtract).then_inc(s_wl, 1)
                        dve.wait_ge(s_wh, 13)
                        nc.vector.tensor_tensor(b2b_lo[:], b2b_raw[:], raw(b2b_hi[:]), ALU.subtract).then_inc(s_wl, 1)
            scope.pop()
            experts("e1_", E1, g1_hi, g1_lo, bT[:, 0], g3_hi, g3_lo, bT[:, 1], g2_hi, g2_lo, b2b_hi, b2b_lo,
                    ACT.Silu, True)
        scope.pop()


_INS = ['L0_attn_x', 'L0_attn_W_in', 'L0_attn_conv_w', 'L0_attn_conv_b', 'L0_attn_W_g', 'L0_attn_b_g',
        'L0_attn_forget_base', 'L0_attn_W_out', 'L0_ffn_router_w', 'L0_ffn_router_b', 'L0_ffn_w1', 'L0_ffn_b1',
        'L0_ffn_w2', 'L0_ffn_b2', 'L1_attn_Wk', 'L1_attn_Wv', 'L1_attn_Wq', 'L1_attn_Wp', 'L1_attn_bp',
        'L1_ffn_Wg', 'L1_ffn_W1', 'L1_ffn_b1', 'L1_ffn_A1', 'L1_ffn_B1', 'L1_ffn_W2', 'L1_ffn_b2', 'L1_ffn_A2',
        'L1_ffn_B2', 'L1_ffn_W3', 'L1_ffn_b3', 'L1_ffn_A3', 'L1_ffn_B3']


def kernel(**inputs):
    import numpy as _np
    import concourse.bacc as _bacc
    from concourse import mybir as _mybir
    from concourse.bass_utils import run_bass_kernel_spmd as _run

    nc = _bacc.Bacc("TRN2", target_bir_lowering=False, num_devices=1)
    arrays, args = {}, []
    for name in _INS:
        a = _np.ascontiguousarray(inputs[name])
        arrays[f"in_{name}_dram"] = a
        args.append(nc.dram_tensor(f"in_{name}_dram", a.shape, _mybir.dt.from_np(a.dtype), kind="ExternalInput").ap())
    shape = inputs['L0_attn_x'].shape
    args.append(nc.dram_tensor("out_0_dram", shape, _mybir.dt.float32, kind="ExternalOutput").ap())
    two_block_kernel(nc, *args)
    r = _run(nc, [arrays], core_ids=[0])
    return r.results[0]["out_0_dram"]
```

```python
from contextlib import ExitStack

import concourse.bass as bass
from concourse import mybir

ALU = mybir.AluOpType
ACT = mybir.ActivationFunctionType
AX = mybir.AxisListType
F32 = mybir.dt.float32
F32R = mybir.dt.float32r
BF16 = mybir.dt.bfloat16
I32 = mybir.dt.int32

P = 128
T = 512
J = T // P
LN_EPS = 1e-5
ALPHA_SCALE = 8.0
BETA_EPS = 1e-6
MASKED = -1e30


def raw(ap):
    return ap.bitcast(F32)


def two_block_kernel(nc, x_in, W_in, conv_w, conv_b, W_g, b_g, forget_base, W_out,
                     router_w, router_b, w1, b1, w2, b2,
                     Wk, Wv, Wq, Wp, bp,
                     Wg, W1, b1_1, A1, B1, W2, b2_1, A2, B2, W3, b3_1, A3, B3, out):
    N, _, D = x_in.shape
    HR = W_out.shape[1]
    C2 = HR // 2
    TAPS = conv_w.shape[2]
    E0, _, I0 = w1.shape
    E1, I1, _ = W1.shape
    R = A1.shape[1]
    NQ, _, DH = Wq.shape
    K0, K1 = 4, 2
    NB = N * J
    SCALE = float(D) ** -0.5
    assert D == P and I0 == 2 * P and I1 == 2 * P and T == x_in.shape[1]

    root = ExitStack()
    scope = [root]

    def sb(name, shape, dt=F32):
        return scope[-1].enter_context(nc.sbuf_tensor(name, shape, dt))

    def ps(name, shape, dt=F32):
        return scope[-1].enter_context(nc.psum_tensor(name, shape, dt))

    def sem(name):
        return root.enter_context(nc.semaphore(name))

    def tile_cols(n):
        return bass.ds(n * T, T)

    def wait_apart(eng, semaphore, value):
        eng.wait_ge(semaphore, 1)
        eng.wait_ge(semaphore, value)
        eng.wait_ge(semaphore, 1)

    def mm3(dst, w_hi, w_lo, m_hi, m_lo, start=True, stop=True):
        nc.tensor.matmul(dst, w_hi, m_hi, start=start, stop=False)
        nc.tensor.matmul(dst, w_hi, m_lo, start=False, stop=False)
        return nc.tensor.matmul(dst, w_lo, m_hi, start=False, stop=stop)

    with root:
        xres = sb("xres", [P, NB, D])
        x_hi = sb("x_hi", [P, N * T], F32R)
        x_lo = sb("x_lo", [P, N * T], F32R)
        yT = sb("yT", [P, N * T])
        gT = sb("gT", [P, N * T], F32R)
        ident = sb("ident", [P, P])
        stats = sb("stats", [P, NB, 6])
        ROWS = 4
        sel = sb("sel", [P, E0 // ROWS, P], F32R)

        s_const0 = sem("const_zeroed")
        s_const = sem("const_made")
        s_xload = [sem(f"x_loaded_{n}") for n in range(N // 2)]

        class Router:
            def __init__(self, tag, E, K):
                self.E, self.K = E, K
                self.lg = sb(tag + "lg", [P, NB, E])
                self.pr = sb(tag + "pr", [P, NB, E])
                self.mx = sb(tag + "mx", [P, NB])
                self.sm = sb(tag + "sm", [P, NB])
                self.top = sb(tag + "top", [P, NB, 8])
                self.cut = sb(tag + "cut", [P, NB, E])
                self.c_hi = sb(tag + "c_hi", [P, NB, E], F32R)
                self.c2 = sb(tag + "c2", [P, NB, 32])
                self.s_lg = sem(tag + "logits_ready")
                self.s_rt = sem(tag + "route_step")
                self.s_exp = sem(tag + "exp_ready")
                self.s_c2z = sem(tag + "gates_zeroed")
                self.s_c2 = sem(tag + "gates_ready")
                self.s_gt = sem(tag + "gates_transposed")
                self.s_gc = sem(tag + "gates_stored")

        def fetch_logits(dve, r, p_lg, bias, s_bias):
            if bias is not None:
                dve.wait_ge(s_bias, 16)
            for half in range(2):
                dve.wait_ge(r.s_lg, half + 1)
                src = p_lg[:, half, :].rearrange("p (j n e) -> p j n e", j=J, e=32)[:, :, :, 0:r.E]
                dst = r.lg[:, half * NB // 2:(half + 1) * NB // 2, :].rearrange("p (n j) e -> p j n e", j=J)
                for j in range(J):
                    if bias is None:
                        last = nc.vector.tensor_copy(dst[:, j], src[:, j])
                    else:
                        last = nc.vector.tensor_tensor(dst[:, j], src[:, j],
                                                       bias.unsqueeze(1).broadcast_to([P, J, r.E]), ALU.add)
            last.then_inc(r.s_rt, 1)

        def route_vector(dve, r):
            E, step = r.E, [1]
            dve.wait_ge(r.s_rt, 1)

            def chain(ins):
                step[0] += 1
                ins.then_inc(r.s_rt, 1)
                dve.wait_ge(r.s_rt, step[0])

            def over_experts(ap):
                return ap.unsqueeze(2).broadcast_to([P, NB, E])

            chain(nc.vector.tensor_reduce(out=r.mx[:], in_=r.lg[:], op=ALU.max, axis=AX.X))
            chain(nc.vector.tensor_tensor(r.lg[:], r.lg[:], over_experts(r.mx[:]), ALU.subtract))
            dve.wait_ge(r.s_exp, 1)
            chain(nc.vector.tensor_reduce(out=r.sm[:], in_=r.pr[:], op=ALU.add, axis=AX.X))
            chain(nc.vector.reciprocal(r.sm[:], r.sm[:]))
            chain(nc.vector.tensor_tensor(r.pr[:], r.pr[:], over_experts(r.sm[:]), ALU.mult))
            for k in range(NB):
                nc.vector.max(r.top[:, k, :], r.pr[:, k, :]).then_inc(r.s_rt, 1)
            step[0] += NB
            dve.wait_ge(r.s_rt, step[0])
            chain(nc.vector.memset(r.top[:, :, r.K:8], -1.0))
            for k in range(NB):
                nc.vector.match_replace(out=r.cut[:, k, :], in_to_replace=r.top[:, k, :],
                                        in_values=r.pr[:, k, :], imm_value=-2.0).then_inc(r.s_rt, 1)
            step[0] += NB
            dve.wait_ge(r.s_rt, step[0])
            chain(nc.vector.tensor_scalar(r.cut[:], r.cut[:], -2.0, None, ALU.is_equal))
            chain(nc.vector.tensor_tensor(r.pr[:], r.pr[:], r.cut[:], ALU.mult))
            chain(nc.vector.tensor_reduce(out=r.sm[:], in_=r.pr[:], op=ALU.add, axis=AX.X))
            chain(nc.vector.reciprocal(r.sm[:], r.sm[:]))
            chain(nc.vector.tensor_tensor(r.pr[:], r.pr[:], over_experts(r.sm[:]), ALU.mult))
            dve.wait_ge(r.s_c2z, 1)
            chain(nc.vector.tensor_copy(r.c_hi[:], r.pr[:]))
            chain(nc.vector.tensor_copy(r.c2[:, :, 0:E], raw(r.c_hi[:])))
            nc.vector.tensor_tensor(r.c2[:, :, 16:16 + E], r.pr[:], raw(r.c_hi[:]), ALU.subtract).then_inc(r.s_c2, 1)

        def route_scalar(act, r):
            act.wait_ge(r.s_rt, 3)
            nc.scalar.activation(r.pr[:], r.lg[:], ACT.Exp).then_inc(r.s_exp, 1)

        def store_gates(act, r, p_g, banks):
            act.wait_ge(s_const0, 3)
            for n in range(N):
                act.wait_ge(r.s_gt, n + 1)
                nc.scalar.activation(gT[0:32, n * T:(n + 1) * T], p_g[0:32, n % banks, :],
                                     ACT.Copy).then_inc(r.s_gc, 1)

        def turn_gates(pe, r, p_g, banks):
            pe.wait_ge(r.s_c2, 1)
            for n in range(N):
                if n >= banks:
                    pe.wait_ge(r.s_gc, n - banks + 1)
                for j in range(J):
                    last = nc.tensor.transpose(p_g[0:32, n % banks, j * P:(j + 1) * P],
                                               r.c2[:, n * J + j, :], ident[:])
                last.then_inc(r.s_gt, 1)

        def normalise_stream(tag, r, route_now, router_load, router_transposed, bias_load, x_loads, aside,
                             aside_read=None):
            E = r.E
            scope.append(ExitStack())
            with scope[-1]:
                mv = sb(tag + "mv", [P, NB, 2])
                rstd = sb(tag + "rstd", [P, NB])
                xn = sb(tag + "xn", [P, 2, J, D])
                rw = sb(tag + "rw", [P, 32])
                lt = sb(tag + "lt", [P, 2, T])
                rw_raw = sb(tag + "rwraw", [16, P])
                rw_hi = sb(tag + "rw_hi", [P, 4, P], F32R)
                rw_lo = sb(tag + "rw_lo", [P, 4, P], F32R)
                rb = sb(tag + "rb", [P, 16])
                p_x = ps(tag + "p_x", [P, 2, T])
                p_lt = ps(tag + "p_lt", [P, 2, T])
                p_g = ps(tag + "p_g", [P, 2, T])
                p_aside = ps(tag + "p_aside", [P, 2, T])
                p_rw = p_aside[:, 0, 0:16]
                p_lg = p_x
                s_lt = sem(tag + "logits_made")
                s_ltc = sem(tag + "logits_in_sbuf")
                s_rw = sem(tag + "router_loaded")
                s_rb = sem(tag + "router_bias_loaded") if bias_load is not None else None
                s_rwz = sem(tag + "router_zeroed")
                if router_transposed:
                    s_rwt = sem(tag + "router_transposed")
                    s_rwf = sem(tag + "router_in_sbuf")
                s_rwh = sem(tag + "router_split")
                if x_loads:
                    s_st = sem(tag + "stats_made")
                s_mv = sem(tag + "moments_made")
                s_var = sem(tag + "variance_eps")
                s_std = sem(tag + "std_made")
                s_rstd = sem(tag + "rstd_made")
                s_xn = sem(tag + "normalised")
                s_tr = sem(tag + "transposed")
                s_hi = sem(tag + "x_hi_ready")
                s_lo = sem(tag + "x_lo_ready")
                with nc.Block() as block:
                    @block.sync
                    def _(sp):
                        if x_loads:
                            for n in range(N):
                                sp.dma_start(xres[:, n * J:(n + 1) * J, :],
                                             x_in[n].rearrange("(j p) d -> p j d", p=P)).then_inc(s_xload[n // 2], 16)
                        sp.wait_ge(s_rwz, 1)
                        if router_transposed:
                            sp.dma_start(rw_raw[0:E, :], router_load).then_inc(s_rw, 16)
                        else:
                            sp.dma_start(rw[:, 0:E], router_load).then_inc(s_rw, 16)
                        sp.wait_ge(s_rw, 16)
                        if bias_load is not None:
                            sp.dma_start(rb[:, 0:E], bias_load).then_inc(s_rb, 16)
                            sp.wait_ge(s_rb, 16)
                        aside["sync"](sp)

                    @block.gpsimd
                    def _(pool):
                        pool.memset(r.c2[:], 0.0).then_inc(r.s_c2z, 1)
                        aside["gpsimd"](pool)

                    @block.vector
                    def _(dve):
                        nc.vector.memset(rw[:], 0.0).then_inc(s_rwz, 1)
                        nc.vector.memset(raw(rw_hi[:]), 0.0).then_inc(s_rwz, 1)
                        nc.vector.memset(raw(rw_lo[:]), 0.0).then_inc(s_rwz, 1)
                        if x_loads:
                            for k in range(NB):
                                if k % (2 * J) == 0:
                                    dve.wait_ge(s_xload[k // (2 * J)], 2 * 16)
                                nc.vector.bn_stats(stats[:, k, :], xres[:, k, :]).then_inc(s_st, 1)
                        for k in range(NB):
                            if x_loads:
                                dve.wait_ge(s_st, k + 1)
                            nc.vector.bn_aggr(mv[:, k, :], stats[:, k, :]).then_inc(s_mv, 1)
                        dve.wait_ge(s_mv, NB)
                        nc.vector.tensor_scalar(rstd[:], mv[:, :, 1], LN_EPS, None, ALU.add).then_inc(s_var, 1)
                        if router_transposed:
                            dve.wait_ge(s_rwt, 1)
                            dve.wait_ge(s_rwz, 1)
                            nc.vector.tensor_copy(rw[:, 0:E], p_rw[:, 0:E]).then_inc(s_rwf, 1)
                            dve.wait_ge(s_rwf, 1)
                        else:
                            dve.wait_ge(s_rw, 16)
                        dve.wait_ge(s_rwz, 3)
                        for k in range(4):
                            nc.vector.tensor_copy(rw_hi[:, k, 32 * k:32 * k + 32], rw[:]).then_inc(s_rwh, 1)
                        dve.wait_ge(s_rwh, 4)
                        for k in range(4):
                            nc.vector.tensor_tensor(rw_lo[:, k, 32 * k:32 * k + 32], rw[:],
                                                    raw(rw_hi[:, k, 32 * k:32 * k + 32]),
                                                    ALU.subtract).then_inc(s_rwh, 1)
                        dve.wait_ge(s_std, 1)
                        nc.vector.reciprocal(rstd[:], rstd[:]).then_inc(s_rstd, 1)
                        dve.wait_ge(s_rstd, 1)
                        for n in range(N):
                            if n >= 2:
                                dve.wait_ge(s_tr, n - 1)
                            for j in range(J):
                                k = n * J + j
                                nc.vector.tensor_scalar(xn[:, n % 2, j, :], xres[:, k, :], mv[:, k, 0:1],
                                                        rstd[:, k:k + 1], ALU.subtract,
                                                        ALU.mult).then_inc(s_xn, 1)
                            if n >= 1:
                                dve.wait_ge(s_hi, n)
                                nc.vector.tensor_tensor(x_lo[:, (n - 1) * T:n * T], p_x[:, (n - 1) % 2, :],
                                                        raw(x_hi[:, (n - 1) * T:n * T]),
                                                        ALU.subtract).then_inc(s_lo, 1)
                        dve.wait_ge(s_hi, N)
                        nc.vector.tensor_tensor(x_lo[:, (N - 1) * T:N * T], p_x[:, (N - 1) % 2, :],
                                                raw(x_hi[:, (N - 1) * T:N * T]), ALU.subtract).then_inc(s_lo, 1)
                        aside["vector"](dve, p_aside, p_g)
                        fetch_logits(dve, r, p_lg, None if bias_load is None else rb[:, 0:E], s_rb)
                        if route_now:
                            route_vector(dve, r)

                    @block.scalar
                    def _(act):
                        act.wait_ge(s_var, 1)
                        nc.scalar.activation(rstd[:], rstd[:], ACT.Sqrt).then_inc(s_std, 1)
                        for n in range(N):
                            act.wait_ge(s_tr, n + 1)
                            nc.scalar.activation(x_hi[:, n * T:(n + 1) * T], p_x[:, n % 2, :],
                                                 ACT.Copy).then_inc(s_hi, 1)
                        for half in range(2):
                            act.wait_ge(s_lt, 4 * (half + 1))
                            nc.scalar.activation(lt[:, half, :], p_lt[:, half, :], ACT.Copy).then_inc(s_ltc, 1)
                        aside["scalar"](act, p_aside, p_g)
                        if route_now:
                            route_scalar(act, r)
                            store_gates(act, r, p_g, 2)

                    @block.tensor
                    def _(pe):
                        pe.wait_ge(s_const, 1)
                        if router_transposed:
                            pe.wait_ge(s_rw, 16)
                            nc.tensor.transpose(p_rw[:, 0:E], rw_raw[0:E, :], ident[0:E, 0:E]).then_inc(s_rwt, 1)
                        def logits(n):
                            if n == 0:
                                pe.wait_ge(s_rwh, 8)
                            pe.wait_ge(s_lo, n + 1)
                            mm3(p_lt[:, n // 4, :], rw_hi[:, n % 4, :], rw_lo[:, n % 4, :],
                                x_hi[:, n * T:(n + 1) * T], x_lo[:, n * T:(n + 1) * T],
                                start=n % 4 == 0, stop=n % 4 == 3).then_inc(s_lt, 1)

                        def turn_logits(half):
                            pe.wait_ge(s_lo, N)
                            pe.wait_ge(s_ltc, half + 1)
                            for j in range(J):
                                last = nc.tensor.transpose(p_lg[:, half, j * P:(j + 1) * P],
                                                           lt[:, half, j * P:(j + 1) * P], ident[:])
                            last.then_inc(r.s_lg, 1)

                        for n in range(N):
                            pe.wait_ge(s_xn, (n + 1) * J)
                            if n >= 2:
                                pe.wait_ge(s_lo, n - 1)
                            for j in range(J):
                                last = nc.tensor.transpose(p_x[:, n % 2, j * P:(j + 1) * P],
                                                           xn[:, n % 2, j, :], ident[:])
                            last.then_inc(s_tr, 1)
                            if n >= 2:
                                logits(n - 2)
                        if "tensor" in aside:
                            aside["tensor"](pe, p_aside, p_g)
                        logits(N - 2)
                        logits(N - 1)
                        turn_logits(0)
                        turn_logits(1)
                        if aside_read is not None:
                            pe.wait_ge(*aside_read)
                        if route_now:
                            turn_gates(pe, r, p_g, 2)
            scope.pop()

        layer0 = ExitStack()
        root.enter_context(layer0)
        scope.append(layer0)
        hg = sb("hg", [P, 2, 2, 2, T])
        b1_raw = sb("b1_raw", [2 * E0, P])
        b2_raw = sb("b2_raw", [P, D])
        s_w1 = sem("e0_w1_loaded")
        s_eb = sem("e0_biases_loaded")
        s_b2z = sem("e0_bias_zeroed")
        w1_raw = hg[:].rearrange("p b c i (e h) -> p (b c i e) h", h=2 * P)
        scope.append(ExitStack())
        with scope[-1]:
            win_raw = sb("win_raw", [C2, 4, D])
            wg_raw = sb("wg_raw", [C2, 4, HR])
            wout_raw = sb("wout_raw", [D, HR])
            win_hi = sb("win_hi", [D, 4, C2], F32R)
            win_lo = sb("win_lo", [D, 4, C2], F32R)
            wg_hi = sb("wg_hi", [C2, 8, C2], F32R)
            wg_lo = sb("wg_lo", [C2, 8, C2], F32R)
            wo = sb("wo", [C2, 2, D])
            cw = sb("cw", [C2, 2, TAPS])
            cb = sb("cb", [C2, 2])
            bg = sb("bg", [C2, 4])
            fb = sb("fb", [C2, 2])
            kf = sb("kf", [C2, 2])
            spt = sb("spt", [C2, 2])
            one_eps = sb("one_eps", [C2, 1])
            xp = sb("xp", [C2, 4, 4 + T])
            sel_f = sb("sel_f", [P, E0 // ROWS, P])
            s_ld = sem("r_weights_loaded")
            s_wt = sem("r_weights_transposed")
            s_wh = sem("r_weights_high")
            s_wl = sem("r_weights_low")
            s_small = sem("r_small_step")
            s_sp = sem("r_softplus_step")
            pad = TAPS - 1

            def mixer_sync(sp):
                sp.dma_start(win_raw[:], W_in.rearrange("(c p) d -> p c d", p=C2)).then_inc(s_ld, 16)
                sp.dma_start(wg_raw[:], W_g.rearrange("(c p) h -> p c h", p=C2)).then_inc(s_ld, 16)
                sp.dma_start(wout_raw[:], W_out).then_inc(s_ld, 16)
                sp.dma_start(cw[:], conv_w.rearrange("(c p) a k -> p c (a k)", p=C2)).then_inc(s_ld, 16)
                with nc.allow_non_contiguous_dma(reason="a few hundred bias values"):
                    sp.dma_start(cb[:], conv_b.rearrange("(c p) -> p c", p=C2)).then_inc(s_ld, 16)
                    sp.dma_start(bg[:], b_g.rearrange("(c p) -> p c", p=C2)).then_inc(s_ld, 16)
                    sp.dma_start(fb[:], forget_base.rearrange("(c p) -> p c", p=C2)).then_inc(s_ld, 16)
                sp.wait_ge(s_ld, 7 * 16)

            def constants_pool(pool):
                pool.memset(ident[:], 0.0).then_inc(s_const0, 1)
                pool.wait_ge(s_const0, 1)
                pool.affine_select(out=ident[:], in_=ident[:], compare_op=ALU.not_equal, fill=1.0,
                                   base=0, pattern=[[-1, P]], channel_multiplier=1).then_inc(s_const, 1)
                pool.memset(sel_f[:], 0.0).then_inc(s_const0, 1)
                pool.memset(raw(gT[:]), 0.0).then_inc(s_const0, 1)
                pool.wait_ge(s_const0, 3)
                for part_ in range(2):
                    for row in range(ROWS):
                        column = sel_f[:, :, 32 * row]
                        pool.wait_ge(s_const, ROWS * part_ + row + 1)
                        pool.affine_select(out=column, in_=column, compare_op=ALU.not_equal, fill=1.0,
                                           base=-(row + 16 * part_), pattern=[[-ROWS, E0 // ROWS]],
                                           channel_multiplier=1).then_inc(s_const, 1)
                pool.wait_ge(s_const, 2 * ROWS + 1)
                pool.tensor_copy(sel[:], sel_f[:]).then_inc(s_const, 1)

            def mixer_tensor(pe, p_aside, p_g):
                pe.wait_ge(s_ld, 7 * 16)
                for c in range(4):
                    last = nc.tensor.transpose(p_g[:, 0, c * C2:(c + 1) * C2], win_raw[:, c, :],
                                               ident[0:C2, 0:C2])
                last.then_inc(s_wt, 1)
                for hc in range(2):
                    for gc in range(4):
                        last = nc.tensor.transpose(p_aside[0:C2, hc, gc * C2:(gc + 1) * C2],
                                                   wg_raw[:, gc, hc * C2:(hc + 1) * C2], ident[0:C2, 0:C2])
                last.then_inc(s_wt, 1)
                for hc in range(2):
                    last = nc.tensor.transpose(p_g[0:C2, 1, hc * P:(hc + 1) * P],
                                               wout_raw[:, hc * C2:(hc + 1) * C2], ident[:])
                last.then_inc(s_wt, 1)

            def mixer_splits(p_aside, p_g):
                return [(v_hi.rearrange("p a b -> p (a b)"), v_lo.rearrange("p a b -> p (a b)"), src, need)
                        for v_hi, v_lo, src, need in (
                            (win_hi[:], win_lo[:], p_g[:, 0, 0:4 * C2], 1),
                            (wg_hi[:, 0:4, :], wg_lo[:, 0:4, :], p_aside[0:C2, 0, 0:4 * C2], 2),
                            (wg_hi[:, 4:8, :], wg_lo[:, 4:8, :], p_aside[0:C2, 1, 0:4 * C2], 2))]

            def mixer_scalar(act, p_aside, p_g):
                for hi, lo, src, need in mixer_splits(p_aside, p_g):
                    act.wait_ge(s_wt, need)
                    nc.scalar.activation(hi, src, ACT.Copy).then_inc(s_wh, 1)
                act.wait_ge(s_ld, 7 * 16)
                nc.scalar.activation(spt[:], fb[:], ACT.Abs).then_inc(s_sp, 1)
                act.wait_ge(s_sp, 1)
                nc.scalar.activation(spt[:], spt[:], ACT.Exp, scale=-1.0).then_inc(s_sp, 1)
                act.wait_ge(s_sp, 2)
                nc.scalar.activation(spt[:], spt[:], ACT.Ln, bias=1.0).then_inc(s_sp, 1)

            def mixer_vector(dve, p_aside, p_g):
                for k, (hi, lo, src, need) in enumerate(mixer_splits(p_aside, p_g)):
                    dve.wait_ge(s_wh, k + 1)
                    nc.vector.tensor_tensor(lo, src, raw(hi), ALU.subtract).then_inc(s_wl, 1)
                dve.wait_ge(s_wt, 3)
                nc.vector.tensor_copy(wo[:].rearrange("p a b -> p (a b)"), p_g[0:C2, 1, 0:2 * P]).then_inc(s_wl, 1)
                nc.vector.memset(xp[:, :, 0:pad], 0.0)
                nc.vector.memset(one_eps[:], (1.0 + BETA_EPS) / 4)
                dve.wait_ge(s_ld, 7 * 16)
                nc.vector.tensor_scalar(bg[:], bg[:], 0.5, None, ALU.mult)
                nc.vector.tensor_scalar(kf[:], fb[:], 0.0, None, ALU.max).then_inc(s_small, 1)
                dve.wait_ge(s_sp, 3)
                dve.wait_ge(s_small, 1)
                nc.vector.tensor_tensor(kf[:], kf[:], spt[:], ALU.add).then_inc(s_small, 1)
                dve.wait_ge(s_small, 2)
                nc.vector.tensor_scalar(kf[:], kf[:], -ALPHA_SCALE / 2, None, ALU.mult).then_inc(s_small, 1)

            scope.append(ExitStack())
            with scope[-1]:
                normalise_stream("a_", Router("a_", E0, K0), True, router_w, False,
                                 router_b.rearrange("(a e) -> a e", a=1).broadcast_to([P, E0]), True,
                                 {"sync": mixer_sync, "gpsimd": constants_pool, "tensor": mixer_tensor,
                                  "scalar": mixer_scalar, "vector": mixer_vector}, (s_wl, 4))
            scope.pop()

            cv = sb("cv", [C2, 2, T])
            xb = sb("xb", [C2, 4, T])
            xb_hi = sb("xb_hi", [C2, 2, T], F32R)
            xb_lo = sb("xb_lo", [C2, 2, T], F32R)
            tf = sb("tf", [C2, 2, T])
            ti = sb("ti", [C2, 4, T])
            al = sb("al", [C2, 4, T])
            sq = sb("sq", [C2, 2, T])
            be = sb("be", [C2, 2, T])
            gl = sb("gl", [C2, 4, T])
            xs = sb("xs", [C2, 2, T])
            hs = sb("hs", [C2, 2, T])
            z = sb("z", [C2, 2, T])
            p_gate = ps("p_gate", [P, 2, T])
            p_xb = ps("p_xb", [P, 2, T])
            p_f = ps("p_f", [P, 3, T])
            p_y = ps("p_y", [P, T])

            s_a = sem("r_input_projected")
            s_g = sem("r_gate_projected")
            s_xp = sem("r_conv_input")
            s_xb = sem("r_conv_step")
            s_xh = sem("r_conv_high")
            s_xl = sem("r_conv_low")
            s_fi = sem("r_gates_projected")
            s_tf = sem("r_forget_tanh")
            s_ti = sem("r_input_tanh")
            s_al = sem("r_alpha")
            s_a2 = sem("r_alpha_squared")
            s_be = sem("r_beta")
            s_gl = sem("r_gelu")
            s_u = sem("r_scan_input_step")
            s_h = sem("r_scanned")
            s_z = sem("r_gated")
            s_y = sem("r_output")
            s_yc = sem("r_output_stored")

            def both(buf, n):
                return buf[:, bass.ds((n % 2) * 2, 2), :]

            def chunk(buf, n, c):
                return buf[:, bass.ds((n % 2) * 2 + c, 1), :]

            with nc.Block() as block:
                @block.sync
                def _(sp):
                    sp.dma_start(w1_raw, w1.rearrange("e h i -> h e i")).then_inc(s_w1, 16)
                    sp.dma_start(b1_raw[:], b1.rearrange("e (c p) -> (e c) p", p=P)).then_inc(s_eb, 16)
                    sp.wait_ge(s_b2z, 1)
                    for k in range(2):
                        sp.dma_start(b2_raw[16 * k:16 * k + E0, :], b2).then_inc(s_eb, 16)

                @block.gpsimd
                def _(pool):
                    pool.memset(b2_raw[:], 0.0).then_inc(s_b2z, 1)

                @block.tensor
                def _(pe):
                    def project_input(n):
                        for c in range(2):
                            last = mm3(p_xb[0:C2, c, :], win_hi[:, 2 + c, :], win_lo[:, 2 + c, :],
                                       x_hi[:, tile_cols(n)], x_lo[:, tile_cols(n)])
                        last.then_inc(s_a, 1)

                    def project_gate(n):
                        for c in range(2):
                            last = mm3(p_gate[0:C2, c, :], win_hi[:, c, :], win_lo[:, c, :],
                                       x_hi[:, tile_cols(n)], x_lo[:, tile_cols(n)])
                        last.then_inc(s_g, 1)

                    def gates(n):
                        pe.wait_ge(s_xl, n + 1)
                        pe.wait_ge(s_ti, 2 * n + 1)
                        for gc in range(4):
                            if gc == 3:
                                pe.wait_ge(s_tf, 2 * n + 1)
                            for hc in range(2):
                                last = mm3(p_f[0:C2, gc % 3, :], wg_hi[:, 4 * hc + gc, :], wg_lo[:, 4 * hc + gc, :],
                                           xb_hi[:, hc, :], xb_lo[:, hc, :], start=hc == 0, stop=hc == 1)
                            last.then_inc(s_fi, 1)

                    def output(n):
                        pe.wait_ge(s_yc, n + 1)
                        pe.wait_ge(s_z, n + 1)
                        for hc in range(2):
                            last = nc.tensor.matmul(p_y[:], wo[:, hc, :], z[:, hc, :],
                                                    start=hc == 0, stop=hc == 1)
                        last.then_inc(s_y, 1)

                    def turn(n, before=True, after=2):
                        gates(n)
                        if before:
                            output(n - 1)
                        if after == 2:
                            pe.wait_ge(s_xp, n + 2)
                            project_input(n + 2)
                        if after >= 1:
                            pe.wait_ge(s_gl, n + 1)
                            project_gate(n + 1)

                    pe.sem_inc(s_y, 1)
                    project_input(0)
                    project_gate(0)
                    pe.wait_ge(s_xp, 1)
                    project_input(1)
                    turn(0, before=False)
                    with pe.Fori(1, N - 2) as n:
                        turn(n)
                    turn(N - 2, after=1)
                    turn(N - 1, after=0)
                    output(N - 1)

                @block.scalar
                def _(act):
                    act.sem_inc(s_yc, 1)
                    act.sem_inc(s_ti, 1)

                    def conv_input(n):
                        wait_apart(act, s_a, n + 1)
                        nc.scalar.activation(xp[:, bass.ds((n % 2) * 2, 2), pad:pad + T], p_xb[0:C2, :, :],
                                             ACT.Copy).then_inc(s_xp, 1)

                    def gelu(n):
                        wait_apart(act, s_g, n + 1)
                        nc.scalar.activation(both(gl, n), p_gate[0:C2, :, :], ACT.Gelu).then_inc(s_gl, 1)

                    def gates(n):
                        for c in range(2):
                            act.wait_ge(s_fi, n * 4 + c + 1)
                            nc.scalar.activation(tf[:, c, :], p_f[0:C2, c, :], ACT.Tanh, bias=bg[:, c:c + 1],
                                                 scale=0.5).then_inc(s_tf, 1)
                        for c in range(2):
                            wait_apart(act, s_fi, n * 4 + c + 3)
                            b = (2 + c) % 3
                            nc.scalar.activation(chunk(ti, n, c), p_f[0:C2, b:b + 1, :], ACT.Tanh,
                                                 bias=bg[:, 2 + c:3 + c], scale=0.5).then_inc(s_ti, 1)
                        for c in range(2):
                            wait_apart(act, s_tf, 2 * n + c + 1)
                            nc.scalar.activation(chunk(al, n, c), tf[:, c:c + 1, :], ACT.Exp, bias=kf[:, c:c + 1],
                                                 scale=kf[:, c:c + 1]).then_inc(s_al, 1)
                        wait_apart(act, s_al, 2 * n + 2)
                        nc.scalar.activation(sq[:], both(al, n), ACT.Square).then_inc(s_a2, 1)
                        act.wait_ge(s_u, 2 * n + 1)
                        act.wait_ge(s_a2, n + 1)
                        nc.scalar.activation(be[:], sq[:], ACT.Sqrt, bias=one_eps[:, 0:1],
                                             scale=-0.25).then_inc(s_be, 1)

                    def store(n):
                        wait_apart(act, s_y, n + 2)
                        nc.scalar.activation(yT[:, tile_cols(n)], p_y[:], ACT.Copy).then_inc(s_yc, 1)

                    def turn(n, before=True, after=2):
                        gates(n)
                        if before:
                            store(n - 1)
                        if after == 2:
                            conv_input(n + 2)
                        if after >= 1:
                            gelu(n + 1)

                    conv_input(0)
                    gelu(0)
                    conv_input(1)
                    turn(0, before=False)
                    with act.Fori(1, N - 2) as n:
                        turn(n)
                    turn(N - 2, after=1)
                    turn(N - 1, after=0)
                    store(N - 1)

                @block.vector
                def _(dve):
                    def convolve(n):
                        dve.wait_ge(s_xp, n + 1)
                        for k in range(TAPS):
                            for c in range(2):
                                tap = xp[:, bass.ds((n % 2) * 2 + c, 1), pad - k:pad - k + T]
                                w = cw[:, c, TAPS - 1 - k:TAPS - k]
                                steps = [cv[:, c:c + 1, :], chunk(xb, n, c)]
                                if k == 0:
                                    nc.vector.tensor_scalar(steps[0], tap, w, cb[:, c:c + 1], ALU.mult,
                                                            ALU.add).then_inc(s_xb, 1)
                                else:
                                    dve.wait_ge(s_xb, n * (2 * TAPS) + 2 * (k - 1) + c + 1)
                                    nc.vector.scalar_tensor_tensor(out=steps[k % 2], in0=tap, scalar=w,
                                                                   in1=steps[1 - k % 2], op0=ALU.mult,
                                                                   op1=ALU.add).then_inc(s_xb, 1)
                        dve.wait_ge(s_xb, n * (2 * TAPS) + 2 * TAPS)

                    def split(n):
                        nc.vector.tensor_scalar(xb_hi[:], both(xb, n), 1.0, None, ALU.mult).then_inc(s_xh, 1)
                        dve.wait_ge(s_xh, n + 1)
                        nc.vector.tensor_tensor(xb_lo[:], both(xb, n), raw(xb_hi[:]), ALU.subtract).then_inc(s_xl, 1)

                    def scan(n):
                        dve.wait_ge(s_ti, 2 * n + 3)
                        nc.vector.scalar_tensor_tensor(out=xs[:], in0=both(ti, n), scalar=1.0, in1=both(xb, n),
                                                       op0=ALU.add, op1=ALU.mult).then_inc(s_u, 1)
                        dve.wait_ge(s_u, 2 * n + 2)
                        dve.wait_ge(s_be, n + 1)
                        nc.vector.tensor_tensor(xs[:], xs[:], be[:], ALU.mult).then_inc(s_u, 1)
                        dve.wait_ge(s_u, 2 * n + 3)
                        for c in range(2):
                            nc.vector.tensor_tensor_scan(hs[:, c, :], al[:, bass.ds((n % 2) * 2 + c, 1), :].rearrange(
                                "p a t -> p (a t)"), xs[:, c, :], 0.0, ALU.mult, ALU.add).then_inc(s_h, 1)
                        dve.wait_ge(s_h, 2 * n + 2)
                        dve.wait_ge(s_gl, n + 1)
                        dve.wait_ge(s_y, n + 1)
                        nc.vector.tensor_tensor(z[:], both(gl, n), hs[:], ALU.mult).then_inc(s_z, 1)

                    dve.sem_inc(s_u, 1)
                    convolve(0)
                    split(0)
                    with dve.Fori(0, N - 1) as n:
                        convolve(n + 1)
                        dve.wait_ge(s_fi, n * 4 + 4)
                        split(n + 1)
                        scan(n)
                    scan(N - 1)
        scope.pop()

        def experts(tag, E, up_hi, up_lo, bias_up, lin_hi, lin_lo, bias_lin, dn_hi, dn_lo, b2_hi, b2_lo, act_fn,
                    store, hg):
            gated = lin_hi is not None
            LAG = 3
            BUFS = 4
            scope.append(ExitStack())
            with scope[-1]:
                if hg is None:
                    hg = sb(tag + "hg", [P, 2, 2, 2, T])
                h, g = hg[:, 0], hg[:, 1]
                g_hi = sb(tag + "g_hi", [P, BUFS, 2, T], F32R)
                g_lo = sb(tag + "g_lo", [P, BUFS, 2, T], F32R)
                ys = sb(tag + "ys", [P, T])
                rows_in = sb(tag + "rows", [P, 2, T])
                gb = sb(tag + "gb", [P, 2, T])
                p_up = ps(tag + "p_up", [P, 2, 2, T]) if not gated else ps(tag + "p_up", [P, 1, 2, T])
                p_lin = ps(tag + "p_lin", [P, 1, 2, T]) if gated else None
                p_row = ps(tag + "p_row", [P, T])
                p_acc = ps(tag + "p_acc", [P, 2, T])
                p_tr = ps(tag + "p_tr", [P, T])
                B = 1 if gated else 2
                s_up = sem(tag + "up_done")
                s_h = sem(tag + "activated")
                if gated:
                    s_lin = sem(tag + "linear_done")
                    s_hg = sem(tag + "half_gated")
                STEPS = 2 if gated else 1
                s_g = sem(tag + "gated")
                s_hi = sem(tag + "gated_high")
                s_lo = sem(tag + "gated_low")
                s_row = sem(tag + "rows_made")
                s_rs = sem(tag + "rows_stored")
                s_gb = sem(tag + "gate_broadcast")
                s_go = sem(tag + "broadcast_started")
                s_dn = sem(tag + "down_done")
                s_ys = sem(tag + "tile_sum")
                s_tr = sem(tag + "tile_transposed")
                s_xr = sem(tag + "residual_added")
                if store:
                    s_out = sem(tag + "stored")

                GROUPS = E // ROWS

                def acc(n):
                    return p_acc[:, bass.ds(n % 2, 1), :].rearrange("p a t -> p (a t)")

                def next_group(n, e, end):
                    if e // ROWS + 1 < GROUPS:
                        return n, e // ROWS + 1
                    return None if end else (n + 1, 0)

                with nc.Block() as block:
                    @block.tensor
                    def _(pe):
                        pe.sem_inc(s_dn, BUFS)

                        def rows(n, group):
                            pe.wait_ge(s_rs, n * GROUPS + group + 1)
                            nc.tensor.matmul(p_row[:], sel[:, group, :], gT[:, tile_cols(n)],
                                             start=True, stop=True).then_inc(s_row, 1)

                        def up(n, e, end=False):
                            q = n * E + e
                            x_h, x_l = x_hi[:, tile_cols(n)], x_lo[:, tile_cols(n)]
                            if e % ROWS == 1 and next_group(n, e, end) is not None:
                                rows(*next_group(n, e, end))
                            pe.wait_ge(s_h, q + 1)
                            for c in range(2):
                                last = mm3(p_up[:, e % B, c, :], up_hi[:, e, c, :], up_lo[:, e, c, :], x_h, x_l)
                            last.then_inc(s_up, 1)
                            if gated:
                                for c in range(2):
                                    pe.wait_ge(s_g, 2 * q + c + 3)
                                    mm3(p_lin[:, 0, c, :], lin_hi[:, e, c, :], lin_lo[:, e, c, :], x_h,
                                        x_l).then_inc(s_lin, 1)

                        def down(n, e):
                            pe.wait_ge(s_lo, n * E + e + 3)
                            if e == 0:
                                pe.wait_ge(s_ys, n + 1)
                                for k, b in enumerate((b2_hi, b2_lo)):
                                    nc.tensor.matmul(acc(n), b[:], gT[:, tile_cols(n)],
                                                     start=k == 0, stop=False)
                            for c in range(2):
                                last = mm3(acc(n), dn_hi[:, e, c, :], dn_lo[:, e, c, :], g_hi[:, e % BUFS, c, :],
                                           g_lo[:, e % BUFS, c, :], start=False, stop=(e == E - 1 and c == 1))
                            last.then_inc(s_dn, 1)

                        def turn_back(n):
                            pe.wait_ge(s_ys, n + 3)
                            pe.wait_ge(s_xr, n + 1)
                            for j in range(J):
                                last = nc.tensor.transpose(p_tr[:, j * P:(j + 1) * P], ys[:, j * P:(j + 1) * P],
                                                           ident[:])
                            last.then_inc(s_tr, 1)

                        def tile(n, first, last):
                            if first:
                                rows(n, 0)
                                for e in range(LAG):
                                    up(n, e)
                            for k in range(LAG, E + LAG):
                                if k < E:
                                    up(n, k, end=last)
                                elif not last:
                                    up(n + 1, k - E)
                                if k == 6 and not first:
                                    turn_back(n - 1)
                                down(n, k - LAG)
                            if last:
                                turn_back(n)

                        tile(0, True, False)
                        with pe.Fori(1, N - 1) as n:
                            tile(n, False, False)
                        tile(N - 1, False, True)

                    @block.scalar
                    def _(act):
                        act.sem_inc(s_h, B)

                        def store_rows(n, group):
                            wait_apart(act, s_row, n * GROUPS + group + 1)
                            act.wait_ge(s_gb, (n * GROUPS + group) * ROWS + 1)
                            nc.scalar.activation(rows_in[:, group % 2, :], p_row[:], ACT.Copy).then_inc(s_rs, 1)

                        def activate(n, e, end=False):
                            q = n * E + e
                            act.wait_ge(s_up, q + 1)
                            act.wait_ge(s_g, STEPS * (q + 1))
                            for c in range(2):
                                last = nc.scalar.activation(h[:, e % 2, c, :], p_up[:, e % B, c, :], act_fn,
                                                            bias=bias_up[:, e, c:c + 1])
                            last.then_inc(s_h, 1)
                            if e % ROWS == 1 and next_group(n, e, end) is not None:
                                store_rows(*next_group(n, e, end))

                        def high(n, e):
                            q = n * E + e
                            act.wait_ge(s_g, STEPS * (q + 3))
                            act.wait_ge(s_dn, q + 1)
                            nc.scalar.activation(g_hi[:, e % BUFS, :, :], g[:, e % 2, :, :], ACT.Copy).then_inc(s_hi, 1)

                        def tile(n, first, last):
                            if first:
                                store_rows(n, 0)
                                activate(n, 0)
                            for k in range(1, E + 1):
                                if k < E:
                                    activate(n, k, end=last)
                                elif not last:
                                    activate(n + 1, 0)
                                high(n, k - 1)

                        tile(0, True, False)
                        with act.Fori(1, N - 1) as n:
                            tile(n, False, False)
                        tile(N - 1, False, True)

                    @block.vector
                    def _(dve):
                        dve.sem_inc(s_g, 2 * STEPS)
                        if gated:
                            dve.sem_inc(s_hg, 2)
                        dve.sem_inc(s_lo, 2)
                        dve.sem_inc(s_ys, 2)
                        dve.sem_inc(s_xr, 1)

                        def gate(n, e):
                            q = n * E + e
                            dve.wait_ge(s_gb, q + ROWS + 2)
                            dve.wait_ge(s_h, q + B + 1)
                            dve.wait_ge(s_lo, q + 1)
                            if not gated:
                                nc.vector.tensor_tensor(g[:, e % 2, :, :], h[:, e % 2, :, :],
                                                        gb[:, e % 2, :].unsqueeze(1).broadcast_to([P, 2, T]),
                                                        ALU.mult).then_inc(s_g, 1)
                            else:
                                nc.vector.tensor_tensor(h[:, e % 2, :, :], h[:, e % 2, :, :],
                                                        gb[:, e % 2, :].unsqueeze(1).broadcast_to([P, 2, T]),
                                                        ALU.mult).then_inc(s_hg, 1)
                                dve.wait_ge(s_hg, q + 3)
                                for c in range(2):
                                    dve.wait_ge(s_lin, 2 * q + c + 1)
                                    nc.vector.scalar_tensor_tensor(
                                        out=g[:, e % 2, c, :], in0=p_lin[:, 0, c, :], scalar=bias_lin[:, e, c:c + 1],
                                        in1=h[:, e % 2, c, :], op0=ALU.add, op1=ALU.mult).then_inc(s_g, 1)

                        def low(n, e):
                            q = n * E + e
                            dve.wait_ge(s_hi, q + 1)
                            dve.wait_ge(s_dn, q + 1)
                            nc.vector.tensor_tensor(g_lo[:, e % BUFS, :, :], g[:, e % 2, :, :],
                                                    raw(g_hi[:, e % BUFS, :, :]),
                                                    ALU.subtract).then_inc(s_lo, 1)

                        def statistics(n):
                            dve.wait_ge(s_xr, n + 2)
                            for j in range(J):
                                nc.vector.bn_stats(stats[:, bass.ds(n * J + j, 1), :].rearrange("p a s -> p (a s)"),
                                                   xres[:, bass.ds(n * J + j, 1), :].rearrange("p a d -> p (a d)"))

                        def tile_sum(n):
                            dve.wait_ge(s_dn, n * E + E + BUFS)
                            dve.wait_ge(s_xr, n + 1)
                            nc.vector.tensor_tensor(ys[:], acc(n), yT[:, tile_cols(n)], ALU.add).then_inc(s_ys, 1)

                        def residual(n):
                            dve.wait_ge(s_tr, n + 1)
                            rows = xres[:, bass.ds(n * J, J), :]
                            nc.vector.tensor_tensor(rows, p_tr[:].rearrange("p (j d) -> p j d", j=J), rows,
                                                    ALU.add).then_inc(s_xr, 1)

                        def tile(n, first, last):
                            if first:
                                gate(n, 0)
                            for k in range(1, E + 1):
                                if k < E:
                                    gate(n, k)
                                elif not last:
                                    gate(n + 1, 0)
                                low(n, k - 1)
                                if not first and k == 4:
                                    tile_sum(n - 1)
                                if not first and k == 6:
                                    residual(n - 1)
                                if not first and k == 7 and not store:
                                    statistics(n - 1)
                            if last:
                                tile_sum(n)
                                residual(n)
                                if not store:
                                    statistics(n)

                        tile(0, True, False)
                        with dve.Fori(1, N - 1) as n:
                            tile(n, False, False)
                        tile(N - 1, False, True)

                    @block.gpsimd
                    def _(pool):
                        pool.sem_inc(s_rs, 1)
                        pool.sem_inc(s_gb, ROWS + 1)

                        def spread(n, e):
                            q = n * E + e
                            pool.wait_ge(s_rs, n * GROUPS + e // ROWS + 2)
                            gate_read = s_g if not gated else s_hg
                            pool.wait_ge(gate_read, q + 1)
                            pool.sem_inc(s_go, 1)
                            row = 32 * (e % ROWS)
                            pool.partition_broadcast(gb[:, e % 2, :], rows_in[row:row + 1, (e // ROWS) % 2, :],
                                                     channels=P).then_inc(s_gb, 1)

                        with pool.Fori(0, N) as n:
                            for e in range(E):
                                spread(n, e)

                    if store:
                        @block.sync
                        def _(sp):
                            with sp.Fori(0, N) as n:
                                sp.wait_ge(s_xr, n + 2)
                                sp.dma_start(out[bass.ds(n, 1)].rearrange("a (j p) d -> p (a j) d", p=P),
                                             xres[:, bass.ds(n * J, J), :]).then_inc(s_out, 16)
                            sp.wait_ge(s_out, 16 * N)
            scope.pop()

        scope.append(ExitStack())
        with scope[-1]:
            w1_hi = sb("w1_hi", [P, E0, 2, P], F32R)
            w1_lo = sb("w1_lo", [P, E0, 2, P], F32R)
            w2_hi = sb("w2_hi", [P, E0, 2, P], F32R)
            w2_lo = sb("w2_lo", [P, E0, 2, P], F32R)
            b1T = sb("b1T", [P, E0, 2])
            b2_hi = sb("b2_hi", [P, D], F32R)
            b2_lo = sb("b2_lo", [P, D], F32R)
            scope.append(ExitStack())
            with scope[-1]:
                w2_raw = sb("w2_raw", [P, E0, 2, P])
                p_b1 = ps("p_b1", [P, 2 * E0])
                GROUP = E0 // 4
                s_w2 = [sem(f"e0_w2_loaded_{k}") for k in range(4)]
                s_ewh = sem("e0_high")
                s_ewl = sem("e0_low")
                s_b1t = sem("e0_bias_transposed")

                def group(k):
                    return slice(k * GROUP, (k + 1) * GROUP)

                parts = [(w1_hi[:, group(k)], w1_lo[:, group(k)],
                          w1_raw[:, group(k), :].rearrange("p e (c m) -> p e c m", c=2), (s_w1, 16)) for k in range(4)]
                parts += [(b2_hi[:], b2_lo[:], b2_raw[:], (s_eb, 3 * 16))]
                parts += [(w2_hi[:, group(k)], w2_lo[:, group(k)], w2_raw[:, group(k)], (s_w2[k], 16))
                          for k in range(4)]
                with nc.Block() as block:
                    @block.sync
                    def _(sp):
                        for k in range(4):
                            sp.dma_start(w2_raw[:, group(k)],
                                         w2[group(k)].rearrange("e (c p) d -> p e c d", p=P)).then_inc(s_w2[k], 16)
                        for k in range(4):
                            sp.wait_ge(s_w2[k], 16)

                    @block.tensor
                    def _(pe):
                        pe.wait_ge(s_eb, 3 * 16)
                        nc.tensor.transpose(p_b1[:], b1_raw[:], ident[0:2 * E0, 0:2 * E0]).then_inc(s_b1t, 1)

                    @block.scalar
                    def _(act):
                        for hi, lo, src, (loaded, count) in parts:
                            act.wait_ge(loaded, count)
                            nc.scalar.activation(hi, src, ACT.Copy).then_inc(s_ewh, 1)

                    @block.vector
                    def _(dve):
                        for k, (hi, lo, src, (loaded, count)) in enumerate(parts):
                            dve.wait_ge(s_ewh, k + 1)
                            nc.vector.tensor_tensor(lo, src, raw(hi), ALU.subtract).then_inc(s_ewl, 1)
                        dve.wait_ge(s_b1t, 1)
                        nc.vector.tensor_copy(b1T[:].rearrange("p e c -> p (e c)"), p_b1[:]).then_inc(s_ewl, 1)
            scope.pop()
            experts("e0_", E0, w1_hi, w1_lo, b1T, None, None, None, w2_hi, w2_lo, b2_hi, b2_lo, ACT.Gelu, False, hg)
        scope.pop()
        scope.pop().close()

        layer1 = ExitStack()
        root.enter_context(layer1)
        scope.append(layer1)
        router1 = Router("b_", E1, K1)
        scope.append(ExitStack())
        with scope[-1]:
            bp_col = sb("bp_col", [D, 1])
            wq_hi = sb("wq_hi", [D, NQ // 2, P], F32R)
            wq_lo = sb("wq_lo", [D, NQ // 2, P], F32R)
            wk_hi = sb("wk_hi", [D, P], F32R)
            wk_lo = sb("wk_lo", [D, P], F32R)
            wv_hi = sb("wv_hi", [D, P], F32R)
            wv_lo = sb("wv_lo", [D, P], F32R)
            wp_hi = sb("wp_hi", [D, P], F32R)
            wp_lo = sb("wp_lo", [D, P], F32R)
            q_m = sb("q_m", [P, 1])
            k_m = sb("k_m", [P, 1])
            k_one = sb("k_one", [P, 1])
            idb = sb("idb", [P, P], BF16)
            mask_t = sb("mask_t", [P, P], BF16)
            place = sb("place", [P, NQ // 2, P], F32R)
            kz = sb("kz", [P, 2, 2, T], F32R)
            va = sb("va", [P, 2, NQ, J, P])
            mx2 = sb("mx2", [P, J, P])
            scope.append(ExitStack())
            wq_raw = sb("wq_raw", [D, NQ, DH])
            wk_raw = sb("wk_raw", [D, DH])
            wv_raw = sb("wv_raw", [D, DH])
            wp_raw = sb("wp_raw", [NQ * DH, D])
            wq_rep = sb("wq_rep", [D, NQ // 2, 2, 4, DH])
            wk_rep = sb("wk_rep", [D, 8, DH])
            wv_rep = sb("wv_rep", [D, 8, DH])
            part = sb("part", [P, 1], I32)
            bit = sb("bit", [P, 3], I32)
            place_f = sb("place_f", [P, NQ // 2, P])

            s_tw = sem("t_loaded")
            s_rep = sem("t_replicated")
            s_th = sem("t_high")
            s_tl = sem("t_low")
            s_io = sem("t_iota")
            s_pm = sem("t_mask_zero")
            s_pm2 = sem("t_masks_made")
            s_bits = sem("t_bits")
            wparts = [(wq_hi[:].rearrange("p a b -> p (a b)"), wq_lo[:].rearrange("p a b -> p (a b)"),
                       wq_rep[:].rearrange("p a b c d -> p (a b c d)")),
                      (wk_hi[:], wk_lo[:], wk_rep[:].rearrange("p a b -> p (a b)")),
                      (wv_hi[:], wv_lo[:], wv_rep[:].rearrange("p a b -> p (a b)")),
                      (wp_hi[:], wp_lo[:], wp_raw[:])]
            def attention_sync(sp):
                sp.dma_start(wq_raw[:], Wq.rearrange("q c d -> c q d")).then_inc(s_tw, 16)
                sp.dma_start(wk_raw[:], Wk).then_inc(s_tw, 16)
                sp.dma_start(wv_raw[:], Wv).then_inc(s_tw, 16)
                sp.dma_start(wp_raw[:], Wp).then_inc(s_tw, 16)
                with nc.allow_non_contiguous_dma(reason="128 bias values"):
                    sp.dma_start(bp_col[:], bp.rearrange("(p a) -> p a", a=1)).then_inc(s_tw, 16)
                sp.wait_ge(s_tw, 5 * 16)

            def attention_pool(pool):
                pool.iota(part[:], pattern=[[0, 1]], base=0, channel_multiplier=1).then_inc(s_io, 1)
                pool.memset(idb[:], 0.0).then_inc(s_pm, 1)
                pool.memset(mask_t[:], 0.0).then_inc(s_pm, 1)
                pool.memset(place_f[:], 0.0).then_inc(s_pm, 1)
                pool.wait_ge(s_pm, 3)
                pool.affine_select(out=idb[:], in_=idb[:], compare_op=ALU.not_equal, fill=1.0, base=0,
                                   pattern=[[-1, P]], channel_multiplier=1).then_inc(s_pm2, 1)
                pool.affine_select(out=mask_t[:], in_=mask_t[:], compare_op=ALU.is_ge, fill=MASKED, base=0,
                                   pattern=[[-1, P]], channel_multiplier=1).then_inc(s_pm2, 1)
                for head in range(2):
                    for part_ in range(2):
                        row = 64 * head + 3 * DH + part_
                        pool.affine_select(out=place_f[:, :, row], in_=place_f[:, :, row],
                                           compare_op=ALU.not_equal, fill=-1.0, base=-(head + NQ * part_),
                                           pattern=[[-2, NQ // 2]],
                                           channel_multiplier=1).then_inc(s_pm2, 1)
                pool.wait_ge(s_pm2, 6)
                pool.tensor_copy(place[:], place_f[:]).then_inc(s_pm2, 1)
                pool.memset(raw(kz[:]), 0.0)
                pool.memset(mx2[:], 0.0)
                pool.memset(va[:], 0.0).then_inc(s_pm, 1)
                pool.wait_ge(s_pm, 4)
                for hd in range(NQ):
                    one = (64 if hd < 4 else 0) + DH * (hd % 4)
                    pool.memset(va[:, :, hd, :, one:one + DH], 1.0)

            def attention_vector(dve, p_aside, p_g):
                dve.wait_ge(s_tw, 5 * 16)
                nc.vector.memset(wq_rep[:], 0.0).then_inc(s_rep, 1)
                nc.vector.memset(wk_rep[:], 0.0).then_inc(s_rep, 1)
                dve.wait_ge(s_rep, 2)
                nc.vector.tensor_copy(wq_rep[:].rearrange("p a b c d -> p (a b) c d")[:, :, 0:3, :],
                                      wq_raw[:].unsqueeze(2).broadcast_to([D, NQ, 3, DH])).then_inc(s_rep, 1)
                for half in range(2):
                    nc.vector.tensor_copy(wk_rep[:, 4 * half:4 * half + 3, :],
                                          wk_raw[:].unsqueeze(1).broadcast_to([D, 3, DH])).then_inc(s_rep, 1)
                nc.vector.tensor_copy(wv_rep[:], wv_raw[:].unsqueeze(1).broadcast_to([D, 8, DH])).then_inc(s_rep, 1)
                dve.wait_ge(s_io, 1)
                nc.vector.tensor_scalar(bit[:, 0:1], part[:], 4, 1, ALU.logical_shift_right,
                                        ALU.bitwise_and).then_inc(s_bits, 1)
                nc.vector.tensor_scalar(bit[:, 1:2], part[:], 5, 1, ALU.logical_shift_right,
                                        ALU.bitwise_and).then_inc(s_bits, 1)
                nc.vector.tensor_scalar(bit[:, 2:3], part[:], 1, 31, ALU.logical_shift_right,
                                        ALU.bitwise_and).then_inc(s_bits, 1)
                dve.wait_ge(s_bits, 3)
                nc.vector.tensor_scalar(q_m[:], bit[:, 0:1], -1.0, None, ALU.mult).then_inc(s_bits, 1)
                nc.vector.tensor_scalar(k_one[:], bit[:, 2:3], 3 * DH // 2, None, ALU.is_equal).then_inc(s_bits, 1)
                nc.vector.tensor_scalar(k_m[:], bit[:, 1:2], -1.0, None, ALU.mult).then_inc(s_bits, 1)
                dve.wait_ge(s_bits, 6)
                nc.vector.scalar_tensor_tensor(out=k_m[:], in0=k_one[:], scalar=2.0, in1=k_m[:],
                                               op0=ALU.mult, op1=ALU.add).then_inc(s_bits, 1)
                for k, (hi, lo, src) in enumerate(wparts):
                    dve.wait_ge(s_th, k + 1)
                    nc.vector.tensor_tensor(lo, src, raw(hi), ALU.subtract).then_inc(s_tl, 1)

            def attention_scalar(act, p_aside, p_g):
                act.wait_ge(s_rep, 6)
                act.wait_ge(s_tw, 5 * 16)
                for hi, lo, src in wparts:
                    nc.scalar.activation(hi, src, ACT.Copy).then_inc(s_th, 1)

            normalise_stream("b_", router1, False, Wg, True, None, False,
                             {"sync": attention_sync, "gpsimd": attention_pool, "vector": attention_vector,
                              "scalar": attention_scalar})
            scope.pop().close()

            qs = sb("qs", [P, 2, NQ // 2, T], F32R)
            ktmp = sb("ktmp", [P, T], F32R)
            qtmp = sb("qtmp", [P, T], F32R)
            vT = sb("vT", [P, T])
            mxs = sb("mxs", [P, J, NQ])
            mx_hi = sb("mx_hi", [P, J, NQ], F32R)
            mT = sb("mT", [P, 2, T], F32R)
            ex = sb("ex", [P, 2, 3 * T])
            ob = sb("ob", [P, T])
            ob_den = sb("ob_den", [P, T])
            rd = sb("rd", [P, T])
            at = sb("at", [P, T])
            at_hi = sb("at_hi", [P, T], F32R)
            at_lo = sb("at_lo", [P, T], F32R)
            p_a = ps("p_a", [P, T])
            p_s = ps("p_s", [P, 3 * T])
            p_st = ps("p_st", [P, 3 * T])
            p_o = ps("p_o", [P, T])

            COL = {0: 0, 1: T, 3: T + 3 * P, 2: 2 * T}
            CMAX = {3: 0, 2: T, 0: 2 * T, 1: 2 * T + P}
            WID = {b: T - P * b for b in range(J)}

            FRONT0 = ["k", "q0", "q1", "q2", "q3", "v", "vt", "m"]
            FRONT = ["k", "q0", "q1", "q2", "q3", "v", "vt", "o", "m"]

            def use(n, what):
                if isinstance(n, int) and n < 1:
                    return (n + 1) * len(FRONT0) + FRONT0.index(what)
                base = len(FRONT) * n + (2 * len(FRONT0) - len(FRONT))
                if isinstance(n, int) and n == N - 1:
                    return base + {"o": 0, "last": 1}[what]
                return base + FRONT.index(what)

            s_pa = sem("t_projected")
            s_pad = sem("t_projection_used")
            s_pah = sem("t_projection_high")
            s_sc = sem("t_scores")
            s_mx = sem("t_maxima")
            s_m1 = sem("t_maxima_high")
            s_m2 = sem("t_maxima_split")
            s_ss = sem("t_shifted_scores")
            s_pl = sem("t_maxima_placed")
            s_qm = sem("t_queries_shifted")
            s_cut = sem("t_future_cut")
            s_go = sem("t_cut_started")
            s_ex = sem("t_exp")
            s_pv = sem("t_values_summed")
            s_po = sem("t_sums_copied")
            s_rd = sem("t_reciprocal")
            s_at = sem("t_normalised")
            s_ah = sem("t_out_high")
            s_all = sem("t_out_low")
            HALF = NQ // 2
            with nc.Block() as block:
                @block.gpsimd
                def _(pool):
                    def cut_future(n, hd):
                        pool.wait_ge(s_ex, n * NQ + hd + 2)
                        pool.sem_inc(s_go, 1)
                        first = ex[:, hd % 2, :].rearrange("p (b t) -> p b t", b=3)[:, :, 0:P]
                        pool.affine_select(out=first, in_=first, compare_op=ALU.is_ge, fill=0.0, base=0,
                                           pattern=[[0, 3], [1, P]], channel_multiplier=-1)
                        other = ex[:, hd % 2, COL[3]:COL[3] + P]
                        pool.affine_select(out=other, in_=other, compare_op=ALU.is_ge, fill=0.0, base=0,
                                           pattern=[[1, P]], channel_multiplier=-1).then_inc(s_cut, 1)

                    with pool.Fori(0, N) as n:
                        for hd in range(NQ):
                            cut_future(n, hd)

                @block.tensor
                def _(pe):
                    pe.sem_inc(s_pv, 2)

                    def claim(u):
                        pe.wait_ge(s_pad, u + 1)

                    def project(n, f, what):
                        claim(use(n, what))
                        w_hi_, w_lo_ = {"k": (wk_hi[:], wk_lo[:]), "v": (wv_hi[:], wv_lo[:])}.get(what) or \
                            (wq_hi[:, int(what[1]), :], wq_lo[:, int(what[1]), :])
                        mm3(p_a[:], w_hi_, w_lo_, x_hi[:, tile_cols(f)], x_lo[:, tile_cols(f)]).then_inc(s_pa, 1)

                    def turn_values(n):
                        claim(use(n, "vt"))
                        for j in range(J):
                            last = nc.tensor.transpose(p_a[:, j * P:(j + 1) * P], vT[:, j * P:(j + 1) * P], ident[:])
                        last.then_inc(s_pa, 1)

                    def scores(n, f, fp, hd, p_s=p_s, buffers=1):
                        if buffers == 1 or hd >= 2:
                            pe.wait_ge(s_mx, f * NQ + hd + 2 - buffers)
                        if hd == 0:
                            wait_placed(n)
                        if hd % 2 == 0:
                            pe.wait_ge(s_pad, use(n, f"q{hd // 2}") + 2)
                        for b in (3, 2, 0, 1):
                            w = (b + 1) * P
                            wide = max(w, 2 * P)
                            nc.tensor.matmul(p_s[:, CMAX[b]:CMAX[b] + wide], qs[:, fp, hd // 2, b * P:(b + 1) * P],
                                             kz[:, fp, hd % 2, 0:wide], start=True, stop=False)
                            last = nc.tensor.matmul(p_s[:, CMAX[b] + b * P:CMAX[b] + w], idb[:], mask_t[:],
                                                    start=False, stop=True)
                        last.then_inc(s_sc, 1)

                    def turn_maxima(n, f):
                        claim(use(n, "m"))
                        pe.wait_ge(s_m2, f * 2 + 2)
                        for j in range(J):
                            last = nc.tensor.transpose(p_a[:, j * P:(j + 1) * P], mx2[:, j, :], ident[:])
                        last.then_inc(s_pa, 1)

                    def place_maxima(n, f, fp):
                        pe.wait_ge(s_pad, use(n, "m") + 2)
                        pe.wait_ge(s_mx, f * NQ + NQ + 1)
                        for pair in range(HALF):
                            if pair == 3:
                                pe.wait_ge(s_qm, f * HALF + 1)
                            bank = (pair % 3) * T
                            nc.tensor.matmul(p_s[:, bank:bank + T], place[:, pair, :], mT[:, fp, :],
                                             start=True, stop=True).then_inc(s_pl, 1)

                    def wait_placed(f):
                        if not (isinstance(f, int) and f < 0):
                            pe.wait_ge(s_qm, f * HALF + HALF)

                    def shifted(n, par, hd):
                        pe.wait_ge(s_ex, n * NQ + hd + 1)
                        if hd % 2 == 0:
                            pe.wait_ge(s_qm, n * HALF + hd // 2 + 1)
                        for b in (0, 3, 1, 2):
                            wide = max(WID[b], 2 * P)
                            end = COL[b] + WID[b]
                            last = nc.tensor.matmul(p_st[:, end - wide:end], kz[:, par, hd % 2, b * P:(b + 1) * P],
                                                    qs[:, par, hd // 2, T - wide:T], start=True, stop=True)
                        last.then_inc(s_ss, 1)

                    def weigh(n, par, hd):
                        pe.wait_ge(s_cut, n * NQ + hd + 1)
                        if hd % HALF == 0:
                            pe.wait_ge(s_po, 2 * n + hd // HALF + 1)
                        for b in range(J):
                            last = nc.tensor.matmul(p_o[:, b * P:T], va[:, par, hd, b, :],
                                                    ex[:, hd % 2, COL[b]:COL[b] + WID[b]],
                                                    start=(hd % HALF == 0 and b == 0),
                                                    stop=(hd % HALF == HALF - 1 and b == J - 1))
                        last.then_inc(s_pv, 1)

                    def output(n, m, what):
                        claim(use(n, what))
                        pe.wait_ge(s_all, m + 1)
                        mm3(p_a[:], wp_hi[:], wp_lo[:], at_hi[:], at_lo[:]).then_inc(s_pa, 1)

                    def turn(n, par, front=True, before=True):
                        f, fp = n + 1, 1 - par
                        for hd in range(NQ):
                            shifted(n, par, hd)
                            if front:
                                if hd == 0:
                                    project(n, f, "k")
                                elif hd in (2, 3, 4):
                                    project(n, f, ("q2", "q3", "v")[hd - 2])
                                    scores(n, f, fp, 2 * hd - 3)
                                elif hd == 5:
                                    turn_values(n)
                                    scores(n, f, fp, 7)
                                elif hd == 7:
                                    place_maxima(n, f, fp)
                            if hd > 0:
                                weigh(n, par, hd - 1)
                            elif before:
                                weigh(n - 1, 1 - par, NQ - 1)
                            if front:
                                if hd <= 1:
                                    project(n, f, f"q{hd}")
                                if 1 <= hd <= 4:
                                    scores(n, f, fp, 2 * hd - 2)
                            if hd == 5 and before:
                                output(n, n - 1, "o")
                            if front and hd == 6:
                                turn_maxima(n, f)

                    for hd in range(NQ):
                        if hd % 2 == 0:
                            if hd == 0:
                                project(-1, 0, "k")
                            project(-1, 0, f"q{hd // 2}")
                        scores(-1, 0, 0, hd, (p_s, p_st)[hd % 2], buffers=2)
                    project(-1, 0, "v")
                    turn_values(-1)
                    turn_maxima(-1, 0)
                    place_maxima(-1, 0, 0)
                    turn(0, 0, before=False)
                    with pe.Fori(0, (N - 2) // 2) as m:
                        for par in (1, 0):
                            n = m * 2 + (2 - par)
                            turn(n, par)
                    turn(N - 1, 1, front=False)
                    weigh(N - 1, 1, NQ - 1)
                    output(N - 1, N - 1, "last")

                @block.scalar
                def _(act):
                    act.sem_inc(s_ex, 1)
                    act.sem_inc(s_po, 1)

                    def high(n, what):
                        act.wait_ge(s_pa, use(n, what) + 1)
                        if what == "k":
                            nc.scalar.activation(ktmp[:], p_a[:], ACT.Identity, bias=k_one[:]).then_inc(s_pah, 1)
                        else:
                            nc.scalar.activation(qtmp[:], p_a[:], ACT.Copy).then_inc(s_pah, 1)

                    def copy(n, what, dst):
                        act.wait_ge(s_pa, use(n, what) + 1)
                        nc.scalar.activation(dst, p_a[:], ACT.Copy).then_inc(s_pad, 1)

                    def exp(n, hd):
                        act.wait_ge(s_ss, n * NQ + hd + 1)
                        act.wait_ge(s_pv, n * NQ + hd + 1)
                        nc.scalar.activation(ex[:, hd % 2, 0:1280], p_st[:, 0:1280], ACT.Exp, scale=SCALE).then_inc(s_ex, 1)

                    def sums(n, half):
                        num = slice(64 * half, 64 * half + 64)
                        den = slice(64 - 64 * half, 128 - 64 * half)
                        act.wait_ge(s_pv, n * NQ + HALF * (half + 1) + 2)
                        act.wait_ge(s_at, n + 1)
                        nc.scalar.activation(ob[num, :], p_o[num, :], ACT.Copy)
                        nc.scalar.activation(ob_den[num, :], p_o[den, :], ACT.Copy).then_inc(s_po, 1)

                    def store(n, m, what):
                        wait_apart(act, s_pa, use(n, what) + 1)
                        nc.scalar.activation(yT[:, tile_cols(m)], p_a[:], ACT.Identity, bias=bp_col[:]).then_inc(s_pad, 1)

                    def turn(n, par, front=True, before=True):
                        fp = 1 - par
                        for hd in range(NQ):
                            exp(n, hd)
                            if front and hd == 0:
                                high(n, "k")
                            if hd == 0 and before:
                                sums(n - 1, 1)
                            if front and hd <= 3:
                                high(n, f"q{hd}")
                            if front and hd == 4:
                                copy(n, "v", vT[:])
                            if hd == HALF:
                                sums(n, 0)
                            if hd == 5 and before:
                                store(n, n - 1, "o")
                            if front and hd == 6:
                                copy(n, "m", mT[:, fp, :])
                            if hd == 3 and not front:
                                route_scalar(act, router1)

                    for what in FRONT0[:5]:
                        high(-1, what)
                    copy(-1, "v", vT[:])
                    copy(-1, "m", mT[:, 0, :])
                    turn(0, 0, before=False)
                    with act.Fori(0, (N - 2) // 2) as m:
                        for par in (1, 0):
                            turn(m * 2 + (2 - par), par)
                    turn(N - 1, 1, front=False)
                    sums(N - 1, 1)
                    store(N - 1, N - 1, "last")

                @block.vector
                def _(dve):
                    dve.sem_inc(s_pad, 1)
                    dve.sem_inc(s_mx, 1)
                    dve.sem_inc(s_at, 1)

                    def stack(n, f, fp, what):
                        dve.wait_ge(s_pah, f * (HALF + 1) + 1 + ["k", "q0", "q1", "q2", "q3"].index(what))
                        if what == "k":
                            for half in range(2):
                                r = slice(64 * half, 64 * half + 64)
                                last = nc.vector.scalar_tensor_tensor(
                                    out=kz[r, fp, half, :], in0=raw(ktmp[r, :]), scalar=k_m[r, :],
                                    in1=p_a[r, :], op0=ALU.mult, op1=ALU.add)
                        else:
                            last = nc.vector.scalar_tensor_tensor(out=qs[:, fp, int(what[1]), :], in0=raw(qtmp[:]),
                                                                  scalar=q_m[:], in1=p_a[:], op0=ALU.mult,
                                                                  op1=ALU.add)
                        last.then_inc(s_pad, 1)

                    def values(n, fp):
                        dve.wait_ge(s_pa, use(n, "vt") + 1)
                        for hd in range(NQ):
                            c0 = (0 if hd < HALF else 64) + DH * (hd % HALF)
                            last = nc.vector.tensor_copy(va[:, fp, hd, :, c0:c0 + DH],
                                                         p_a[:].rearrange("p (j c) -> p j c", j=J)[:, :, 0:DH])
                        last.then_inc(s_pad, 1)

                    def maxima(f, hd, p_s=p_s):
                        dve.wait_ge(s_sc, f * NQ + hd + 1)
                        for b in range(J):
                            last = nc.vector.tensor_reduce(out=mxs[:, b, hd:hd + 1],
                                                           in_=p_s[:, CMAX[b]:CMAX[b] + (b + 1) * P],
                                                           op=ALU.max, axis=AX.X)
                        last.then_inc(s_mx, 1)

                    def split_maxima(n, f):
                        dve.wait_ge(s_mx, f * NQ + NQ + 1)
                        nc.vector.tensor_copy(mx_hi[:], mxs[:]).then_inc(s_m1, 1)
                        dve.wait_ge(s_m1, f + 1)
                        nc.vector.tensor_copy(mx2[:, :, 0:NQ], raw(mx_hi[:])).then_inc(s_m2, 1)
                        nc.vector.tensor_tensor(mx2[:, :, NQ:2 * NQ], mxs[:], raw(mx_hi[:]), ALU.subtract).then_inc(s_m2, 1)

                    def shift_queries(f, fp):
                        for pair in range(HALF):
                            dve.wait_ge(s_pl, f * HALF + pair + 1)
                            bank = (pair % 3) * T
                            nc.vector.tensor_tensor(qs[:, fp, pair, :], raw(qs[:, fp, pair, :]),
                                                    p_s[:, bank:bank + T], ALU.add).then_inc(s_qm, 1)

                    def invert(n, half):
                        dve.wait_ge(s_po, 2 * n + 3)
                        cols = slice(half * T // 2, (half + 1) * T // 2)
                        nc.vector.reciprocal(rd[:, cols], ob_den[:, cols]).then_inc(s_rd, 1)

                    def normalise(n):
                        dve.wait_ge(s_rd, 2 * n + 2)
                        nc.vector.tensor_tensor(at[:], ob[:], rd[:], ALU.mult).then_inc(s_at, 1)

                    def split_out(n):
                        dve.wait_ge(s_at, n + 2)
                        nc.vector.tensor_copy(at_hi[:], at[:]).then_inc(s_ah, 1)
                        dve.wait_ge(s_ah, n + 1)
                        nc.vector.tensor_tensor(at_lo[:], at[:], raw(at_hi[:]), ALU.subtract).then_inc(s_all, 1)

                    def turn(n, par, before=True):
                        f, fp = n + 1, 1 - par
                        stack(n, f, fp, "k")
                        stack(n, f, fp, "q0")
                        if before:
                            invert(n - 1, 0)
                        stack(n, f, fp, "q1")
                        maxima(f, 0)
                        if before:
                            invert(n - 1, 1)
                        stack(n, f, fp, "q2")
                        maxima(f, 1)
                        if before:
                            normalise(n - 1)
                        maxima(f, 2)
                        stack(n, f, fp, "q3")
                        maxima(f, 3)
                        if before:
                            split_out(n - 1)
                        for hd in range(4, 7):
                            maxima(f, hd)
                        values(n, fp)
                        maxima(f, 7)
                        split_maxima(n, f)
                        shift_queries(f, fp)

                    def finish(n):
                        for half in range(2):
                            invert(n, half)
                        normalise(n)
                        split_out(n)

                    for hd in range(NQ):
                        if hd == 0:
                            stack(-1, 0, 0, "k")
                        if hd % 2 == 0:
                            stack(-1, 0, 0, f"q{hd // 2}")
                        maxima(0, hd, (p_s, p_st)[hd % 2])
                    values(-1, 0)
                    split_maxima(-1, 0)
                    shift_queries(0, 0)
                    turn(0, 0, before=False)
                    with dve.Fori(0, (N - 2) // 2) as m:
                        for par in (1, 0):
                            turn(m * 2 + (2 - par), par)
                    finish(N - 2)
                    route_vector(dve, router1)
                    finish(N - 1)
        scope.pop()

        scope.append(ExitStack())
        with scope[-1]:
            g1_hi = sb("g1_hi", [P, E1, 2, P], F32R)
            g1_lo = sb("g1_lo", [P, E1, 2, P], F32R)
            g3_hi = sb("g3_hi", [P, E1, 2, P], F32R)
            g3_lo = sb("g3_lo", [P, E1, 2, P], F32R)
            g2_hi = sb("g2_hi", [P, E1, 2, P], F32R)
            g2_lo = sb("g2_lo", [P, E1, 2, P], F32R)
            bT = sb("bT", [P, 2, E1, 2])
            b2b_hi = sb("b2b_hi", [P, D], F32R)
            b2b_lo = sb("b2b_lo", [P, D], F32R)
            scope.append(ExitStack())
            with scope[-1]:
                wr = sb("wr", [P, 3, E1, 2, P])
                br = sb("br", [P, 3, 2 * E1, 32])
                az = sb("az", [P, 2, 4, 4, P])
                az2 = sb("az2", [P, 2, 4, 2 * P])
                bt = sb("bt", [P, 10, P])
                bi_raw = sb("bi_raw", [4 * E1, P])
                b2b_raw = sb("b2b_raw", [P, D])
                p_bt = ps("p_bt", [P, 2, 4, P])
                p_w = ps("p_w", [P, 4, 4, P])
                p_bi = ps("p_bi", [P, 4 * E1])
                p_g = p_w[:].rearrange("p b m t -> p b (m t)")
                s_z = sem("m_zeroed")
                s_zp = sem("m_zeroed_pool")
                s_bl = sem("m_b_loaded")
                s_kl = [sem("m_w1_loaded"), sem("m_w3_loaded"), sem("m_w2_loaded")]
                s_l = sem("m_biases_loaded")
                s_bt = sem("m_b_transposed")
                s_btc = sem("m_b_stored")
                s_w = sem("m_merged")
                s_wh = sem("m_high")
                s_wl = sem("m_low")
                s_bi = sem("m_bias_transposed")
                with nc.Block() as block:
                    @block.gpsimd
                    def _(pool):
                        for k in range(2):
                            pool.memset(az[:, k], 0.0).then_inc(s_zp, 1)
                        pool.memset(az2[:], 0.0).then_inc(s_zp, 1)

                    @block.sync
                    def _(sp):
                        for k, (w, a) in enumerate(((W1, A1), (W3, A3))):
                            sp.dma_start(wr[:, k, :, :, :],
                                         w.rearrange("e (c p) d -> p e c d", p=P)).then_inc(s_kl[k], 16)
                            if k == 0:
                                sp.wait_ge(s_z, 1)
                                for kind, b in enumerate((B1, B3)):
                                    sp.dma_start(br[:, kind, :, 0:R],
                                                 b.rearrange("e (c p) r -> p (e c) r", p=P)).then_inc(s_bl, 16)
                                sp.dma_start(br[:, 2, 0:E1, 0:R], B2.rearrange("e p r -> p e r")).then_inc(s_bl, 16)
                            sp.wait_ge(s_zp, k + 1)
                            av = a.rearrange("(g f) r d -> f r g d", f=2)
                            for j in range(4):
                                sp.dma_start(az[32 * j:32 * j + R, k, :, j, :], av[j // 2]).then_inc(s_kl[k], 16)
                        sp.dma_start(wr[:, 2, :, :, :].rearrange("p e c m -> p e (c m)"),
                                     W2.rearrange("e d i -> d e i")).then_inc(s_kl[2], 16)
                        sp.wait_ge(s_zp, 3)
                        a2v = A2.rearrange("(g f) r h -> f r g h", f=4)
                        for j in range(4):
                            sp.dma_start(az2[32 * j:32 * j + R, :, j, :], a2v[j]).then_inc(s_kl[2], 16)
                        sp.dma_start(bi_raw[0:2 * E1, :], b1_1.rearrange("e (c p) -> (e c) p", p=P)).then_inc(s_l, 16)
                        sp.dma_start(bi_raw[2 * E1:4 * E1, :], b3_1.rearrange("e (c p) -> (e c) p", p=P)).then_inc(s_l, 16)
                        sp.wait_ge(s_z, 2)
                        for k in range(2):
                            sp.dma_start(b2b_raw[16 * k:16 * k + E1, :], b2_1).then_inc(s_l, 16)
                        sp.wait_ge(s_l, 4 * 16)

                    @block.tensor
                    def _(pe):
                        turn_gates(pe, router1, p_g, 4)
                        pe.wait_ge(s_bl, 3 * 16)
                        for t in range(10):
                            if t % 4 == 0 and t >= 8:
                                pe.wait_ge(s_btc, 1)
                            k, grp = (t // 4, t % 4)
                            last = nc.tensor.transpose(p_bt[:, (t // 4) % 2, t % 4, :],
                                                       br[:, k, 4 * grp:4 * grp + 4, :].rearrange("p a b -> p (a b)"),
                                                       ident[:])
                            if t in (3, 7, 9):
                                last.then_inc(s_bt, 1)
                        pe.wait_ge(router1.s_gc, N)
                        pe.wait_ge(s_btc, 3)
                        for s in range(12):
                            kind, pair = s // 4, s % 4
                            if pair == 0:
                                pe.wait_ge(s_kl[kind], 5 * 16)
                            if s >= 4:
                                pe.wait_ge(s_wl, s - 3)
                            for m in range(4):
                                e, c = 2 * pair + m // 2, m % 2
                                dst = p_w[:, s % 4, m, :]
                                nc.tensor.matmul(dst, wr[:, kind, e, c, :], ident[:], start=True, stop=False)
                                if kind < 2:
                                    a, b = az[:, kind, pair, m, :], bt[:, 4 * kind + pair, :]
                                else:
                                    a, b = az2[:, e // 4, e % 4, c * P:(c + 1) * P], bt[:, 8 + e // 4, :]
                                last = nc.tensor.matmul(dst, a, b, start=False, stop=True)
                            last.then_inc(s_w, 1)
                        pe.wait_ge(s_l, 4 * 16)
                        nc.tensor.transpose(p_bi[:], bi_raw[:], ident[0:4 * E1, 0:4 * E1]).then_inc(s_bi, 1)

                    def target(s):
                        kind, pair = s // 4, s % 4
                        hi = (g1_hi, g3_hi, g2_hi)[kind][:, 2 * pair:2 * pair + 2, :, :]
                        lo = (g1_lo, g3_lo, g2_lo)[kind][:, 2 * pair:2 * pair + 2, :, :]
                        return [v.rearrange("p e c m -> p (e c) m") for v in (hi, lo)]

                    @block.scalar
                    def _(act):
                        store_gates(act, router1, p_g, 4)
                        for s in range(12):
                            act.wait_ge(s_w, s + 1)
                            nc.scalar.activation(target(s)[0], p_w[:, s % 4, :, :], ACT.Copy).then_inc(s_wh, 1)
                        act.wait_ge(s_l, 4 * 16)
                        nc.scalar.activation(b2b_hi[:], b2b_raw[:], ACT.Copy).then_inc(s_wh, 1)

                    @block.vector
                    def _(dve):
                        nc.vector.memset(br[:], 0.0).then_inc(s_z, 1)
                        nc.vector.memset(b2b_raw[:], 0.0).then_inc(s_z, 1)
                        for t, (a, w) in enumerate(((0, 4), (4, 4), (8, 2))):
                            dve.wait_ge(s_bt, t + 1)
                            nc.vector.tensor_copy(bt[:, a:a + w, :], p_bt[:, t % 2, 0:w, :]).then_inc(s_btc, 1)
                        for s in range(12):
                            dve.wait_ge(s_wh, s + 1)
                            hi, lo = target(s)
                            nc.vector.tensor_tensor(lo, p_w[:, s % 4, :, :], raw(hi), ALU.subtract).then_inc(s_wl, 1)
                        dve.wait_ge(s_wh, 13)
                        nc.vector.tensor_tensor(b2b_lo[:], b2b_raw[:], raw(b2b_hi[:]), ALU.subtract).then_inc(s_wl, 1)
                        dve.wait_ge(s_bi, 1)
                        nc.vector.tensor_copy(bT[:].rearrange("p a e c -> p (a e c)"), p_bi[:])
            scope.pop()
            experts("e1_", E1, g1_hi, g1_lo, bT[:, 0], g3_hi, g3_lo, bT[:, 1], g2_hi, g2_lo, b2b_hi, b2b_lo,
                    ACT.Silu, True, None)
        scope.pop()


_INS = ['L0_attn_x', 'L0_attn_W_in', 'L0_attn_conv_w', 'L0_attn_conv_b', 'L0_attn_W_g', 'L0_attn_b_g',
        'L0_attn_forget_base', 'L0_attn_W_out', 'L0_ffn_router_w', 'L0_ffn_router_b', 'L0_ffn_w1', 'L0_ffn_b1',
        'L0_ffn_w2', 'L0_ffn_b2', 'L1_attn_Wk', 'L1_attn_Wv', 'L1_attn_Wq', 'L1_attn_Wp', 'L1_attn_bp',
        'L1_ffn_Wg', 'L1_ffn_W1', 'L1_ffn_b1', 'L1_ffn_A1', 'L1_ffn_B1', 'L1_ffn_W2', 'L1_ffn_b2', 'L1_ffn_A2',
        'L1_ffn_B2', 'L1_ffn_W3', 'L1_ffn_b3', 'L1_ffn_A3', 'L1_ffn_B3']


def kernel(**inputs):
    import numpy as _np
    import concourse.bacc as _bacc
    from concourse import mybir as _mybir
    from concourse.bass_utils import run_bass_kernel_spmd as _run

    nc = _bacc.Bacc("TRN2", target_bir_lowering=False, num_devices=1)
    arrays, args = {}, []
    for name in _INS:
        a = _np.ascontiguousarray(inputs[name])
        arrays[f"in_{name}_dram"] = a
        args.append(nc.dram_tensor(f"in_{name}_dram", a.shape, _mybir.dt.from_np(a.dtype), kind="ExternalInput").ap())
    shape = inputs['L0_attn_x'].shape
    args.append(nc.dram_tensor("out_0_dram", shape, _mybir.dt.float32, kind="ExternalOutput").ap())
    two_block_kernel(nc, *args)
    r = _run(nc, [arrays], core_ids=[0])
    return r.results[0]["out_0_dram"]
```
